# Optimizing a Trainium2 kernel written in Bass

```python
import numpy as np
import jax
import jax.numpy as jnp

def _softmax(x, axis=-1):
    return jax.nn.softmax(x, axis=axis)

def _gelu(x):
    return jax.nn.gelu(x, approximate=True)

def _silu(x):
    return jax.nn.silu(x)

def _sigmoid(x):
    return jax.nn.sigmoid(x)

def _layernorm(x, axis=-1, eps=1e-05):
    m = jnp.mean(x, axis=axis, keepdims=True)
    v = jnp.var(x, axis=axis, keepdims=True)
    return (x - m) / jnp.sqrt(v + eps)

def _scatter_add(tgt, idx, src, axis=0):
    return tgt.at[idx].add(src)

def _segment_sum(src, seg, n):
    return jax.ops.segment_sum(src, seg, n)
kernel_name = 'mk_gnn_resnorm_d4_gnn_r32_e0e936'

def setup_inputs(seed: int=0):
    np.random.seed(seed)
    _w = jnp.asarray

    def _rec_inputs():
        import jax
        import jax.numpy as jnp
        _gk = jax.random.key(seed)
        x = -0.0005121 + 1.001 * jax.random.normal(jax.random.fold_in(_gk, 1), (50000, 160), jnp.float32)
        src = jax.random.randint(jax.random.fold_in(_gk, 2), (25000,), 0, 50000, jnp.int32)
        dst = jax.random.randint(jax.random.fold_in(_gk, 3), (25000,), 0, 50000, jnp.int32)
        _o = jnp.argsort(dst, stable=True)
        src = src[_o]
        dst = dst[_o]
        edge_attr_16 = jax.random.uniform(jax.random.fold_in(_gk, 12), (25000, 16), jnp.float32, 0.0, 1)
        edge_attr_4 = 0.000898722 + 1.00012 * jax.random.normal(jax.random.fold_in(_gk, 13), (25000, 4), jnp.float32)
        edge_attr_64 = 0.000127647 + 1.00004 * jax.random.normal(jax.random.fold_in(_gk, 14), (25000, 64), jnp.float32)
        edge_attr_8 = jax.random.uniform(jax.random.fold_in(_gk, 15), (25000, 8), jnp.float32, 0.0, 1)
        node_vec1 = jax.random.uniform(jax.random.fold_in(_gk, 17), (50000, 1), jnp.float32, 0.0, 1)
        return (x, src, dst, edge_attr_16, edge_attr_4, edge_attr_64, edge_attr_8, node_vec1)
    x, src, dst, edge_attr_16, edge_attr_4, edge_attr_64, edge_attr_8, node_vec1 = _rec_inputs()

    def _L0_gnn_setup():
        import jax, jax.numpy as jnp
        import numpy as np
        N, E = (625, 10000)
        CS, CV = (64, 32)
        AS_, AV, H = (16, 8, 4)
        NB = 16
        SQRT3 = 1.7320508075688772
        SQRT2 = 1.4142135623730951
        EPS = 1e-05

        def _cg_tp(s, v, y0, y1, w_ss, w_sv, w_vs, w_vv0, w_vv1):
            out_s = jnp.concatenate([w_ss * s * y0[:, None], w_vv0 * (jnp.einsum('eci,ei->ec', v, y1) / SQRT3)], axis=-1)
            out_v = jnp.concatenate([(w_sv * s)[:, :, None] * y1[:, None, :], (w_vs * jnp.ones_like(v[..., 0]))[..., None] * v * y0[:, None, None], (w_vv1 * jnp.ones_like(v[..., 0]))[..., None] * (jnp.cross(v, y1[:, None, :]) / SQRT2)], axis=1)
            return (out_s, out_v)

        def _equiv_layernorm(s, v, gamma_s, beta_s, gamma_v):
            mu = jnp.mean(s, axis=-1, keepdims=True)
            var = jnp.var(s, axis=-1, keepdims=True)
            s_n = (s - mu) * jax.lax.rsqrt(var + EPS) * gamma_s + beta_s
            rms = jnp.sqrt(jnp.mean(jnp.sum(v * v, axis=-1), axis=-1, keepdims=True) + EPS)
            v_n = v / rms[..., None] * gamma_v[None, :, None]
            return (s_n, v_n)
        key = jax.random.key(seed)
        ks = jax.random.split(key, 26)

        def rn(k, shape, fan):
            return jax.random.normal(k, shape, jnp.float32) / np.sqrt(fan)
        D1S, D1V = (CS + CV, CS + 2 * CV)
        WN = 2 * CS + 3 * CV
        inp = {'node': jax.random.normal(ks[0], (N, CS + 3 * CV), jnp.float32), 'edge_index': jax.random.randint(ks[1], (2, E), 0, N, jnp.int64 if jax.config.jax_enable_x64 else jnp.int32), 'rbf': jax.random.uniform(ks[2], (E, NB), jnp.float32), 'rsh': jax.random.normal(ks[3], (E, 4), jnp.float32), 'gamma_s': jnp.ones((CS,), jnp.float32), 'beta_s': jnp.zeros((CS,), jnp.float32), 'gamma_v': jnp.ones((CV,), jnp.float32), 'Ws_src': rn(ks[4], (CS, CS), CS), 'Wv_src': rn(ks[5], (CV, CV), CV), 'Ws_dst': rn(ks[6], (CS, CS), CS), 'Wv_dst': rn(ks[7], (CV, CV), CV), 'W_rbf': rn(ks[8], (NB, WN), NB), 'W_alpha': rn(ks[9], (D1S, H * AS_), D1S), 'alpha_dot': rn(ks[10], (1, H, AS_), AS_), 'Ws_val': rn(ks[11], (D1S, CS), D1S), 'Wv_val': rn(ks[12], (D1V, CV), D1V), 'Wg': rn(ks[13], (CS, CV), CS), 'w2_ss': rn(ks[14], (CS,), 1), 'w2_sv': rn(ks[15], (CS,), 1), 'w2_vs': rn(ks[16], (CV,), 1), 'w2_vv0': rn(ks[17], (CV,), 1), 'w2_vv1': rn(ks[18], (CV,), 1), 'Ws_vlin': rn(ks[19], (D1S, H * AS_), D1S), 'Wv_vlin': rn(ks[20], (D1V, H * AV), D1V), 'Wps': rn(ks[21], (H * AS_, CS), H * AS_), 'Wpv': rn(ks[22], (H * AV, CV), H * AV)}
        return inp
    _L0_gnn_all = _L0_gnn_setup()
    _L0_gnn_in = {k: v for k, v in _L0_gnn_all.items() if k in ('gamma_s', 'beta_s', 'gamma_v', 'Ws_src', 'Wv_src', 'Ws_dst', 'Wv_dst', 'W_rbf', 'W_alpha', 'alpha_dot', 'Ws_val', 'Wv_val', 'Wg', 'w2_ss', 'w2_sv', 'w2_vs', 'w2_vv0', 'w2_vv1', 'Ws_vlin', 'Wv_vlin', 'Wps', 'Wpv')}
    del _L0_gnn_all

    def _L1_gnn_setup():
        import jax, jax.numpy as jnp
        import numpy as np
        N = 1250
        E = 12500
        MUL0, MUL1 = (64, 32)
        RAD, HID = (8, 64)
        WNUM = 192
        NUM_NEIGHBORS = 10.0
        INV3 = 1.0 / np.sqrt(3.0)

        def _lin(s, v, Ws, Wv, attr):
            out_s = s @ Ws * attr * (1.0 / np.sqrt(Ws.shape[0]))
            out_v = jnp.einsum('nud,uv->nvd', v, Wv) * attr[..., None] * (1.0 / np.sqrt(Wv.shape[0]))
            return (out_s, out_v)
        key = jax.random.key(seed)
        ks = jax.random.split(key, 16)
        return {'node_input': jax.random.normal(ks[0], (N, MUL0 + 3 * MUL1), jnp.float32), 'node_attr': jnp.ones((N, 1), jnp.float32), 'edge_attr': jax.random.normal(ks[1], (E, 4), jnp.float32), 'edge_scalars': jax.random.uniform(ks[2], (E, RAD), jnp.float32), 'W_sc_s': jax.random.normal(ks[3], (MUL0, MUL0), jnp.float32), 'W_sc_v': jax.random.normal(ks[4], (MUL1, MUL1), jnp.float32), 'W1_s': jax.random.normal(ks[5], (MUL0, MUL0), jnp.float32), 'W1_v': jax.random.normal(ks[6], (MUL1, MUL1), jnp.float32), 'W2_s': jax.random.normal(ks[7], (MUL0 + MUL1, MUL0), jnp.float32), 'W2_v': jax.random.normal(ks[8], (MUL0 + MUL1, MUL1), jnp.float32), 'W3': jax.random.normal(ks[9], (MUL0 + MUL1, 1), jnp.float32), 'fcW1': jax.random.normal(ks[10], (RAD, HID), jnp.float32), 'fcW2': jax.random.normal(ks[11], (HID, WNUM), jnp.float32), 'edge_src': jax.random.randint(ks[12], (E,), 0, N, jnp.int32), 'edge_dst': jax.random.randint(ks[13], (E,), 0, N, jnp.int32)}
    _L1_gnn_all = _L1_gnn_setup()
    _L1_gnn_in = {k: v for k, v in _L1_gnn_all.items() if k in ('W_sc_s', 'W_sc_v', 'W1_s', 'W1_v', 'W2_s', 'W2_v', 'W3', 'fcW1', 'fcW2')}
    del _L1_gnn_all

    def _L2_gnn_setup():
        import jax, jax.numpy as jnp
        import numpy as np
        N = 625
        E = 10000
        MUL0 = 64
        MUL1 = 32
        FC_IN = 16
        FC_H = 64
        WNUM = 192
        key = jax.random.key(seed)
        ks = jax.random.split(key, 16)
        return {'x': jax.random.normal(ks[0], (N, MUL0 + 3 * MUL1), jnp.float32), 'node_attr': jnp.ones((N, 1), jnp.float32), 'edge_scalars': jax.random.normal(ks[1], (E, FC_IN), jnp.float32), 'edge_attr_sh': jax.random.normal(ks[2], (E, 4), jnp.float32), 'edge_src': jax.random.randint(ks[3], (E,), 0, N), 'edge_dst': jax.random.randint(ks[4], (E,), 0, N), 'Wfc1': jax.random.normal(ks[5], (FC_IN, FC_H), jnp.float32), 'Wfc2': jax.random.normal(ks[6], (FC_H, WNUM), jnp.float32), 'Wsc0': jax.random.normal(ks[7], (MUL0, MUL0), jnp.float32), 'Wsc1': jax.random.normal(ks[8], (MUL1, MUL1), jnp.float32), 'Wl1_0': jax.random.normal(ks[9], (MUL0, MUL0), jnp.float32), 'Wl1_1': jax.random.normal(ks[10], (MUL1, MUL1), jnp.float32), 'Wl2_s': jax.random.normal(ks[11], (MUL0 + MUL1, MUL0), jnp.float32), 'Wl2_v': jax.random.normal(ks[12], (MUL0 + MUL1, MUL1), jnp.float32), 'Wa': 0.1 * jax.random.normal(ks[13], (MUL0 + MUL1, 1), jnp.float32)}
    _L2_gnn_all = _L2_gnn_setup()
    _L2_gnn_in = {k: v for k, v in _L2_gnn_all.items() if k in ('Wfc1', 'Wfc2', 'Wsc0', 'Wsc1', 'Wl1_0', 'Wl1_1', 'Wl2_s', 'Wl2_v', 'Wa')}
    del _L2_gnn_all

    def _L3_gnn_setup():
        import jax, jax.numpy as jnp
        import numpy as np
        N, E = (1250, 20000)
        S_IN, V_IN = (64, 32)
        S_MID, V_MID = (96, 128)
        S_OUT, V_OUT = (96, 32)
        R = 64
        FC_HID = 64
        W_NUMEL = 64 + 64 + 32 + 32 + 32
        NUM_NEIGHBORS = 16.0

        def _inv(d):
            return 1.0 / jnp.sqrt(jnp.float32(d))

        def _forward(node_features, node_attr, edge_attr, edge_scalars, lin1_ws, lin1_wv, fc_w1, fc_w2, sc_ws, sc_wv, lin2_ws, lin2_wv, edge_src, edge_dst):
            n = node_features.shape[0]
            s = node_features[:, :S_IN]
            v = node_features[:, S_IN:].reshape(n, V_IN, 3)
            a = node_attr
            sc_s = s @ sc_ws * a * _inv(S_IN)
            sc_v = jnp.einsum('nci,cd->ndi', v, sc_wv) * a[:, :, None] * _inv(V_IN)
            h_s = s @ lin1_ws * a * _inv(S_IN)
            h_v = jnp.einsum('nci,cd->ndi', v, lin1_wv) * a[:, :, None] * _inv(V_IN)
            hid = jax.nn.silu(edge_scalars @ fc_w1 * _inv(R))
            w = hid @ fc_w2 * _inv(FC_HID)
            w1, w2, w3, w4, w5 = jnp.split(w, [64, 128, 160, 192], axis=-1)
            es = h_s[edge_src]
            ev = h_v[edge_src]
            e0 = edge_attr[:, :1]
            e1 = edge_attr[:, 1:4]
            m_s1 = w1 * es * e0
            m_s2 = w4 * jnp.einsum('eci,ei->ec', ev, e1) * _inv(3)
            m_v1 = (w2 * es)[:, :, None] * e1[:, None, :]
            m_v2 = w3[:, :, None] * ev * e0[:, :, None]
            m_v3 = w5[:, :, None] * jnp.cross(ev, e1[:, None, :]) * _inv(2)
            mid_s = jnp.concatenate([m_s1, m_s2], axis=-1)
            mid_v = jnp.concatenate([m_v1, m_v2, m_v3], axis=1)
            inv_nn = 1.0 / jnp.sqrt(jnp.float32(NUM_NEIGHBORS))
            agg_s = jax.ops.segment_sum(mid_s, edge_dst, num_segments=n) * inv_nn
            agg_v = jax.ops.segment_sum(mid_v, edge_dst, num_segments=n) * inv_nn
            o_s = agg_s @ lin2_ws * a * _inv(S_MID)
            o_v = jnp.einsum('nci,cd->ndi', agg_v, lin2_wv) * a[:, :, None] * _inv(V_MID)
            pre_s = sc_s + o_s
            pre_v = sc_v + o_v
            scalars = jax.nn.silu(pre_s[:, :64])
            gates = jax.nn.sigmoid(pre_s[:, 64:96])
            gated = gates[:, :, None] * pre_v
            return jnp.concatenate([scalars, gated.reshape(n, 3 * V_OUT)], axis=-1)
        key = jax.random.key(seed)
        ks = jax.random.split(key, 13)
        return {'node_features': jax.random.normal(ks[0], (N, S_IN + 3 * V_IN), jnp.float32), 'node_attr': jnp.ones((N, 1), jnp.float32), 'edge_src': jax.random.randint(ks[1], (E,), 0, N), 'edge_dst': jax.random.randint(ks[2], (E,), 0, N), 'edge_attr': jax.random.normal(ks[3], (E, 4), jnp.float32), 'edge_scalars': jax.random.normal(ks[4], (E, R), jnp.float32), 'lin1_ws': jax.random.normal(ks[5], (S_IN, S_IN), jnp.float32), 'lin1_wv': jax.random.normal(ks[6], (V_IN, V_IN), jnp.float32), 'fc_w1': jax.random.normal(ks[7], (R, FC_HID), jnp.float32), 'fc_w2': jax.random.normal(ks[8], (FC_HID, W_NUMEL), jnp.float32), 'sc_ws': jax.random.normal(ks[9], (S_IN, S_OUT), jnp.float32), 'sc_wv': jax.random.normal(ks[10], (V_IN, V_OUT), jnp.float32), 'lin2_ws': jax.random.normal(ks[11], (S_MID, S_OUT), jnp.float32), 'lin2_wv': jax.random.normal(ks[12], (V_MID, V_OUT), jnp.float32)}
    _L3_gnn_all = _L3_gnn_setup()
    _L3_gnn_in = {k: v for k, v in _L3_gnn_all.items() if k in ('lin1_ws', 'lin1_wv', 'fc_w1', 'fc_w2', 'sc_ws', 'sc_wv', 'lin2_ws', 'lin2_wv')}
    del _L3_gnn_all
    return {'x': x, 'src': src, 'dst': dst, 'edge_attr_16': edge_attr_16, 'edge_attr_4': edge_attr_4, 'edge_attr_64': edge_attr_64, 'edge_attr_8': edge_attr_8, 'node_vec1': node_vec1, 'L0_gnn_gamma_s': _L0_gnn_in['gamma_s'], 'L0_gnn_beta_s': _L0_gnn_in['beta_s'], 'L0_gnn_gamma_v': _L0_gnn_in['gamma_v'], 'L0_gnn_Ws_src': _L0_gnn_in['Ws_src'], 'L0_gnn_Wv_src': _L0_gnn_in['Wv_src'], 'L0_gnn_Ws_dst': _L0_gnn_in['Ws_dst'], 'L0_gnn_Wv_dst': _L0_gnn_in['Wv_dst'], 'L0_gnn_W_rbf': _L0_gnn_in['W_rbf'], 'L0_gnn_W_alpha': _L0_gnn_in['W_alpha'], 'L0_gnn_alpha_dot': _L0_gnn_in['alpha_dot'], 'L0_gnn_Ws_val': _L0_gnn_in['Ws_val'], 'L0_gnn_Wv_val': _L0_gnn_in['Wv_val'], 'L0_gnn_Wg': _L0_gnn_in['Wg'], 'L0_gnn_w2_ss': _L0_gnn_in['w2_ss'], 'L0_gnn_w2_sv': _L0_gnn_in['w2_sv'], 'L0_gnn_w2_vs': _L0_gnn_in['w2_vs'], 'L0_gnn_w2_vv0': _L0_gnn_in['w2_vv0'], 'L0_gnn_w2_vv1': _L0_gnn_in['w2_vv1'], 'L0_gnn_Ws_vlin': _L0_gnn_in['Ws_vlin'], 'L0_gnn_Wv_vlin': _L0_gnn_in['Wv_vlin'], 'L0_gnn_Wps': _L0_gnn_in['Wps'], 'L0_gnn_Wpv': _L0_gnn_in['Wpv'], 'L1_gnn_W_sc_s': _L1_gnn_in['W_sc_s'], 'L1_gnn_W_sc_v': _L1_gnn_in['W_sc_v'], 'L1_gnn_W1_s': _L1_gnn_in['W1_s'], 'L1_gnn_W1_v': _L1_gnn_in['W1_v'], 'L1_gnn_W2_s': _L1_gnn_in['W2_s'], 'L1_gnn_W2_v': _L1_gnn_in['W2_v'], 'L1_gnn_W3': _L1_gnn_in['W3'], 'L1_gnn_fcW1': _L1_gnn_in['fcW1'], 'L1_gnn_fcW2': _L1_gnn_in['fcW2'], 'L2_gnn_Wfc1': _L2_gnn_in['Wfc1'], 'L2_gnn_Wfc2': _L2_gnn_in['Wfc2'], 'L2_gnn_Wsc0': _L2_gnn_in['Wsc0'], 'L2_gnn_Wsc1': _L2_gnn_in['Wsc1'], 'L2_gnn_Wl1_0': _L2_gnn_in['Wl1_0'], 'L2_gnn_Wl1_1': _L2_gnn_in['Wl1_1'], 'L2_gnn_Wl2_s': _L2_gnn_in['Wl2_s'], 'L2_gnn_Wl2_v': _L2_gnn_in['Wl2_v'], 'L2_gnn_Wa': _L2_gnn_in['Wa'], 'L3_gnn_lin1_ws': _L3_gnn_in['lin1_ws'], 'L3_gnn_lin1_wv': _L3_gnn_in['lin1_wv'], 'L3_gnn_fc_w1': _L3_gnn_in['fc_w1'], 'L3_gnn_fc_w2': _L3_gnn_in['fc_w2'], 'L3_gnn_sc_ws': _L3_gnn_in['sc_ws'], 'L3_gnn_sc_wv': _L3_gnn_in['sc_wv'], 'L3_gnn_lin2_ws': _L3_gnn_in['lin2_ws'], 'L3_gnn_lin2_wv': _L3_gnn_in['lin2_wv']}

def reference(x, src, dst, edge_attr_16, edge_attr_4, edge_attr_64, edge_attr_8, node_vec1, L0_gnn_gamma_s, L0_gnn_beta_s, L0_gnn_gamma_v, L0_gnn_Ws_src, L0_gnn_Wv_src, L0_gnn_Ws_dst, L0_gnn_Wv_dst, L0_gnn_W_rbf, L0_gnn_W_alpha, L0_gnn_alpha_dot, L0_gnn_Ws_val, L0_gnn_Wv_val, L0_gnn_Wg, L0_gnn_w2_ss, L0_gnn_w2_sv, L0_gnn_w2_vs, L0_gnn_w2_vv0, L0_gnn_w2_vv1, L0_gnn_Ws_vlin, L0_gnn_Wv_vlin, L0_gnn_Wps, L0_gnn_Wpv, L1_gnn_W_sc_s, L1_gnn_W_sc_v, L1_gnn_W1_s, L1_gnn_W1_v, L1_gnn_W2_s, L1_gnn_W2_v, L1_gnn_W3, L1_gnn_fcW1, L1_gnn_fcW2, L2_gnn_Wfc1, L2_gnn_Wfc2, L2_gnn_Wsc0, L2_gnn_Wsc1, L2_gnn_Wl1_0, L2_gnn_Wl1_1, L2_gnn_Wl2_s, L2_gnn_Wl2_v, L2_gnn_Wa, L3_gnn_lin1_ws, L3_gnn_lin1_wv, L3_gnn_fc_w1, L3_gnn_fc_w2, L3_gnn_sc_ws, L3_gnn_sc_wv, L3_gnn_lin2_ws, L3_gnn_lin2_wv):
    import jax
    import jax.numpy as jnp

    def _L0_gnn_ref(node, rbf, rsh, gamma_s, beta_s, gamma_v, Ws_src, Wv_src, Ws_dst, Wv_dst, W_rbf, W_alpha, alpha_dot, Ws_val, Wv_val, Wg, w2_ss, w2_sv, w2_vs, w2_vv0, w2_vv1, Ws_vlin, Wv_vlin, Wps, Wpv, edge_index):
        import jax, jax.numpy as jnp
        import numpy as np
        N, E = (625, 10000)
        CS, CV = (64, 32)
        AS_, AV, H = (16, 8, 4)
        NB = 16
        SQRT3 = 1.7320508075688772
        SQRT2 = 1.4142135623730951
        EPS = 1e-05

        def _cg_tp(s, v, y0, y1, w_ss, w_sv, w_vs, w_vv0, w_vv1):
            out_s = jnp.concatenate([w_ss * s * y0[:, None], w_vv0 * (jnp.einsum('eci,ei->ec', v, y1) / SQRT3)], axis=-1)
            out_v = jnp.concatenate([(w_sv * s)[:, :, None] * y1[:, None, :], (w_vs * jnp.ones_like(v[..., 0]))[..., None] * v * y0[:, None, None], (w_vv1 * jnp.ones_like(v[..., 0]))[..., None] * (jnp.cross(v, y1[:, None, :]) / SQRT2)], axis=1)
            return (out_s, out_v)

        def _equiv_layernorm(s, v, gamma_s, beta_s, gamma_v):
            mu = jnp.mean(s, axis=-1, keepdims=True)
            var = jnp.var(s, axis=-1, keepdims=True)
            s_n = (s - mu) * jax.lax.rsqrt(var + EPS) * gamma_s + beta_s
            rms = jnp.sqrt(jnp.mean(jnp.sum(v * v, axis=-1), axis=-1, keepdims=True) + EPS)
            v_n = v / rms[..., None] * gamma_v[None, :, None]
            return (s_n, v_n)
        n = node.shape[0]
        e = rsh.shape[0]
        s = node[:, :CS]
        v = node[:, CS:].reshape(n, CV, 3)
        s_n, v_n = _equiv_layernorm(s, v, gamma_s, beta_s, gamma_v)
        src, dst = (edge_index[0], edge_index[1])
        msg_s = (s_n @ Ws_src)[src] + (s_n @ Ws_dst)[dst]
        msg_v = jnp.einsum('ncx,cd->ndx', v_n, Wv_src)[src] + jnp.einsum('ncx,cd->ndx', v_n, Wv_dst)[dst]
        y0, y1 = (rsh[:, 0], rsh[:, 1:4])
        w1 = rbf @ W_rbf
        m1_s, m1_v = _cg_tp(msg_s, msg_v, y0, y1, w1[:, :CS], w1[:, CS:2 * CS], w1[:, 2 * CS:2 * CS + CV], w1[:, 2 * CS + CV:2 * CS + 2 * CV], w1[:, 2 * CS + 2 * CV:])
        a = (m1_s @ W_alpha).reshape(e, H, AS_)
        a = jnp.where(a > 0, a, 0.2 * a)
        a = jnp.sum(a * alpha_dot, axis=-1, keepdims=True)
        amax = jax.ops.segment_max(a, dst, num_segments=n)
        amax = jnp.where(jnp.isfinite(amax), amax, 0.0)
        ex = jnp.exp(a - amax[dst])
        den = jax.ops.segment_sum(ex, dst, num_segments=n)
        alpha = ex / (den[dst] + 1e-16)
        val_s = m1_s @ Ws_val
        val_v = jnp.einsum('ecx,cd->edx', m1_v, Wv_val)
        val_v = val_v * jax.nn.sigmoid(val_s @ Wg)[..., None]
        val_s = jax.nn.sigmoid(val_s)
        m2_s, m2_v = _cg_tp(val_s, val_v, y0, y1, w2_ss, w2_sv, w2_vs, w2_vv0, w2_vv1)
        hs = (m2_s @ Ws_vlin).reshape(e, H, AS_)
        hv = jnp.einsum('ecx,cd->edx', m2_v, Wv_vlin).reshape(e, H, AV, 3)
        h = jnp.concatenate([hs, hv.reshape(e, H, AV * 3)], axis=-1)
        agg = jax.ops.segment_sum(alpha * h, dst, num_segments=n)
        agg_s = agg[:, :, :AS_].reshape(n, H * AS_)
        agg_v = agg[:, :, AS_:].reshape(n, H * AV, 3)
        out = node + jnp.concatenate([agg_s @ Wps, jnp.einsum('ncx,cd->ndx', agg_v, Wpv).reshape(n, CV * 3)], axis=-1)
        return out

    def _L1_gnn_ref(node_input, node_attr, edge_attr, edge_scalars, W_sc_s, W_sc_v, W1_s, W1_v, W2_s, W2_v, W3, fcW1, fcW2, edge_src, edge_dst):
        import jax, jax.numpy as jnp
        import numpy as np
        N = 1250
        E = 12500
        MUL0, MUL1 = (64, 32)
        RAD, HID = (8, 64)
        WNUM = 192
        NUM_NEIGHBORS = 10.0
        INV3 = 1.0 / np.sqrt(3.0)

        def _lin(s, v, Ws, Wv, attr):
            out_s = s @ Ws * attr * (1.0 / np.sqrt(Ws.shape[0]))
            out_v = jnp.einsum('nud,uv->nvd', v, Wv) * attr[..., None] * (1.0 / np.sqrt(Wv.shape[0]))
            return (out_s, out_v)
        n = node_input.shape[0]
        s_in = node_input[:, :MUL0]
        v_in = node_input[:, MUL0:].reshape(n, MUL1, 3)
        sc_s, sc_v = _lin(s_in, v_in, W_sc_s, W_sc_v, node_attr)
        f_s, f_v = _lin(s_in, v_in, W1_s, W1_v, node_attr)
        h = jax.nn.silu(edge_scalars @ fcW1 * (1.0 / np.sqrt(RAD)))
        w = h @ fcW2 * (1.0 / np.sqrt(HID))
        wA, wB, wC, wD = (w[:, :64], w[:, 64:128], w[:, 128:160], w[:, 160:192])
        xs = f_s[edge_src]
        xv = f_v[edge_src]
        y0 = edge_attr[:, :1]
        y1 = edge_attr[:, 1:4]
        outA = wA * xs * y0
        outD = wD * jnp.einsum('eud,ed->eu', xv, y1) * INV3
        outB = wB[:, :, None] * xs[:, :, None] * y1[:, None, :]
        outC = wC[:, :, None] * xv * y0[:, :, None]
        edge_feat = jnp.concatenate([outA, outD, outB.reshape(-1, MUL0 * 3), outC.reshape(-1, MUL1 * 3)], axis=1)
        agg = jax.ops.segment_sum(edge_feat, edge_dst, num_segments=n)
        agg = agg * (1.0 / np.sqrt(NUM_NEIGHBORS))
        ms = agg[:, :MUL0 + MUL1]
        mv = agg[:, MUL0 + MUL1:].reshape(n, MUL0 + MUL1, 3)
        c_s, c_v = _lin(ms, mv, W2_s, W2_v, node_attr)
        conv = jnp.concatenate([c_s, c_v.reshape(n, -1)], axis=1)
        sc = jnp.concatenate([sc_s, sc_v.reshape(n, -1)], axis=1)
        angle = 0.1 * (ms @ W3) * node_attr * (1.0 / np.sqrt(MUL0 + MUL1))
        cos, sin = (jnp.cos(angle), jnp.sin(angle))
        return cos * sc + sin * conv

    def _L2_gnn_ref(x, node_attr, edge_scalars, edge_attr_sh, edge_src, edge_dst, Wfc1, Wfc2, Wsc0, Wsc1, Wl1_0, Wl1_1, Wl2_s, Wl2_v, Wa):
        import jax, jax.numpy as jnp
        import numpy as np
        N = 625
        E = 10000
        MUL0 = 64
        MUL1 = 32
        FC_IN = 16
        FC_H = 64
        WNUM = 192
        n = x.shape[0]
        x0 = x[:, :MUL0]
        x1 = x[:, MUL0:].reshape(n, MUL1, 3)
        a = node_attr
        h = jax.nn.silu(edge_scalars @ (Wfc1 / jnp.sqrt(jnp.float32(FC_IN))))
        w = h @ (Wfc2 / jnp.sqrt(jnp.float32(FC_H)))
        w0 = w[:, :64]
        w1 = w[:, 64:128]
        w2 = w[:, 128:160]
        w3 = w[:, 160:192]
        inv8 = 1.0 / jnp.sqrt(jnp.float32(MUL0))
        inv32 = 1.0 / jnp.sqrt(jnp.float32(MUL1))
        sc = jnp.concatenate([x0 @ Wsc0 * a * inv8, (jnp.einsum('num,uv->nvm', x1, Wsc1) * a[..., None] * inv32).reshape(n, 3 * MUL1)], axis=1)
        f0 = x0 @ Wl1_0 * a * inv8
        f1 = jnp.einsum('num,uv->nvm', x1, Wl1_1) * a[..., None] * inv32
        e0 = f0[edge_src]
        e1 = f1[edge_src]
        sh0 = edge_attr_sh[:, :1]
        sh1 = edge_attr_sh[:, 1:4]
        mid0 = w0 * e0 * sh0
        mid1 = w3 * jnp.einsum('eum,em->eu', e1, sh1) / jnp.sqrt(3.0)
        mid2 = w1[:, :, None] * e0[:, :, None] * sh1[:, None, :]
        mid3 = w2[:, :, None] * e1 * sh0[:, :, None]
        cnt = jnp.clip(jax.ops.segment_sum(jnp.ones(edge_dst.shape, x.dtype), edge_dst, num_segments=n), 1.0)

        def smean(v):
            s = jax.ops.segment_sum(v, edge_dst, num_segments=n)
            return s / cnt.reshape((n,) + (1,) * (v.ndim - 1))
        n0, n1 = (smean(mid0), smean(mid1))
        n2, n3 = (smean(mid2), smean(mid3))
        scal = jnp.concatenate([n0, n1], axis=1)
        vec = jnp.concatenate([n2, n3], axis=1)
        inv96 = 1.0 / jnp.sqrt(jnp.float32(MUL0 + MUL1))
        alpha = scal @ Wa * a * inv96
        out_s = scal @ Wl2_s * a * inv96
        out_v = jnp.einsum('num,uv->nvm', vec, Wl2_v) * a[..., None] * inv96
        conv = jnp.concatenate([out_s, out_v.reshape(n, 3 * MUL1)], axis=1)
        return sc + alpha * conv

    def _L3_gnn_ref(node_features, node_attr, edge_src, edge_dst, edge_attr, edge_scalars, lin1_ws, lin1_wv, fc_w1, fc_w2, sc_ws, sc_wv, lin2_ws, lin2_wv):
        import jax, jax.numpy as jnp
        import numpy as np
        N, E = (1250, 20000)
        S_IN, V_IN = (64, 32)
        S_MID, V_MID = (96, 128)
        S_OUT, V_OUT = (96, 32)
        R = 64
        FC_HID = 64
        W_NUMEL = 64 + 64 + 32 + 32 + 32
        NUM_NEIGHBORS = 16.0

        def _inv(d):
            return 1.0 / jnp.sqrt(jnp.float32(d))

        def _forward(node_features, node_attr, edge_attr, edge_scalars, lin1_ws, lin1_wv, fc_w1, fc_w2, sc_ws, sc_wv, lin2_ws, lin2_wv, edge_src, edge_dst):
            n = node_features.shape[0]
            s = node_features[:, :S_IN]
            v = node_features[:, S_IN:].reshape(n, V_IN, 3)
            a = node_attr
            sc_s = s @ sc_ws * a * _inv(S_IN)
            sc_v = jnp.einsum('nci,cd->ndi', v, sc_wv) * a[:, :, None] * _inv(V_IN)
            h_s = s @ lin1_ws * a * _inv(S_IN)
            h_v = jnp.einsum('nci,cd->ndi', v, lin1_wv) * a[:, :, None] * _inv(V_IN)
            hid = jax.nn.silu(edge_scalars @ fc_w1 * _inv(R))
            w = hid @ fc_w2 * _inv(FC_HID)
            w1, w2, w3, w4, w5 = jnp.split(w, [64, 128, 160, 192], axis=-1)
            es = h_s[edge_src]
            ev = h_v[edge_src]
            e0 = edge_attr[:, :1]
            e1 = edge_attr[:, 1:4]
            m_s1 = w1 * es * e0
            m_s2 = w4 * jnp.einsum('eci,ei->ec', ev, e1) * _inv(3)
            m_v1 = (w2 * es)[:, :, None] * e1[:, None, :]
            m_v2 = w3[:, :, None] * ev * e0[:, :, None]
            m_v3 = w5[:, :, None] * jnp.cross(ev, e1[:, None, :]) * _inv(2)
            mid_s = jnp.concatenate([m_s1, m_s2], axis=-1)
            mid_v = jnp.concatenate([m_v1, m_v2, m_v3], axis=1)
            inv_nn = 1.0 / jnp.sqrt(jnp.float32(NUM_NEIGHBORS))
            agg_s = jax.ops.segment_sum(mid_s, edge_dst, num_segments=n) * inv_nn
            agg_v = jax.ops.segment_sum(mid_v, edge_dst, num_segments=n) * inv_nn
            o_s = agg_s @ lin2_ws * a * _inv(S_MID)
            o_v = jnp.einsum('nci,cd->ndi', agg_v, lin2_wv) * a[:, :, None] * _inv(V_MID)
            pre_s = sc_s + o_s
            pre_v = sc_v + o_v
            scalars = jax.nn.silu(pre_s[:, :64])
            gates = jax.nn.sigmoid(pre_s[:, 64:96])
            gated = gates[:, :, None] * pre_v
            return jnp.concatenate([scalars, gated.reshape(n, 3 * V_OUT)], axis=-1)
        return _forward(node_features, node_attr, edge_attr, edge_scalars, lin1_ws, lin1_wv, fc_w1, fc_w2, sc_ws, sc_wv, lin2_ws, lin2_wv, edge_src, edge_dst)
    edge_index = jnp.stack([src, dst])
    x = _layernorm(x + _L0_gnn_ref(x, edge_attr_16, edge_attr_4, L0_gnn_gamma_s, L0_gnn_beta_s, L0_gnn_gamma_v, L0_gnn_Ws_src, L0_gnn_Wv_src, L0_gnn_Ws_dst, L0_gnn_Wv_dst, L0_gnn_W_rbf, L0_gnn_W_alpha, L0_gnn_alpha_dot, L0_gnn_Ws_val, L0_gnn_Wv_val, L0_gnn_Wg, L0_gnn_w2_ss, L0_gnn_w2_sv, L0_gnn_w2_vs, L0_gnn_w2_vv0, L0_gnn_w2_vv1, L0_gnn_Ws_vlin, L0_gnn_Wv_vlin, L0_gnn_Wps, L0_gnn_Wpv, edge_index), axis=-1)
    x = _layernorm(x + _L1_gnn_ref(x, node_vec1, edge_attr_4, edge_attr_8, L1_gnn_W_sc_s, L1_gnn_W_sc_v, L1_gnn_W1_s, L1_gnn_W1_v, L1_gnn_W2_s, L1_gnn_W2_v, L1_gnn_W3, L1_gnn_fcW1, L1_gnn_fcW2, src, dst), axis=-1)
    x = _layernorm(x + _L2_gnn_ref(x, node_vec1, edge_attr_16, edge_attr_4, src, dst, L2_gnn_Wfc1, L2_gnn_Wfc2, L2_gnn_Wsc0, L2_gnn_Wsc1, L2_gnn_Wl1_0, L2_gnn_Wl1_1, L2_gnn_Wl2_s, L2_gnn_Wl2_v, L2_gnn_Wa), axis=-1)
    x = _layernorm(x + _L3_gnn_ref(x, node_vec1, src, dst, edge_attr_4, edge_attr_64, L3_gnn_lin1_ws, L3_gnn_lin1_wv, L3_gnn_fc_w1, L3_gnn_fc_w2, L3_gnn_sc_ws, L3_gnn_sc_wv, L3_gnn_lin2_ws, L3_gnn_lin2_wv), axis=-1)
    return x

_drawn_inputs = setup_inputs


def setup_inputs(seed=0):
    import zlib

    import numpy as np

    out = dict(_drawn_inputs(seed))
    spreads = {'L0_gnn_gamma_s': (1.0, 0.6), 'L0_gnn_beta_s': (0.0, 0.8), 'L0_gnn_gamma_v': (1.0, 0.6)}
    factors = {'edge_attr_64': 3.359,
     'edge_attr_8': 8.0,
     'L0_gnn_W_alpha': 3.352,
     'L0_gnn_alpha_dot': 3.222,
     'L1_gnn_W1_s': 8.0,
     'L1_gnn_W1_v': 8.0,
     'L1_gnn_W2_s': 8.0,
     'L1_gnn_W2_v': 8.0,
     'L1_gnn_W3': 8.0,
     'L1_gnn_fcW1': 8.0,
     'L1_gnn_fcW2': 8.0,
     'L2_gnn_Wfc1': 8.0,
     'L2_gnn_Wfc2': 8.0,
     'L2_gnn_Wl1_0': 8.0,
     'L2_gnn_Wl1_1': 8.0,
     'L2_gnn_Wl2_s': 8.0,
     'L2_gnn_Wl2_v': 8.0,
     'L2_gnn_Wa': 8.0,
     'L3_gnn_lin1_ws': 4.185,
     'L3_gnn_lin1_wv': 4.612,
     'L3_gnn_fc_w1': 3.365,
     'L3_gnn_fc_w2': 3.174,
     'L3_gnn_lin2_ws': 4.613,
     'L3_gnn_lin2_wv': 4.335}
    for name, (base, spread) in spreads.items():
        noise = np.random.default_rng([zlib.crc32(name.encode()), seed]).standard_normal(out[name].shape)
        drawn = base * np.exp(spread * noise) if base else spread * noise
        out[name] = jnp.asarray(drawn.astype(out[name].dtype))
    for name, factor in factors.items():
        out[name] = (out[name] * factor).astype(out[name].dtype)
    return out
```

```python
from contextlib import ExitStack

import concourse.bass as bass
from concourse import mybir

N = 50000
E = 25000
CS, CV = 64, 32
F = CS + 3 * CV
H = 4
AS, AV = CS // H, CV // H
HC = AS + 3 * AV

EP = 125
ET = E // EP
T = 4
EC = T * EP
ETRIPS = ET // T
NP = 128
NG = T * NP
NTRIPS = -(-N // NG)
NFULL = N // NG
XW = F + 1
AW = 192
AROWS = 392 * 128
SKIP = 65536
BIG = 1.0e30
ATTR = F
OW = 288

C_VY, C_YV, C_YS, C_S, C_X = 0, 32, 128, 192, 256
EW = 352

LAYERS = [
    dict(rad=16, cross=True, msg=H * (HC + 1) + H),
    dict(rad=8, cross=False, msg=F + 1),
    dict(rad=16, cross=False, msg=F + 2),
    dict(rad=64, cross=True, msg=2 * 96),
]


PI, HALF_PI, INV_2PI = 3.1415925, 1.5707963267948966, 0.15915494309189535
TWO_PI = (6.28125, 1.9350051879882812e-03, 3.0199159819567000e-07)
MAGIC = 12582912.0


class Trip:

    def __init__(self, i, off):
        self.i, self.off, self.b = i, off, off % 2
        self.g = off if isinstance(i, int) else None

    def shift(self, d):
        return Trip(self.i, self.off + d)

    def lin(self, per, c):
        c = self.off * per + c
        return c if self.g is not None else self.i * (2 * per) + c

    def half(self, per, c):
        c = (self.off // 2) * per + c
        return c if self.g is not None else self.i * per + c

    def has(self, d, n):
        return self.g is None or 0 <= self.g + d < n


def trips(eng, n, body):
    body(Trip(0, 0))
    body(Trip(0, 1))
    with eng.Fori(1, n // 2 - 1) as i:
        body(Trip(i, 0))
        body(Trip(i, 1))
    body(Trip(0, n - 2))
    body(Trip(0, n - 1))


PHASES = ["E0", "N0", "E1", "N1", "E2", "N2", "E3", "N3"]
RING_E = {0: 10, 1: 6, 2: 6, 3: 8}
CHUNKS = {0: 3, 1: 2, 2: 2, 3: 3}

PER = {}
for _l in range(4):
    PER[f"E{_l}"] = dict(pe_ring=RING_E[_l], act_ring=RING_E[_l], ob_full=4 if _l == 0 else 1,
                         ob_evac=4 if _l == 0 else 1, f_done=CHUNKS[_l], prod_done=CHUNKS[_l], e_done=1,
                         msg_done=1, xn_done=1, e2_done=1, d_ready=1, exp_done=1, tanh_done=1, sq_done=1,
                         stat_done=1, pow_done=1, gp=0, d_norm=0, d_in=0, d_post=0, d_fin=0)
    PER[f"N{_l}"] = dict(pe_ring=2, act_ring=2, ob_full=1, ob_used=1, r_done=1, rstd_done=1, y_done=1, a_done=1,
                         agn_done=int(_l == 0), ang_done=int(_l in (1, 2)), sin_done=int(_l == 1),
                         coef_done=int(_l == 1), t2_done=int(_l in (1, 2)), gate_in=int(_l == 3),
                         sig_done=int(_l == 3), gpn=3)
for _ph, _n in dict(E0=dict(gp=1, d_norm=1, d_in=2, d_post=13, d_fin=10), E1=dict(d_in=2, d_post=5),
                    E2=dict(d_in=2, d_post=5), E3=dict(d_in=2, d_post=5),
                    N0=dict(d_norm=2, dve=2, gp=0), N1=dict(dve=3, gp=11), N2=dict(dve=4, gp=3), N3=dict(dve=3, gp=0)).items():
    PER[_ph].update(_n)
PER2 = {}
for _l in range(4):
    PER2[f"E{_l}"] = dict(gath=16 * T * (2 if _l == 0 else 1), idx=16 * (2 if _l == 0 else 1), lda=48, scid=16,
                          scat=16 * T)
    PER2[f"N{_l}"] = dict(nld=48 if _l == 0 else 32, nst=16)


def bases(per, ntrips):
    out, at = {}, {}
    for ph in PHASES:
        out[ph] = dict(at)
        for k, v in per[ph].items():
            at[k] = at.get(k, 0) + v * ntrips(ph)
    return out


BASE = bases(PER, lambda ph: ETRIPS if ph[0] == "E" else NTRIPS)
BASE2 = bases(PER2, lambda ph: (ETRIPS if ph[0] == "E" else NTRIPS) // 2)


def cnt(ph, sem, tr, k=1):
    return tr.lin(PER[ph][sem], BASE[ph].get(sem, 0) + k)


def cnt2(ph, sem, tr):
    per = PER2[ph][sem]
    return tr.half(per, BASE2[ph].get(sem, 0) + per)


def total(ph, sem):
    return BASE[ph].get(sem, 0) + PER[ph][sem] * (ETRIPS if ph[0] == "E" else NTRIPS)


def total2(ph, sem):
    return BASE2[ph].get(sem, 0) + PER2[ph][sem] * ((ETRIPS if ph[0] == "E" else NTRIPS) // 2)


class Chain:

    def __init__(self, eng, sems, ph, name, tr, held=None):
        self.eng, self.sem, self.ph, self.name, self.tr, self.n = eng, sems[name], ph, name, tr, 0
        self.held = held

    def step(self, ins):
        self.n += 1
        ins.then_inc(self.sem, 1)
        self.eng.wait_ge(self.sem, cnt(self.ph, self.name, self.tr, self.n))
        if self.held is not None:
            self.eng.sem_inc(self.held, 1)

    def end(self):
        assert self.n == PER[self.ph][self.name], (self.ph, self.name, self.n)


class Chain0:

    def __init__(self, eng, sem, at):
        self.eng, self.sem, self.at = eng, sem, at

    def step(self, ins):
        self.at += 1
        ins.then_inc(self.sem, 1)
        self.eng.wait_ge(self.sem, self.at)


def ring_banks(l):
    return 3 if RING_E[l] % 3 == 0 else 2


def ring_step(l, tr, what):
    if l:
        return 0, {"e": 0, "h": 1, "w": 2, "t": 2 + CHUNKS[l]}[what[0]] + int(what[1:] or 0)
    k = int(what[1:] or 0)
    if what[0] == "n":
        return (None, k) if tr.g == 0 else (-1, 7 + k)
    if what[0] == "t":
        return 0, (7 if tr.g == ETRIPS - 1 else 10) + k
    return 0, (3 if what[0] == "e" else 4) + k


def ring_val(ph, l, tr, what):
    d, k = ring_step(l, tr, what)
    if d is None:
        return BASE[ph].get("pe_ring", 0) + k + 1
    return cnt(ph, "pe_ring", tr.shift(d), k + 1)


def ring_pos(l, tr, what):
    d, k = ring_step(l, tr, what)
    return k if d is None else (tr.off + d) % 2 * RING_E[l] + k


def ob_val(ph, tr, what):
    if what == "M":
        return 1 if tr.g == 0 else cnt(ph, "ob_full", tr.shift(-1), 4)
    if what == "O2":
        return cnt(ph, "ob_full", tr, 4 if tr.g == ETRIPS - 1 else 5)
    return cnt(ph, "ob_full", tr, 2 + int(what[1]))


FIX_STEPS = [5, 6, 7, 8]
GRAPH_STEPS = 34
SETUP_STEPS = 79


def wait(eng, sem, value):
    if isinstance(value, int) and value <= 0:
        return
    eng.wait_ge(sem, value)


def gnn_kernel(nc, A, out):
    f32, i32 = mybir.dt.float32, mybir.dt.int32
    ALU, ACT, AX = mybir.AluOpType, mybir.ActivationFunctionType, mybir.AxisListType

    ctx = ExitStack()
    with ctx:
        def sb(name, shape, dt=f32):
            return ctx.enter_context(nc.sbuf_tensor(name, shape, dt))

        def pair(name, shape, dt=f32):
            return [sb(f"{name}{b}", shape, dt) for b in range(2)]

        def sem(name):
            return ctx.enter_context(nc.semaphore(name))

        tabA = nc.dram_tensor("tab_a", (N, XW), f32).ap()
        tabB = nc.dram_tensor("tab_b", (N, XW), f32).ap()
        agg = nc.dram_tensor("agg", (AROWS, AW), f32).ap()
        runs_d = nc.dram_tensor("runs", (EP, ET, 3), f32).ap()
        scix_d = nc.dram_tensor("scatter_ids", (EP, ET), i32).ap()
        TABLE = [A["x"], tabA, tabB, tabA]
        NEXT = [tabA, tabB, tabA, out]
        ES = [A["edge_attr_16"], A["edge_attr_8"], A["edge_attr_16"], A["edge_attr_64"]]

        ident = sb("ident", [128, 128])
        ones_k = sb("ones_k", [EP, EP])
        zeros = sb("zeros", [128, 3136])
        dst_i = sb("dst_i", [EP, ET], i32)
        dst_f = sb("dst_f", [EP, ET])
        runs = sb("runs_sb", [EP, ET, 3])
        wk_one = sb("wk_one", [EP, ET])
        wk1 = sb("wk1", [EP, ET])
        wk2 = sb("wk2", [EP, ET])
        scix = sb("scix", [EP, ET], i32)
        edge_i = sb("edge_i", [EP, 3], i32)
        edge_f = sb("edge_f", [EP, 3])
        pid = sb("pid", [EP, 1], i32)
        cf = sb("cf", [EP, 8])
        head_i = sb("head_i", [EP, 1], i32)
        fixid = sb("fixid", [EP, 1], i32)
        hrow_i = sb("hrow_i", [EP, EP], i32)
        hrow = sb("hrow", [EP, EP])
        same = sb("same", [EP, EP])
        samen = sb("samen", [EP, EP])

        fc1 = {l: sb(f"fc1_{l}", [LAYERS[l]["rad"], CS]) for l in (1, 2, 3)}
        fc2 = {l: sb(f"fc2_{l}", [16 if l == 0 else CS, EW]) for l in range(4)}
        wf1 = {l: sb(f"wf1_{l}", [128, 128]) for l in (1, 2, 3)}
        wf2 = {l: sb(f"wf2_{l}", [128, 128]) for l in (1, 2, 3)}
        EOW = {0: 288, 1: 193, 2: 193, 3: 224}
        ra = {l: sb(f"ra_{l}", [128, EOW[l] - 96]) for l in range(4)}
        rb = {l: sb(f"rb_{l}", [128, EOW[l]]) for l in range(4)}
        rx = {l: sb(f"rx_{l}", [96, 96]) for l in (0, 3)}
        NOW = {0: 160, 1: 160, 2: 160, 3: 192}
        nw1 = {l: sb(f"nw1_{l}", [128, NOW[l]]) for l in range(4)}
        nw2 = {l: sb(f"nw2_{l}", [32, NOW[l]]) for l in range(4)}
        wm_s = sb("wm_s", [128, F])
        wm_d = sb("wm_d", [128, F])
        wm_t = sb("wm_t", [64, F])
        g1 = sb("g1", [128, 1])
        g3 = sb("g3", [64, 1])
        beta = sb("beta", [CS, 1])
        wsrc = sb("wsrc", [CS, CS])
        wdst = sb("wdst", [CS, CS])
        brow = sb("brow", [1, F])
        onerow = sb("onerow", [1, EP])
        wval = sb("wval", [96, CS])
        wg = sb("wg", [CS, CV])
        wvt = sb("wvt", [CS, 96 + 128])
        adot = sb("adot", [EP, CS])
        r2a = sb("r2a", [128, H * 48])
        r2b = sb("r2b", [128, H * 48])
        r2x = sb("r2x", [96, H * 48])
        cA = sb("cA", [128, 1])
        cB = sb("cB", [128, 1])
        cX = sb("cX", [96, 1])

        gidx = pair("gidx", [EP, T], i32)
        gidx2 = pair("gidx2", [EP, T], i32)
        scid = pair("scid", [EP, T], i32)
        es_in = pair("es_in", [EP, T * 64])
        y_in = pair("y_in", [EP, T, 4])
        k_in = pair("k_in", [EP, T, 3])
        yc = pair("yc", [EP, T, 6])
        kc = pair("kc", [EP, T, 3])
        G = pair("G", [EP, T, XW])
        GS = pair("GS", [EP, T, F])
        GD = pair("GD", [EP, T, F])
        XN = sb("XN", [EP, T, 2, F])
        sqv = sb("sqv", [EP, 2 * T, 96])
        bst = sb("bst", [EP, 2 * T, 6])
        lst = sb("lst", [EP, 2 * T, 3])
        lrs = sb("lrs", [EP, 2 * T, 2])
        mhalf = sb("mhalf", [128, 24])
        epsb = sb("epsb", [128, 1])
        MG = sb("MG", [EP, T, F])
        EE = sb("EE", [EP, T, EW])
        E2 = sb("E2", [EP, T, EW])
        tmp = sb("tmp", [EP, T, 96])
        tmp2 = sb("tmp2", [EP, T, 96])
        tmp3 = sb("tmp3", [EP, T, 96])
        esT = sb("esT", [64, EC])
        hidT = sb("hidT", [64, EC])
        wT = [sb(f"wT{c}", [128, EC]) for c in range(3)]
        ET_ = [sb(f"ET{c}", [128, EC]) for c in range(3)]
        PR = [sb(f"PR{c}", [128, EC]) for c in range(3)]
        O = pair("O", [EP, T, OW])
        MG2 = sb("MG2", [EP, T, F])
        O2 = sb("O2", [EP, T * H, 49])
        SG2 = sb("SG2", [EP, T, CV])
        XT = sb("XT", [EP, T, 64])
        SG = sb("SG", [EP, T, 96])
        LK = sb("LK", [EP, T, CS])
        al = sb("al", [EP, T * H])
        mx = pair("mx", [EP, T * H])
        dd = sb("dd", [EP, 2, T * H])
        pc = sb("pc", [EP, 2, T * H])
        MS = sb("MS", [EP, T * H, HC + 1])
        OUT = pair("OUT", [EP, T, AW])
        FX = sb("FX", [EP, AW])
        FB = sb("FB", [EP, AW])
        FN = sb("FN", [EP, AW])
        fm = sb("fm", [EP, 4, H])
        fdg = sb("fdg", [EP, H * EP])

        X = pair("X", [NP, T, XW])
        AG = pair("AG", [NP, T, AW])
        XA = pair("XA", [NP, T])
        AGN = sb("AGN", [NP, T, F])
        rden = sb("rden", [NP, T * H])
        NT1 = sb("NT1", [128, NG])
        NT2 = sb("NT2", [32, NG])
        R = pair("R", [NP, T, F])
        T2B = pair("T2B", [NP, T, F])
        R3 = sb("R3", [NP, T, 192])
        SGN = sb("SGN", [NP, T, 96])
        nbs = sb("nbs", [NP, T, 6])
        nmv = pair("nmv", [NP, T, 2])
        nrs = pair("nrs", [NP, T, 2])
        ang = sb("ang", [NP, 2 * T])
        angk = sb("angk", [NP, 2 * T])
        angr = sb("angr", [NP, 2 * T])
        sc8 = sb("sc8", [NP, 2 * T])
        co = pair("co", [NP, 2 * T])
        Y = pair("Y", [NP, T, XW])

        psR = ctx.enter_context(nc.psum_tensor("psR", [128, 3, 512], f32))
        psF = ctx.enter_context(nc.psum_tensor("psF", [128, 3, 512], f32))
        psO = ctx.enter_context(nc.psum_tensor("psO", [128, 2, 512], f32))

        S = {n: sem(n) for n in (
            "pe_ring", "act_ring", "ob_full", "ob_evac", "ob_used", "f_done", "prod_done", "e_done", "msg_done",
            "xn_done", "e2_done", "d_ready", "exp_done", "tanh_done", "sq_done", "stat_done", "pow_done",
            "r_done", "rstd_done", "y_done", "agn_done", "ang_done", "sin_done", "t2_done", "coef_done",
            "gate_in", "sig_done", "a_done", "dve", "gp", "gpn", "d_norm", "d_in", "d_post",
            "d_fin")}
        S2 = {n: [sem(f"{n}0"), sem(f"{n}1")] for n in ("gath", "idx", "lda", "scid", "scat", "nld", "nst")}
        w_zero = sem("w_zero")
        w_load = sem("w_load")
        w_dve = sem("w_dve")
        w_pe = sem("w_pe")
        w_act = sem("w_act")
        g_load = sem("g_load")
        g_store = sem("g_store")
        z_store = sem("z_store")
        go = sem("go")
        sp_go = sem("sp_go")
        pe_go = sem("pe_go")
        ve_go = sem("ve_go")
        fx_rd = sem("fx_rd")
        fx_g = sem("fx_g")
        fx_mm = sem("fx_mm")
        fx_dve = sem("fx_dve")
        fx_act = sem("fx_act")
        fx_st = sem("fx_st")

        loads = []

        def put(tile, r, c, src):
            loads.append((tile[r:r + src.shape[0], c:c + src.shape[1]], src))

        def col(tile, r, src):
            loads.append((tile[r:r + src.shape[0], 0:1], src.rearrange("(a b) -> a b", b=1)))

        def putn(l, r, c, src):
            m = min(max(128 - r, 0), src.shape[0])
            if m:
                put(nw1[l], r, c, src[0:m])
            if m < src.shape[0]:
                put(nw2[l], r + m - 128, c, src[m:])

        L0 = {k[7:]: v for k, v in A.items() if k.startswith("L0_gnn_")}
        L1 = {k[7:]: v for k, v in A.items() if k.startswith("L1_gnn_")}
        L2 = {k[7:]: v for k, v in A.items() if k.startswith("L2_gnn_")}
        L3 = {k[7:]: v for k, v in A.items() if k.startswith("L3_gnn_")}
        for l, w in ((0, L0["W_rbf"]), (1, L1["fcW2"]), (2, L2["Wfc2"]), (3, L3["fc_w2"])):
            put(fc2[l], 0, 0, w[:, 160:192])
            for d in range(3):
                put(fc2[l], 0, 32 + 32 * d, w[:, 128:160])
                if LAYERS[l]["cross"]:
                    put(fc2[l], 0, 256 + 32 * d, w[:, 192:224])
            put(fc2[l], 0, 128, w[:, 0:128])
        for l, w in ((1, L1["fcW1"]), (2, L2["Wfc1"]), (3, L3["fc_w1"])):
            put(fc1[l], 0, 0, w)
        for l, ws, wv in ((1, L1["W1_s"], L1["W1_v"]), (2, L2["Wl1_0"], L2["Wl1_1"]),
                          (3, L3["lin1_ws"], L3["lin1_wv"])):
            for d in range(2):
                put(wf1[l], 64 * d, 64 * d, ws)
            for d in range(4):
                put(wf2[l], 32 * d, 32 * d, wv)
        for l, ws, wv, w1 in ((1, L1["W2_s"], L1["W2_v"], L1["W3"]), (2, L2["Wl2_s"], L2["Wl2_v"], L2["Wa"]),
                              (3, L3["lin2_ws"], L3["lin2_wv"], None), (0, L0["W_alpha"], L0["Wv_val"], None)):
            put(ra[l], 0, 0, ws[0:64])
            put(rb[l], 0, 96, ws[64:96])
            if w1 is not None:
                put(ra[l], 0, 64, w1[0:64])
                put(rb[l], 0, 160, w1[64:96])
            put(ra[l], 64, EOW[l] - 128, wv[0:64])
            for d in range(3):
                put(rb[l], 32 + 32 * d, 32 * d, wv[64:96])
                if l in rx:
                    put(rx[l], 32 * d, 32 * d, wv[96:128])
        put(ra[0], 0, 64, L0["Ws_val"][0:64])
        put(rb[0], 0, 160, L0["Ws_val"][64:96])
        put(wval, 0, 0, L0["Ws_val"])
        put(wg, 0, 0, L0["Wg"])
        for tile, ws, wv in ((wm_s, L0["Ws_src"], L0["Wv_src"]), (wm_d, L0["Ws_dst"], L0["Wv_dst"])):
            for d in range(3):
                put(tile, 32 * d, 32 * d, wv)
            put(tile, 96, 96, ws[0:32])
        put(wm_t, 0, 96, L0["Ws_src"][32:64])
        put(wm_t, 32, 96, L0["Ws_dst"][32:64])
        put(wsrc, 0, 0, L0["Ws_src"])
        put(wdst, 0, 0, L0["Ws_dst"])
        for d in range(3):
            col(g1, 32 * d, L0["gamma_v"])
        col(g1, 96, L0["gamma_s"][0:32])
        for d in range(2):
            col(g3, 32 * d, L0["gamma_s"][32:64])
        col(beta, 0, L0["beta_s"])
        loads.append((adot[:, :], L0["alpha_dot"].rearrange("a h s -> a (h s)").broadcast_to((EP, CS))))
        for h in range(H):
            put(r2a, 0, 48 * h + 8, L0["Ws_vlin"][0:64, AS * h:AS * h + AS])
            put(r2b, 0, 48 * h + 8, L0["Ws_vlin"][64:96, AS * h:AS * h + AS])
            put(r2a, 64, 48 * h, L0["Wv_vlin"][0:64, AV * h:AV * h + AV])
            for d in range(3):
                put(r2b, 32 + 32 * d, 48 * h + 24 + 8 * d, L0["Wv_vlin"][64:96, AV * h:AV * h + AV])
                put(r2x, 32 * d, 48 * h + 24 + 8 * d, L0["Wv_vlin"][96:128, AV * h:AV * h + AV])
        col(cA, 0, L0["w2_ss"])
        col(cA, 64, L0["w2_sv"])
        col(cB, 0, L0["w2_vv0"])
        for d in range(3):
            col(cB, 32 + 32 * d, L0["w2_vs"])
            col(cX, 32 * d, L0["w2_vv1"])
        for h in range(H):
            putn(0, HC * h, 96, L0["Wps"][AS * h:AS * h + AS, :])
            for d in range(3):
                putn(0, HC * h + AS + AV * d, 32 * d, L0["Wpv"][AV * h:AV * h + AV, :])
        for l, ws, wv in ((1, L1["W_sc_s"], L1["W_sc_v"]), (2, L2["Wsc0"], L2["Wsc1"]),
                          (3, L3["sc_ws"], L3["sc_wv"])):
            for d in range(3):
                putn(l, 32 * d, 32 * d, wv)
            putn(l, 96, 96, ws)

        cleared = ([fc2[l] for l in range(4)] + [wf1[l] for l in (1, 2, 3)] + [wf2[l] for l in (1, 2, 3)]
                   + [t[l] for t in (ra, rb, nw1, nw2) for l in range(4)] + [rx[0], rx[3]]
                   + [wm_s, wm_d, wm_t, r2a, r2b, r2x, brow, wvt])

        r3, r2 = 3.0 ** -0.5, 2.0 ** -0.5
        s64, s32, s96, s128 = 64 ** -0.5, 32 ** -0.5, 96 ** -0.5, 128 ** -0.5
        c1, c2, c3 = 10 ** -0.5 * s96, s96, 0.25 * s96
        scales = [(fc1[1][:, :], 8 ** -0.5), (fc1[2][:, :], 0.25), (fc1[3][:, :], 0.125)]
        for l in (1, 2, 3):
            scales += [(fc2[l][:, 0:(352 if l == 3 else 256)], s64), (wf1[l][:, :], s64), (wf2[l][:, :], s32)]
        scales += [(ra[1][:, 0:64], c1), (ra[1][:, 64:65], 0.1 * c1), (ra[1][:, 65:97], c1),
                   (rb[1][0:32, 96:160], c1 * r3), (rb[1][0:32, 160:161], 0.1 * c1 * r3), (rb[1][:, 0:96], c1),
                   (ra[2][:, :], c2), (rb[2][0:32, 96:161], c2 * r3), (rb[2][:, 0:96], c2),
                   (ra[3][:, 0:96], c3), (ra[3][:, 96:128], 0.25 * s128),
                   (rb[3][0:32, 96:192], c3 * r3), (rb[3][:, 0:96], 0.25 * s128), (rx[3][:, :], 0.25 * s128 * r2),
                   (rx[0][:, :], r2)]
        for l in (1, 2, 3):
            scales += [(nw1[l][:, 0:96], s32), (nw1[l][:, 96:], s64), (nw2[l][:, 96:], s64)]

        N_CLEAR = len(cleared)
        N_LOAD = 16 * len(loads)

        def tab_rows(tab, tr, width):
            if tr.g is not None and tr.g == NTRIPS - 1:
                return tab[N - NG:N, :].rearrange("(p j) f -> p j f", j=T)[:, :, 0:width]
            v = tab[0:NFULL * NG, :].rearrange("(g p j) f -> g p j f", p=NP, j=T)
            return v[tr.lin(1, 0)][:, :, 0:width]

        block = ctx.enter_context(nc.Block())

        @block.sync
        def _(sp):
            sp.dma_start(dst_i[:, :], A["dst"].rearrange("(p t) -> p t", t=ET)).then_inc(g_load, 16)
            sp.dma_start(hrow_i[:, :], A["dst"].rearrange("(a p t) -> t a p", a=1, t=ET)[0]
                         .broadcast_to((EP, EP)), allow_slow_non_contiguous=True).then_inc(g_load, 16)
            dcol = A["dst"].rearrange("(p t) -> p t", t=ET)
            sp.wait_ge(w_zero, 1)
            sp.dma_start(edge_i[1:EP, 0:1], dcol[0:EP - 1, 0:1],
                         allow_slow_non_contiguous=True).then_inc(g_load, 16)
            sp.dma_start(edge_i[1:EP, 1:2], dcol[0:EP - 1, ET - 1:ET],
                         allow_slow_non_contiguous=True).then_inc(g_load, 16)
            sp.dma_start(edge_i[2:EP, 2:3], dcol[0:EP - 2, ET - 1:ET],
                         allow_slow_non_contiguous=True).then_inc(g_load, 16)
            sp.wait_ge(w_zero, 1 + N_CLEAR)
            for dst, src in loads:
                sp.dma_start(dst, src, allow_slow_non_contiguous=True).then_inc(w_load, 16)
            sp.wait_ge(w_dve, GRAPH_STEPS)
            sp.dma_start(runs_d[:, :, :], runs[:, :, :]).then_inc(g_store, 16)
            sp.dma_start(scix_d[:, :], scix[:, :]).then_inc(g_store, 16)
            sp.wait_ge(g_store, 32)

            for l in range(4):
                ph, rad = f"E{l}", LAYERS[l]["rad"]
                es_v = ES[l].rearrange("(p g t) k -> g p (t k)", p=EP, t=T)
                y_v = A["edge_attr_4"].rearrange("(p g t) k -> g p t k", p=EP, t=T)
                k_v = runs_d.rearrange("p (g t) k -> g p t k", t=T)
                s_v = A["src"].rearrange("(p g t) -> g p t", p=EP, t=T)
                d_v = A["dst"].rearrange("(p g t) -> g p t", p=EP, t=T)
                sc_v = scix_d.rearrange("p (g t) -> g p t", t=T)

                def load_idx(tr):
                    sp.dma_start(gidx[tr.b][:, :], s_v[tr.lin(1, 0)]).then_inc(S2["idx"][tr.b], 16)
                    if l == 0:
                        sp.dma_start(gidx2[tr.b][:, :], d_v[tr.lin(1, 0)]).then_inc(S2["idx"][tr.b], 16)

                def load_attrs(tr):
                    sp.dma_start(es_in[tr.b][:, 0:T * rad], es_v[tr.lin(1, 0)]).then_inc(S2["lda"][tr.b], 16)
                    sp.dma_start(y_in[tr.b][:, :, :], y_v[tr.lin(1, 0)]).then_inc(S2["lda"][tr.b], 16)
                    sp.dma_start(k_in[tr.b][:, :, :], k_v[tr.lin(1, 0)]).then_inc(S2["lda"][tr.b], 16)

                for g in range(2):
                    load_idx(Trip(0, g))
                    load_attrs(Trip(0, g))

                def edge_trip(tr):
                    if tr.has(2, ETRIPS):
                        wait(sp, S2["gath"][tr.b], cnt2(ph, "gath", tr))
                        sp.sem_inc(sp_go, 1)
                        load_idx(tr.shift(2))
                        wait(sp, S["e_done"], cnt(ph, "e_done", tr))
                        sp.sem_inc(sp_go, 1)
                        wait(sp, S["pe_ring"], cnt(ph, "pe_ring", tr, (3 if l == 0 else 0) + 1))
                        sp.sem_inc(sp_go, 1)
                        load_attrs(tr.shift(2))
                    if tr.has(-2, ETRIPS):
                        wait(sp, S2["scat"][tr.b], cnt2(ph, "scat", tr.shift(-2)))
                        sp.sem_inc(sp_go, 1)
                    sp.dma_start(scid[tr.b][:, :], sc_v[tr.lin(1, 0)]).then_inc(S2["scid"][tr.b], 16)

                trips(sp, ETRIPS, edge_trip)

                for b in range(2):
                    sp.wait_ge(S2["scat"][b], total2(ph, "scat"))
                sp.dma_start(FX[:, :], agg[N:N + EP, :]).then_inc(fx_rd, 16)
                sp.wait_ge(fx_st, 16 * (l + 1))

                ph = f"N{l}"
                aw = H * (HC + 1) if l == 0 else LAYERS[l]["msg"]
                xw = F if l == 0 else XW

                def load_nodes(tr):
                    b = tr.b
                    sp.dma_start(X[b][:, :, 0:xw], tab_rows(TABLE[l], tr, xw)).then_inc(S2["nld"][b], 16)
                    sp.dma_start(AG[b][:, :, 0:aw], tab_rows(agg[0:N, :], tr, aw)).then_inc(S2["nld"][b], 16)
                    if l == 0:
                        sp.dma_start(XA[b][:, :], tab_rows(A["node_vec1"], tr, 1)
                                     .rearrange("p j f -> p (j f)")).then_inc(S2["nld"][b], 16)

                load_nodes(Trip(0, 0))

                def node_trip(tr):
                    b = tr.b
                    if tr.has(1, NTRIPS):
                        if tr.has(-1, NTRIPS):
                            wait(sp, S["r_done"], cnt(ph, "r_done", tr.shift(-1)))
                            wait(sp, S["a_done"], cnt(ph, "a_done", tr.shift(-1)))
                            sp.sem_inc(sp_go, 1)
                        load_nodes(tr.shift(1))
                    wait(sp, S["y_done"], cnt(ph, "y_done", tr))
                    sp.sem_inc(sp_go, 1)
                    if tr.g == NTRIPS - 1:
                        wait(sp, S2["nst"][1 - b], cnt2(ph, "nst", tr.shift(-1)))
                        sp.sem_inc(sp_go, 1)
                    sp.dma_start(tab_rows(NEXT[l], tr, XW if l < 3 else F),
                                 Y[b][:, :, 0:XW if l < 3 else F]).then_inc(S2["nst"][b], 16)

                trips(sp, NTRIPS, node_trip)
                for b in range(2):
                    sp.wait_ge(S2["nst"][b], total2(ph, "nst"))

        @block.gpsimd
        def _(gp):
            gp.memset(edge_i[:, :], -1).then_inc(w_zero, 1)
            for t in cleared:
                gp.memset(t[:, :], 0.0).then_inc(w_zero, 1)
            gp.memset(zeros[:, :], 0.0).then_inc(w_zero, 1)
            gp.memset(ident[:, :], 0.0).then_inc(w_zero, 1)
            gp.memset(ones_k[:, :], 1.0).then_inc(w_zero, 1)
            gp.memset(onerow[:, :], 1.0).then_inc(w_zero, 1)
            gp.memset(mhalf[:, :], -0.5).then_inc(w_zero, 1)
            gp.iota(pid[:, :], [[0, 1]], base=N, channel_multiplier=1).then_inc(w_zero, 1)
            gp.memset(O2[:, :, 48], 1.0).then_inc(w_zero, 1)
            gp.memset(wk_one[:, :], 1.0).then_inc(w_zero, 1)
            for b in range(2):
                gp.memset(OUT[b][:, :, :], 0.0).then_inc(w_zero, 1)
                gp.memset(mx[b][:, :], 0.0).then_inc(w_zero, 1)
            gp.wait_ge(w_zero, N_CLEAR + 13)
            gp.affine_select(out=ident[:, :], in_=ident[:, :], compare_op=ALU.not_equal, fill=1.0, base=0,
                             pattern=[[-1, 128]], channel_multiplier=1).then_inc(w_zero, 1)
            for l in range(4):
                ph = f"E{l}"
                if l:
                    for b in range(2):
                        gp.wait_ge(S2["nst"][b], total2(f"N{l - 1}", "nst"))

                def rows(dst, j, ids):
                    return gp.indirect_dma_start(dst[:, j, :], None, TABLE[l][:, :],
                                                 bass.IndirectOffsetOnAxis(ap=ids[:, j:j + 1], axis=0))

                def gathers(tr):
                    b = tr.b
                    wait(gp, S2["idx"][b], cnt2(ph, "idx", tr))
                    gp.sem_inc(go, 1)
                    if tr.has(-2, ETRIPS):
                        s = "xn_done" if l == 0 else "e_done"
                        wait(gp, S[s], cnt(ph, s, tr.shift(-2)))
                        gp.sem_inc(go, 1)
                    for j in range(T):
                        if l == 0:
                            rows(GS[b], j, gidx[b]).then_inc(S2["gath"][b], 16)
                            rows(GD[b], j, gidx2[b]).then_inc(S2["gath"][b], 16)
                        else:
                            rows(G[b], j, gidx[b]).then_inc(S2["gath"][b], 16)

                def scatters(tr):
                    b = tr.b
                    wait(gp, S2["scid"][b], cnt2(ph, "scid", tr))
                    gp.sem_inc(go, 1)
                    wait(gp, S["msg_done"], cnt(ph, "msg_done", tr))
                    gp.sem_inc(go, 1)
                    if tr.g == 0 and l == 0:
                        gp.wait_ge(z_store, 16 * 24)
                        gp.sem_inc(go, 1)
                    for j in range(T):
                        gp.indirect_dma_start(agg[:, :], bass.IndirectOffsetOnAxis(ap=scid[b][:, j:j + 1], axis=0),
                                              OUT[b][:, j, :], None, bounds_check=AROWS - 1, oob_is_err=False)\
                          .then_inc(S2["scat"][b], 16)

                def inv_norms(tr):
                    gp.wait_ge(S["stat_done"], cnt(ph, "stat_done", tr))
                    gp.sem_inc(go, 1)
                    c = Chain(gp, S, ph, "gp", tr, go)
                    c.step(gp.tensor_scalar(lrs[:, :, :], lst[:, :, 1:3], 1e-5, None, ALU.add))
                    gp.tensor_tensor(lrs[:, :, :].rearrange("p a b -> p (a b)"),
                                     lrs[:, :, :].rearrange("p a b -> p (a b)"),
                                     mhalf[0:EP, 0:4 * T], ALU.pow).then_inc(S["pow_done"], 1)
                    c.end()

                gathers(Trip(0, 0))
                gathers(Trip(0, 1))
                if l == 0:
                    inv_norms(Trip(0, 0))

                def edge_trip(tr):
                    if l == 0 and tr.has(1, ETRIPS):
                        inv_norms(tr.shift(1))
                    if tr.has(2, ETRIPS):
                        gathers(tr.shift(2))
                    if tr.has(-1, ETRIPS):
                        scatters(tr.shift(-1))

                trips(gp, ETRIPS, edge_trip)
                scatters(Trip(0, ETRIPS - 1))

                for b in range(2):
                    gp.wait_ge(S2["scat"][b], total2(ph, "scat"))
                gp.indirect_dma_start(FB[:, :], None, agg[:, :],
                                      bass.IndirectOffsetOnAxis(ap=head_i[:, 0:1], axis=0)).then_inc(fx_g, 16)
                gp.wait_ge(fx_dve, FIX_STEPS[l])
                gp.indirect_dma_start(agg[:, :], bass.IndirectOffsetOnAxis(ap=fixid[:, 0:1], axis=0),
                                      FN[:, :], None, bounds_check=AROWS - 1, oob_is_err=False).then_inc(fx_st, 16)

                ph = f"N{l}"

                def node_rstd(tr):
                    b = tr.b
                    gp.wait_ge(S["r_done"], cnt(ph, "r_done", tr))
                    if tr.has(-2, NTRIPS):
                        wait(gp, S["y_done"], cnt(ph, "y_done", tr.shift(-2)))
                    gp.sem_inc(go, 1)
                    c = Chain(gp, S, ph, "gpn", tr, go)
                    c.step(gp.tensor_scalar(nrs[b][:, :, 0], nmv[b][:, :, 1], 1e-5, None, ALU.add))
                    c.step(gp.tensor_tensor(nrs[b][:, :, 0], nrs[b][:, :, 0], mhalf[:, 0:T], ALU.pow))
                    c.step(gp.tensor_scalar(nrs[b][:, :, 1], nmv[b][:, :, 0], -1.0, None, ALU.mult))
                    gp.tensor_tensor(nrs[b][:, :, 1], nrs[b][:, :, 1], nrs[b][:, :, 0], ALU.mult)\
                      .then_inc(S["rstd_done"], 1)
                    c.end()

                def attr_out(tr):
                    b = tr.b
                    if tr.has(-2, NTRIPS):
                        wait(gp, S2["nst"][b], cnt2(ph, "nst", tr.shift(-2)))
                    gp.sem_inc(go, 1)
                    src = XA[b][:, :] if l == 0 else X[b][:, :, ATTR]
                    gp.tensor_copy(Y[b][:, :, ATTR], src).then_inc(S["a_done"], 1)

                def node_trip(tr):
                    b = tr.b
                    gp.wait_ge(S2["nld"][b], cnt2(ph, "nld", tr))
                    att = X[b][:, :, ATTR]
                    c = Chain(gp, S, ph, "gp", tr, go)
                    if l == 1:
                        if tr.has(-1, NTRIPS):
                            gp.wait_ge(S["sin_done"], cnt(ph, "sin_done", tr.shift(-1)))
                        c.step(gp.tensor_tensor(ang[:, 0:T], AG[b][:, :, F], att, ALU.mult))
                        c.step(gp.tensor_scalar(ang[:, T:], ang[:, 0:T], HALF_PI, None, ALU.add))
                        c.step(gp.tensor_scalar(angk[:, :], ang[:, :], INV_2PI, MAGIC, ALU.mult, ALU.add))
                        c.step(gp.tensor_scalar(angk[:, :], angk[:, :], -MAGIC, None, ALU.add))
                        for part in TWO_PI:
                            c.step(gp.tensor_scalar(angr[:, :], angk[:, :], -part, None, ALU.mult))
                            c.step(gp.tensor_tensor(ang[:, :], ang[:, :], angr[:, :], ALU.add))
                        gp.tensor_scalar(angr[:, :], ang[:, :], PI, -PI, ALU.min, ALU.max)\
                          .then_inc(S["ang_done"], 1)
                        gp.wait_ge(S["sin_done"], cnt(ph, "sin_done", tr))
                        if tr.has(-2, NTRIPS):
                            wait(gp, S["r_done"], cnt(ph, "r_done", tr.shift(-2)))
                        gp.tensor_tensor(co[b][:, 0:T], sc8[:, T:], att, ALU.mult).then_inc(S["coef_done"], 1)
                        c.step(gp.tensor_tensor(co[b][:, T:], sc8[:, 0:T], att, ALU.mult))
                    if l == 2:
                        gp.wait_ge(S["ang_done"], cnt(ph, "ang_done", tr))
                        c.step(gp.tensor_tensor(co[b][:, T:], co[b][:, T:], att, ALU.mult))
                        c.step(gp.tensor_tensor(co[b][:, 0:T], co[b][:, T:], co[b][:, T:], ALU.mult))
                        c.step(gp.tensor_tensor(co[b][:, T:], co[b][:, 0:T], AG[b][:, :, F], ALU.mult))
                    if l in (1, 2):
                        gp.tensor_tensor(T2B[b][:, :, :], AG[b][:, :, 0:F],
                                         co[b][:, T:].unsqueeze(2).broadcast_to((NP, T, F)), ALU.mult)\
                          .then_inc(S["t2_done"], 1)
                    c.end()
                    attr_out(tr)
                    if tr.has(-1, NTRIPS):
                        node_rstd(tr.shift(-1))

                trips(gp, NTRIPS, node_trip)
                node_rstd(Trip(0, NTRIPS - 1))

        @block.scalar
        def _(ac):
            ac.wait_ge(w_zero, N_CLEAR + 2)
            az = agg.rearrange("(p r) f -> p (r f)", p=128)
            for i in range(24):
                ac.dma_start(az[:, 3136 * i:3136 * (i + 1)], zeros[:, :]).then_inc(z_store, 16)
            ac.wait_ge(w_zero, N_CLEAR + 1)
            ac.wait_ge(w_pe, 1)
            ac.copy(wvt[:, 0:96], psR[0:CS, 0, 0:96]).then_inc(w_act, 1)
            ac.copy(wvt[:, 192:224], psR[0:CS, 0, 64:96]).then_inc(w_act, 1)
            ac.wait_ge(w_pe, 2)
            ac.wait_ge(w_load, N_LOAD)
            ac.copy(ra[0][0:64, 128:160], psR[0:64, 1, 0:32]).then_inc(w_act, 1)
            ac.copy(rb[0][0:32, 224:256], psR[0:32, 2, 0:32]).then_inc(w_act, 1)
            ac.wait_ge(w_pe, 3)
            ac.copy(brow[0:1, 96:160], psF[0:1, 0, 0:64]).then_inc(w_act, 1)

            for l in range(4):
                ph, rad, R_ = f"E{l}", LAYERS[l]["rad"], ring_banks(l)

                def evac(tr, k, dst, rows, cols, func=ACT.Copy, scale=1.0):
                    pos = ring_pos(l, tr, k)
                    ac.wait_ge(S["pe_ring"], ring_val(ph, l, tr, k))
                    ac.activation(dst, psR[0:rows, pos % R_, 0:cols], func, scale=scale)\
                      .then_inc(S["act_ring"], 1)

                def squares(tr):
                    ac.wait_ge(S2["gath"][tr.b], cnt2(ph, "gath", tr))
                    if tr.has(-1, ETRIPS):
                        ac.wait_ge(S["stat_done"], cnt(ph, "stat_done", tr.shift(-1)))
                    ac.activation(sqv[:, 0:T, :], GS[tr.b][:, :, CS:F], ACT.Square, scale=CV ** -0.5)
                    ac.activation(sqv[:, T:, :], GD[tr.b][:, :, CS:F], ACT.Square, scale=CV ** -0.5)\
                      .then_inc(S["sq_done"], 1)

                def norm_and_messages(tr):
                    for c in range(3):
                        evac(tr, f"n{c}", ET_[c][0:(64 if c == 2 else 128), :], 64 if c == 2 else 128, EC)
                    ac.wait_ge(S["ob_full"], ob_val(ph, tr, "M"))
                    ac.copy(MG[:, :, :].rearrange("p (b t) f -> p b (t f)", b=2), psO[0:EP, :, 0:2 * F])\
                      .then_inc(S["ob_evac"], 1)

                if l == 0:
                    squares(Trip(0, 0))
                    norm_and_messages(Trip(0, 0))

                def edge_trip(tr):
                    nc_ = CHUNKS[l]
                    if l == 0:
                        if tr.has(1, ETRIPS):
                            squares(tr.shift(1))
                        evac(tr, "e", esT[0:16, :], 16, EC)
                    else:
                        evac(tr, "e", esT[0:rad, :], rad, EC)
                        evac(tr, "h", hidT[:, :], CS, EC, ACT.Silu)
                    for c in range(nc_):
                        w = 96 if c == 2 else 128
                        evac(tr, f"w{c}", wT[c][0:w, :], w, EC)
                    if l == 0:
                        for h in range(2):
                            ac.wait_ge(S["ob_full"], ob_val(ph, tr, f"o{h}"))
                            ac.copy(O[0][:, 2 * h:2 * h + 2, :], psO[0:EP, :, 0:288]).then_inc(S["ob_evac"], 1)
                        ac.wait_ge(S["ob_evac"], ob_val(ph, tr, "o1"))
                        ac.activation(SG[:, :, :], O[0][:, :, 160:256], ACT.Tanh, scale=0.5)\
                          .then_inc(S["tanh_done"], 1)
                        if tr.has(1, ETRIPS):
                            norm_and_messages(tr.shift(1))
                        ac.wait_ge(S["d_ready"], cnt(ph, "d_ready", tr))
                        ac.activation(pc[:, :, :], dd[:, :, :], ACT.Exp).then_inc(S["exp_done"], 1)
                    for c in range(nc_):
                        w = 96 if c == 2 else 128
                        evac(tr, f"t{c}", ET_[c][0:w, :], w, EC)
                    if l == 0:
                        ac.wait_ge(S["ob_full"], ob_val(ph, tr, "O2"))
                        ac.copy(O2[:, :, 0:48].rearrange("p (b t) f -> p b t f", b=2),
                                psO[0:EP, :, 0:384].rearrange("p b (t f) -> p b t f", t=2 * H))\
                          .then_inc(S["ob_evac"], 1)
                    else:
                        w = EOW[l]
                        ac.wait_ge(S["ob_full"], cnt(ph, "ob_full", tr))
                        ac.copy(O[tr.b][:, :, 0:w].rearrange("p (b t) f -> p b t f", b=2),
                                psO[0:EP, :, 0:2 * w].rearrange("p b (t f) -> p b t f", t=2))\
                          .then_inc(S["ob_evac"], 1)

                trips(ac, ETRIPS, edge_trip)
                if l == 0:
                    ac.wait_ge(fx_dve, 3)
                    ac.activation(fm[:, 2:4, :], fm[:, 2:4, :], ACT.Exp).then_inc(fx_act, 1)

                ph = f"N{l}"

                def normed(tr):
                    b = tr.b
                    ac.wait_ge(S["rstd_done"], cnt(ph, "rstd_done", tr))
                    if tr.has(-2, NTRIPS):
                        wait(ac, S2["nst"][b], cnt2(ph, "nst", tr.shift(-2)))
                    ac.wait_ge(S["a_done"], cnt(ph, "a_done", tr))
                    for j in range(T):
                        last = ac.activation(Y[b][:, j, 0:F], R[b][:, j, 0:F], ACT.Identity,
                                             bias=nrs[b][:, j, 1:2], scale=nrs[b][:, j, 0:1])
                    last.then_inc(S["y_done"], 1)

                def node_trip(tr):
                    for k, dst, rows in ((0, NT1, 128), (1, NT2, 32)):
                        ac.wait_ge(S["pe_ring"], cnt(ph, "pe_ring", tr, k + 1))
                        ac.copy(dst[:, :], psR[0:rows, k, :]).then_inc(S["act_ring"], 1)
                    if l == 1:
                        ac.wait_ge(S["ang_done"], cnt(ph, "ang_done", tr))
                        if tr.has(-1, NTRIPS):
                            ac.wait_ge(S["t2_done"], cnt(ph, "t2_done", tr.shift(-1)))
                        ac.activation(sc8[:, :], angr[:, :], ACT.Sin).then_inc(S["sin_done"], 1)
                    if tr.has(-1, NTRIPS):
                        normed(tr.shift(-1))
                    if l == 3:
                        ac.wait_ge(S["gate_in"], cnt(ph, "gate_in", tr))
                        ac.activation(SGN[:, :, :], R3[:, :, 96:192], ACT.Sigmoid).then_inc(S["sig_done"], 1)

                trips(ac, NTRIPS, node_trip)
                normed(Trip(0, NTRIPS - 1))

        @block.tensor
        def _(pe):
            def tr_(dst, src, parts):
                return pe.transpose(dst, src, ident[0:parts, 0:parts])

            pe.wait_ge(w_zero, N_CLEAR + 14)
            pe.wait_ge(w_load, N_LOAD)
            tr_(psR[0:CS, 0, 0:96], wval[:, :], 96).then_inc(w_pe, 1)
            pe.wait_ge(w_act, 2)
            pe.matmul(psR[0:64, 1, 0:32], wvt[:, 0:64], wg[:, :], start=True, stop=True)
            pe.matmul(psR[0:32, 2, 0:32], wvt[:, 192:224], wg[:, :], start=True, stop=True).then_inc(w_pe, 1)
            pe.matmul(psF[0:1, 0, 0:64], beta[:, :], wsrc[:, :], start=True, stop=False)
            pe.matmul(psF[0:1, 0, 0:64], beta[:, :], wdst[:, :], start=False, stop=True).then_inc(w_pe, 1)
            pe.wait_ge(w_act, 5)
            pe.wait_ge(w_dve, SETUP_STEPS)

            for l in range(4):
                ph, rad, R_ = f"E{l}", LAYERS[l]["rad"], ring_banks(l)
                nc_ = CHUNKS[l]
                if l:
                    pe.wait_ge(S["act_ring"], total(f"N{l - 1}", "act_ring"))
                    pe.wait_ge(S["ob_used"], total(f"N{l - 1}", "ob_used"))

                def slot(tr, k):
                    pos = ring_pos(l, tr, k)
                    v = ring_val(ph, l, tr, k)
                    base = BASE[ph].get("act_ring", 0)
                    if not isinstance(v, int) or v - base > R_:
                        pe.wait_ge(S["act_ring"], v - R_)
                        pe.sem_inc(pe_go, 1)
                    return psR[:, pos % R_, :]

                def out_of_ring(tr, k):
                    pe.wait_ge(S["act_ring"], ring_val(ph, l, tr, k))

                def ob_free(v):
                    if not isinstance(v, int) or v > BASE[ph].get("ob_evac", 0) + 1:
                        pe.wait_ge(S["ob_evac"], v - 1)

                def norm_and_messages(tr):
                    pe.wait_ge(S["xn_done"], cnt(ph, "xn_done", tr))
                    for c in range(3):
                        bank = slot(tr, f"n{c}")
                        for j in range(T):
                            if c < 2:
                                last = tr_(bank[:, j * EP:(j + 1) * EP], XN[:, j, c, 0:128], EP)
                            else:
                                last = tr_(bank[0:64, j * EP:(j + 1) * EP], XT[:, j, :], EP)
                        last.then_inc(S["pe_ring"], 1)
                    out_of_ring(tr, "n2")
                    ob_free(ob_val(ph, tr, "M"))
                    for j in range(T):
                        dst, at = psO[0:EP, j // 2, F * (j % 2):F * (j % 2) + F], slice(j * EP, (j + 1) * EP)
                        pe.matmul(dst, onerow[:, :], brow[:, :], start=True, stop=False)
                        pe.matmul(dst, ET_[0][:, at], wm_s[:, :], start=False, stop=False)
                        pe.matmul(dst, ET_[1][:, at], wm_d[:, :], start=False, stop=False)
                        last = pe.matmul(dst, ET_[2][0:64, at], wm_t[:, :], start=False, stop=True)
                    last.then_inc(S["ob_full"], 1)

                if l == 0:
                    norm_and_messages(Trip(0, 0))

                def edge_trip(tr):
                    b = tr.b
                    pe.wait_ge(S2["lda"][b], cnt2(ph, "lda", tr))
                    bank = slot(tr, "e")
                    for j in range(T):
                        last = tr_(bank[0:rad, j * EP:(j + 1) * EP], es_in[b][:, j * rad:(j + 1) * rad], EP)
                    last.then_inc(S["pe_ring"], 1)
                    out_of_ring(tr, "e")
                    pe.sem_inc(pe_go, 1)
                    src = esT[0:rad, :]
                    if l:
                        bank = slot(tr, "h")
                        pe.matmul(bank[0:CS, 0:EC], fc1[l][:, :], src, start=True, stop=True)\
                          .then_inc(S["pe_ring"], 1)
                        out_of_ring(tr, "h")
                        pe.sem_inc(pe_go, 1)
                        src = hidT[:, :]
                    for c in range(nc_):
                        w = 96 if c == 2 else 128
                        bank = slot(tr, f"w{c}")
                        pe.matmul(bank[0:w, 0:EC], fc2[l][:, 128 * c:128 * c + w], src, start=True, stop=True)\
                          .then_inc(S["pe_ring"], 1)
                    pe.wait_ge(S["e_done"], cnt(ph, "e_done", tr))
                    if l == 0:
                        for c in range(3):
                            w = 96 if c == 2 else 128
                            for j in range(T):
                                last = tr_(psF[0:w, c, j * EP:(j + 1) * EP], EE[:, j, 128 * c:128 * c + w], EP)
                            last.then_inc(S["f_done"], 1)
                    else:
                        for c in range(nc_):
                            w = 96 if c == 2 else 128
                            bank = slot(tr, f"t{c}")
                            for j in range(T):
                                last = tr_(bank[0:w, j * EP:(j + 1) * EP], EE[:, j, 128 * c:128 * c + w], EP)
                            last.then_inc(S["pe_ring"], 1)
                        for c in range(nc_):
                            w = 96 if c == 2 else 128
                            out_of_ring(tr, f"t{c}")
                            wf = wf1[l] if c == 1 else wf2[l]
                            pe.matmul(psF[0:w, c, 0:EC], wf[0:w, 0:w], ET_[c][0:w, :], start=True, stop=True)\
                              .then_inc(S["f_done"], 1)
                    pe.wait_ge(S["prod_done"], cnt(ph, "prod_done", tr, nc_))
                    w = EOW[l]
                    per_bank = 1 if l == 0 else 2
                    for j in range(T):
                        if j % (2 * per_bank) == 0:
                            if l == 0:
                                ob_free(ob_val(ph, tr, f"o{j // 2}"))
                            else:
                                ob_free(cnt(ph, "ob_evac", tr))
                        o = w * (j % per_bank)
                        dst = psO[0:EP, (j // per_bank) % 2, :]
                        at = slice(j * EP, (j + 1) * EP)
                        pe.matmul(dst[:, o:o + w], PR[0][:, at], rb[l][:, :], start=True, stop=True)
                        if nc_ == 3:
                            pe.matmul(dst[:, o:o + 96], PR[2][0:96, at], rx[l][:, :], start=False, stop=True,
                                      skip_group_check=True)
                        last = pe.matmul(dst[:, o + 96:o + w], PR[1][:, at], ra[l][:, :], start=False, stop=True,
                                         skip_group_check=True)
                        if j % (2 * per_bank) == 2 * per_bank - 1:
                            last.then_inc(S["ob_full"], 1)
                    if l == 0:
                        if tr.has(1, ETRIPS):
                            norm_and_messages(tr.shift(1))
                        pe.wait_ge(S["e2_done"], cnt(ph, "e2_done", tr))
                        for c in range(3):
                            w = 96 if c == 2 else 128
                            bank = slot(tr, f"t{c}")
                            for j in range(T):
                                last = tr_(bank[0:w, j * EP:(j + 1) * EP], E2[:, j, 128 * c:128 * c + w], EP)
                            last.then_inc(S["pe_ring"], 1)
                        out_of_ring(tr, "t2")
                        ob_free(ob_val(ph, tr, "O2"))
                        for j in range(T):
                            dst, at = psO[0:EP, j // 2, 192 * (j % 2):192 * (j % 2) + 192], slice(j * EP, (j + 1) * EP)
                            pe.matmul(dst, ET_[1][:, at], r2a[:, :], start=True, stop=False)
                            pe.matmul(dst, ET_[0][:, at], r2b[:, :], start=False, stop=False)
                            last = pe.matmul(dst, ET_[2][0:96, at], r2x[:, :], start=False, stop=True)
                        last.then_inc(S["ob_full"], 1)

                trips(pe, ETRIPS, edge_trip)

                pe.wait_ge(S["ob_evac"], total(ph, "ob_evac"))
                if l == 0:
                    pe.wait_ge(fx_dve, 1)
                    pe.matmul(psF[0:EP, 0, 0:H * EP], ones_k[:, :], fdg[:, :], start=True, stop=True)\
                      .then_inc(fx_mm, 1)
                    pe.wait_ge(fx_dve, 4)
                else:
                    pe.wait_ge(fx_rd, 16 * (l + 1))
                pe.matmul(psO[0:EP, 0, 0:AW], same[:, :], FX[:, :], start=True, stop=True).then_inc(fx_mm, 1)

                ph = f"N{l}"
                pe.wait_ge(fx_dve, FIX_STEPS[l])
                pe.wait_ge(S["act_ring"], total(f"E{l}", "act_ring"))

                def node_trip(tr):
                    b, w = tr.b, NOW[l]
                    if l == 0:
                        pe.wait_ge(S["agn_done"], cnt(ph, "agn_done", tr))
                        src = AGN
                    else:
                        pe.wait_ge(S2["nld"][b], cnt2(ph, "nld", tr))
                        src = X[b]
                    for k, rows in ((0, 128), (1, 32)):
                        if tr.has(-1, NTRIPS):
                            pe.wait_ge(S["act_ring"], cnt(ph, "act_ring", tr.shift(-1), k + 1))
                        for j in range(T):
                            last = tr_(psR[0:rows, k, j * NP:(j + 1) * NP], src[:, j, 128 * k:128 * k + rows], NP)
                        last.then_inc(S["pe_ring"], 1)
                    pe.wait_ge(S["act_ring"], cnt(ph, "act_ring", tr, 2))
                    if tr.has(-1, NTRIPS):
                        pe.wait_ge(S["ob_used"], cnt(ph, "ob_used", tr.shift(-1)))
                    for j in range(T):
                        dst, at = psO[:, j // 2, w * (j % 2):w * (j % 2) + w], slice(j * NP, (j + 1) * NP)
                        pe.matmul(dst, NT1[:, at], nw1[l][:, :], start=True, stop=False)
                        last = pe.matmul(dst, NT2[:, at], nw2[l][:, :], start=False, stop=True)
                    last.then_inc(S["ob_full"], 1)

                trips(pe, NTRIPS, node_trip)

        @block.vector
        def _(ve):
            n = [0]

            def step(ins):
                n[0] += 1
                ins.then_inc(w_dve, 1)
                ve.wait_ge(w_dve, n[0])

            def bc(ap, shape):
                return ap.broadcast_to(shape)

            ve.wait_ge(w_zero, N_CLEAR + 14)
            ve.wait_ge(g_load, 80)
            step(ve.tensor_copy(dst_f[:, :], dst_i[:, :]))
            step(ve.tensor_copy(edge_f[:, :], edge_i[:, :]))
            step(ve.tensor_copy(hrow[:, :], hrow_i[:, :]))
            step(ve.tensor_copy(cf[:, 0:1], pid[:, :]))
            step(ve.tensor_copy(head_i[:, :], dst_i[:, 0:1]))
            step(ve.tensor_scalar(cf[:, 1:2], cf[:, 0:1], float(SKIP - N), None, ALU.add))
            keep, mask = runs[:, :, 0], runs[:, :, 1]
            step(ve.memset(wk1[:, :], 0.0))
            step(ve.tensor_tensor(wk1[:, 1:ET], dst_f[:, 1:ET], dst_f[:, 0:ET - 1], ALU.is_equal))
            step(ve.tensor_copy(keep, wk1[:, :]))
            step(ve.tensor_scalar(mask, wk1[:, :], -1.0, BIG, ALU.add, ALU.mult))
            step(ve.tensor_tensor_scan(wk2[:, :], wk1[:, :], wk_one[:, :], 0.0, ALU.mult, ALU.add))
            step(ve.tensor_copy(runs[:, :, 2], wk2[:, :]))
            step(ve.tensor_tensor(cf[:, 2:3], dst_f[:, 0:1], edge_f[:, 1:2], ALU.is_equal))
            step(ve.tensor_tensor(cf[:, 4:5], dst_f[:, 0:1], edge_f[:, 0:1], ALU.is_equal))
            step(ve.tensor_tensor(cf[:, 5:6], edge_f[:, 0:1], edge_f[:, 2:3], ALU.is_equal))
            step(ve.tensor_tensor(cf[:, 4:5], cf[:, 4:5], cf[:, 5:6], ALU.mult))
            step(ve.tensor_scalar(cf[:, 4:5], cf[:, 4:5], -1.0, 1.0, ALU.mult, ALU.add))
            step(ve.tensor_tensor(cf[:, 3:4], cf[:, 2:3], cf[:, 4:5], ALU.mult))
            step(ve.tensor_tensor(cf[:, 6:7], dst_f[:, 0:1], cf[:, 1:2], ALU.subtract))
            step(ve.tensor_tensor(cf[:, 6:7], cf[:, 6:7], cf[:, 3:4], ALU.mult))
            step(ve.tensor_tensor(cf[:, 6:7], cf[:, 6:7], cf[:, 1:2], ALU.add))
            step(ve.tensor_copy(fixid[:, :], cf[:, 6:7]))
            step(ve.tensor_scalar(wk2[:, :], dst_f[:, :], dst_f[:, 0:1], cf[:, 2:3], ALU.is_equal, ALU.mult))
            step(ve.tensor_scalar(wk1[:, :], dst_f[:, :], cf[:, 0:1], -1.0, ALU.subtract, ALU.mult))
            step(ve.tensor_tensor(wk1[:, :], wk1[:, :], wk2[:, :], ALU.mult))
            step(ve.tensor_tensor(wk1[:, :], wk1[:, :], dst_f[:, :], ALU.add))
            step(ve.tensor_scalar(wk1[:, :], wk1[:, :], cf[:, 1:2], None, ALU.subtract))
            step(ve.memset(wk2[:, :], 1.0))
            step(ve.tensor_scalar(wk2[:, 0:ET - 1], runs[:, 1:ET, 0], -1.0, 1.0, ALU.mult, ALU.add))
            step(ve.tensor_tensor(wk1[:, :], wk1[:, :], wk2[:, :], ALU.mult))
            step(ve.tensor_scalar(wk1[:, :], wk1[:, :], cf[:, 1:2], None, ALU.add))
            step(ve.tensor_copy(scix[:, :], wk1[:, :]))
            step(ve.tensor_scalar(same[:, :], hrow[:, :], dst_f[:, 0:1], None, ALU.is_equal))
            step(ve.tensor_scalar(samen[:, :], same[:, :], -1.0, BIG, ALU.add, ALU.mult))
            assert n[0] == GRAPH_STEPS, n
            ve.wait_ge(w_load, N_LOAD)
            ve.wait_ge(w_act, 5)
            for region, factor in scales:
                step(ve.tensor_scalar(region, region, factor, None, ALU.mult))
            step(ve.tensor_scalar(rb[0][0:32, 96:256], rb[0][0:32, 96:256], r3, None, ALU.mult))
            for t, g in ((wm_s, g1), (wm_d, g1), (wm_t, g3), (r2a, cA), (r2b, cB), (r2x, cX)):
                step(ve.tensor_scalar(t[:, :], t[:, :], g[:, 0:1], None, ALU.mult))
            step(ve.tensor_scalar(r2b[0:32, :], r2b[0:32, :], r3, None, ALU.mult))
            step(ve.tensor_scalar(r2x[:, :], r2x[:, :], r2, None, ALU.mult))
            assert n[0] == SETUP_STEPS, n

            fx = [0]

            def fstep(ins, own=False):
                fx[0] += 1
                ins.then_inc(fx_dve, 1)
                ve.wait_ge(fx_dve, fx[0])

            for l in range(4):
                ph, nc_, cross = f"E{l}", CHUNKS[l], LAYERS[l]["cross"]

                def attrs(tr, c):
                    b = tr.b
                    wait(ve, S2["lda"][b], cnt2(ph, "lda", tr))
                    if l == 0:
                        ve.tensor_copy(yc[b][:, :, 0:4], y_in[b][:, :, :])
                        ve.tensor_copy(yc[b][:, :, 4:6], y_in[b][:, :, 1:3])
                    else:
                        att = G[b][:, :, ATTR:ATTR + 1]
                        ve.tensor_tensor(yc[b][:, :, 0:4], y_in[b][:, :, :], bc(att, (EP, T, 4)), ALU.mult)
                        ve.tensor_tensor(yc[b][:, :, 4:6], y_in[b][:, :, 1:3], bc(att, (EP, T, 2)), ALU.mult)
                    c.step(ve.tensor_copy(kc[b][:, :, :], k_in[b][:, :, :]))

                def tp_inputs(src, y, dst, c, done):
                    v = src[:, :, 0:96].rearrange("p t (d c) -> p t d c", d=3)
                    sh = (EP, T, 3, CV)

                    def times(out, vd, yd, m):
                        return ve.tensor_tensor(out, v[:, :, vd:vd + m, :],
                                                bc(y[:, :, yd:yd + m].unsqueeze(3), (EP, T, m, CV)), ALU.mult)

                    t4 = tmp[:, :, :].rearrange("p t (d c) -> p t d c", d=3)
                    t5 = tmp2[:, :, :].rearrange("p t (d c) -> p t d c", d=3)
                    times(t4, 0, 1, 3)
                    if cross:
                        x4 = dst[:, :, C_X:C_X + 96].rearrange("p t (d c) -> p t d c", d=3)
                        times(x4[:, :, 0:2, :], 1, 3, 2)
                        times(x4[:, :, 2:3, :], 0, 5, 1)
                        times(t5[:, :, 0:1, :], 2, 2, 1)
                        times(t5[:, :, 1:3, :], 0, 3, 2)
                    ve.tensor_copy(dst[:, :, C_S:C_S + CS], src[:, :, 96:F])
                    c.step(ve.tensor_tensor(dst[:, :, C_YV:C_YV + F], src[:, :, 0:F],
                                            bc(y[:, :, 0:1], (EP, T, F)), ALU.mult))
                    if cross:
                        xs = dst[:, :, C_X:C_X + 96]
                        ve.tensor_tensor(xs, xs, tmp2[:, :, :], ALU.subtract)
                    ve.tensor_reduce(dst[:, :, C_VY:C_VY + CV], tmp[:, :, :].rearrange("p t (d c) -> p t c d", d=3),
                                     AX.X, ALU.add).then_inc(S[done], 1)

                def inputs(tr):
                    b = tr.b
                    c = Chain(ve, S, ph, "d_in", tr)
                    if l == 0:
                        ve.wait_ge(S["ob_evac"], ob_val(ph, tr, "M"))
                        src = MG
                    else:
                        ve.wait_ge(S2["gath"][b], cnt2(ph, "gath", tr))
                        src = G[b]
                    attrs(tr, c)
                    tp_inputs(src, yc[b], EE, c, "e_done")
                    c.end()

                def products(tr):
                    for c in range(nc_):
                        w = 96 if c == 2 else 128
                        ve.wait_ge(S["f_done"], cnt(ph, "f_done", tr, c + 1))
                        if c == 0:
                            ve.wait_ge(S["act_ring"], ring_val(ph, l, tr, f"w{nc_ - 1}"))
                        ve.tensor_tensor(PR[c][0:w, :], psF[0:w, c, 0:EC], wT[c][0:w, :], ALU.mult)\
                          .then_inc(S["prod_done"], 1)

                def times_u(o, uo, y, c):
                    u = o[:, :, uo:uo + CV].unsqueeze(2)
                    t4 = tmp3[:, :, :].rearrange("p t (d c) -> p t d c", d=3)
                    c.step(ve.tensor_tensor(t4, bc(u, (EP, T, 3, CV)), bc(y[:, :, 1:4].unsqueeze(3), (EP, T, 3, CV)),
                                            ALU.mult))
                    c.step(ve.tensor_tensor(o[:, :, 0:96], o[:, :, 0:96], tmp3[:, :, :], ALU.add))

                def out_free(tr):
                    if tr.has(-2, ETRIPS):
                        wait(ve, S2["scat"][tr.b], cnt2(ph, "scat", tr.shift(-2)))

                def messages(tr):
                    b = tr.b
                    c = Chain(ve, S, ph, "d_post", tr)
                    w = EOW[l] - 32
                    ve.wait_ge(S["ob_evac"], cnt(ph, "ob_evac", tr))
                    times_u(O[b], w, yc[b], c)
                    out_free(tr)
                    if l == 2:
                        ve.tensor_copy(OUT[b][:, :, w], kc[b][:, :, 2])
                    for t in range(T):
                        prev = OUT[b][:, t - 1, 0:w] if t else OUT[1 - b][:, T - 1, 0:w]
                        ins = ve.scalar_tensor_tensor(OUT[b][:, t, 0:w], prev, kc[b][:, t, 0:1], O[b][:, t, 0:w],
                                                      op0=ALU.mult, op1=ALU.add)
                        if t < T - 1:
                            c.step(ins)
                    ins.then_inc(S["msg_done"], 1)
                    ve.wait_ge(S["msg_done"], cnt(ph, "msg_done", tr))
                    c.end()

                def norm_stats(tr):
                    b = tr.b
                    c = Chain(ve, S, ph, "d_norm", tr)
                    ve.wait_ge(S2["gath"][b], cnt2(ph, "gath", tr))
                    for i in range(2 * T):
                        src = (GS, GD)[i // T][b]
                        ins = ve.bn_stats(bst[:, i, :], src[:, i % T, 0:CS])
                    c.step(ins)
                    ve.sem_inc(ve_go, 1)
                    for i in range(2 * T):
                        ve.bn_aggr(lst[:, i, 0:2], bst[:, i, :])
                    ve.wait_ge(S["sq_done"], cnt(ph, "sq_done", tr))
                    ve.tensor_reduce(lst[:, :, 2], sqv[:, :, :], AX.X, ALU.add).then_inc(S["stat_done"], 1)
                    ve.wait_ge(S["stat_done"], cnt(ph, "stat_done", tr))
                    c.end()

                def norm_rows(tr):
                    b = tr.b
                    ve.wait_ge(S["pow_done"], cnt(ph, "pow_done", tr))
                    for i in range(2 * T):
                        src = (GS, GD)[i // T][b]
                        o = XN[:, i % T, i // T, 96:F]
                        ve.tensor_scalar(o, src[:, i % T, 0:CS], lst[:, i, 0:1], lrs[:, i, 0:1],
                                         ALU.subtract, ALU.mult)
                        ve.tensor_scalar(XT[:, i % T, 32 * (i // T):32 * (i // T) + 32], src[:, i % T, 32:CS],
                                         lst[:, i, 0:1], lrs[:, i, 0:1], ALU.subtract, ALU.mult)
                    for side in range(2):
                        src = (GS, GD)[side][b][:, :, CS:F].rearrange("p t (c d) -> p t d c", d=3)
                        ins = ve.tensor_tensor(XN[:, :, side, 0:96].rearrange("p t (d c) -> p t d c", d=3), src,
                                               bc(lrs[:, side * T:side * T + T, 1:2].unsqueeze(3), (EP, T, 3, CV)),
                                               ALU.mult)
                    ins.then_inc(S["xn_done"], 1)

                def first_outputs(tr):
                    b = tr.b
                    c = Chain(ve, S, ph, "d_post", tr)
                    o = O[0]
                    ve.wait_ge(S["ob_evac"], ob_val(ph, tr, "o1"))
                    c.step(ve.scalar_tensor_tensor(LK[:, :, :], o[:, :, 96:160], 0.2, o[:, :, 96:160],
                                                   op0=ALU.mult, op1=ALU.max))
                    c.step(ve.tensor_tensor(LK[:, :, :], LK[:, :, :], bc(adot[:, :].unsqueeze(1), (EP, T, CS)), ALU.mult))
                    c.step(ve.tensor_reduce(al[:, :], LK[:, :, :].rearrange("p t (h s) -> p (t h) s", s=AS),
                                            AX.X, ALU.add))
                    for t in range(T):
                        prev = mx[b][:, H * (t - 1):H * t] if t else mx[1 - b][:, H * (T - 1):]
                        c.step(ve.scalar_tensor_tensor(mx[b][:, H * t:H * t + H], prev, kc[b][:, t, 1:2],
                                                       al[:, H * t:H * t + H], op0=ALU.add, op1=ALU.max))
                    ve.tensor_tensor(dd[:, 0, :], al[:, :], mx[b][:, :], ALU.subtract)
                    ve.tensor_tensor(dd[:, 1, 0:H], mx[1 - b][:, H * (T - 1):], mx[b][:, 0:H], ALU.subtract)
                    c.step(ve.tensor_tensor(dd[:, 1, H:], mx[b][:, 0:H * (T - 1)], mx[b][:, H:], ALU.subtract))
                    d1 = dd[:, 1, :].rearrange("p (t h) -> p t h", h=H)
                    ve.tensor_tensor(d1, d1, bc(kc[b][:, :, 1:2], (EP, T, H)), ALU.add).then_inc(S["d_ready"], 1)
                    times_u(o, 256, yc[b], c)
                    ve.wait_ge(S["tanh_done"], cnt(ph, "tanh_done", tr))
                    ve.tensor_scalar(MG2[:, :, 96:F], SG[:, :, 0:CS], 0.5, 0.5, ALU.mult, ALU.add)
                    c.step(ve.tensor_scalar(SG2[:, :, :], SG[:, :, CS:96], 0.5, 0.5, ALU.mult, ALU.add))
                    c.step(ve.tensor_tensor(MG2[:, :, 0:96].rearrange("p t (d c) -> p t d c", d=3),
                                            o[:, :, 0:96].rearrange("p t (d c) -> p t d c", d=3),
                                            bc(SG2[:, :, :].unsqueeze(2), (EP, T, 3, CV)), ALU.mult))
                    tp_inputs(MG2, yc[b], E2, c, "e2_done")
                    c.end()

                def attention(tr):
                    b = tr.b
                    c = Chain(ve, S, ph, "d_fin", tr)
                    ve.wait_ge(S["ob_evac"], ob_val(ph, tr, "O2"))
                    o4 = O2[:, :, :].rearrange("p (t h) f -> p t h f", h=H)
                    y = yc[b]
                    for d in range(3):
                        ins = ve.tensor_tensor(tmp[:, :, 32 * d:32 * d + 32].rearrange("p t (h f) -> p t h f", h=H),
                                               o4[:, :, :, 0:AV],
                                               bc(y[:, :, 1 + d:2 + d].unsqueeze(3), (EP, T, H, AV)), ALU.mult)
                    c.step(ins)
                    for d in range(3):
                        hv = o4[:, :, :, 24 + AV * d:24 + AV * d + AV]
                        ins = ve.tensor_tensor(hv, hv,
                                               tmp[:, :, 32 * d:32 * d + 32].rearrange("p t (h f) -> p t h f", h=H),
                                               ALU.add)
                    c.step(ins)
                    ve.wait_ge(S["exp_done"], cnt(ph, "exp_done", tr))
                    c.step(ve.tensor_tensor(MS[:, :, :], O2[:, :, 8:49],
                                            bc(pc[:, 0, :].unsqueeze(2), (EP, T * H, HC + 1)), ALU.mult))
                    out_free(tr)
                    mw = H * (HC + 1)
                    ve.tensor_copy(OUT[b][:, :, mw:mw + H], mx[b][:, :].rearrange("p (t h) -> p t h", h=H))
                    for t in range(T):
                        prev = OUT[b][:, t - 1, 0:mw] if t else OUT[1 - b][:, T - 1, 0:mw]
                        c.step(ve.tensor_tensor(OUT[b][:, t, 0:mw].rearrange("p (h f) -> p h f", h=H),
                                                prev.rearrange("p (h f) -> p h f", h=H),
                                                bc(pc[:, 1, H * t:H * t + H].unsqueeze(2), (EP, H, HC + 1)), ALU.mult))
                        ins = ve.tensor_tensor(OUT[b][:, t, 0:mw], OUT[b][:, t, 0:mw],
                                               MS[:, H * t:H * t + H, :].rearrange("p h f -> p (h f)"), ALU.add)
                        if t < T - 1:
                            c.step(ins)
                    ins.then_inc(S["msg_done"], 1)
                    ve.wait_ge(S["msg_done"], cnt(ph, "msg_done", tr))
                    c.end()

                if l == 0:
                    norm_stats(Trip(0, 0))
                    norm_rows(Trip(0, 0))

                    def edge_trip(tr):
                        inputs(tr)
                        if tr.has(1, ETRIPS):
                            norm_stats(tr.shift(1))
                        products(tr)
                        if tr.has(1, ETRIPS):
                            norm_rows(tr.shift(1))
                        if tr.has(-1, ETRIPS):
                            attention(tr.shift(-1))
                        first_outputs(tr)

                    trips(ve, ETRIPS, edge_trip)
                    attention(Trip(0, ETRIPS - 1))
                else:
                    inputs(Trip(0, 0))

                    def edge_trip(tr):
                        if tr.has(-1, ETRIPS):
                            messages(tr.shift(-1))
                        products(tr)
                        if tr.has(1, ETRIPS):
                            inputs(tr.shift(1))

                    trips(ve, ETRIPS, edge_trip)
                    messages(Trip(0, ETRIPS - 1))

                ve.wait_ge(fx_rd, 16 * (l + 1))
                mw = H * (HC + 1)
                if l == 0:
                    cn, mrow = cf[:, 2:3], FX[:, mw:mw + H]
                    fxx = Chain0(ve, w_dve, SETUP_STEPS)
                    fxx.step(ve.tensor_scalar(fm[:, 0, :], mrow, cn, None, ALU.mult))
                    fxx.step(ve.tensor_scalar(cf[:, 7:8], cn, -1.0, BIG, ALU.add, ALU.mult))
                    fxx.step(ve.tensor_scalar(fm[:, 0, :], fm[:, 0, :], cf[:, 7:8], None, ALU.add))
                    for h in range(H):
                        ins = ve.tensor_scalar(fdg[:, h * EP:(h + 1) * EP], ident[0:EP, 0:EP], fm[:, 0, h:h + 1],
                                               None, ALU.mult)
                    fstep(ins)
                    ve.wait_ge(fx_mm, 1)
                    f3 = fdg[:, :].rearrange("p (h q) -> p h q", h=H)
                    fxx.step(ve.tensor_tensor(f3, psF[0:EP, 0, 0:H * EP].rearrange("p (h q) -> p h q", h=H),
                                              bc(samen[:, :].unsqueeze(1), (EP, H, EP)), ALU.add))
                    fxx.step(ve.tensor_reduce(fm[:, 1, :], f3, AX.X, ALU.max))
                    ve.wait_ge(fx_g, 16)
                    fstep(ve.tensor_tensor(fm[:, 1, :], fm[:, 1, :], FB[:, mw:mw + H], ALU.max))
                    ve.tensor_tensor(fm[:, 2, :], fm[:, 0, :], fm[:, 1, :], ALU.subtract)
                    fstep(ve.tensor_tensor(fm[:, 3, :], FB[:, mw:mw + H], fm[:, 1, :], ALU.subtract))
                    ve.wait_ge(fx_act, 1)
                    for row, k in ((FX, 2), (FB, 3)):
                        r4 = row[:, 0:mw].rearrange("p (h f) -> p h f", h=H)
                        ins = ve.tensor_tensor(r4, r4, bc(fm[:, k, :].unsqueeze(2), (EP, H, HC + 1)), ALU.mult)
                    fstep(ins)
                    ve.wait_ge(fx_mm, 2)
                    ve.tensor_copy(FN[:, mw + H:AW], FB[:, mw + H:AW])
                    ve.tensor_copy(FN[:, mw:mw + H], fm[:, 1, :])
                    fstep(ve.tensor_tensor(FN[:, 0:mw], FB[:, 0:mw], psO[0:EP, 0, 0:mw], ALU.add))
                else:
                    ve.wait_ge(fx_g, 16 * (l + 1))
                    ve.wait_ge(fx_mm, l + 2)
                    fstep(ve.tensor_tensor(FN[:, :], FB[:, :], psO[0:EP, 0, 0:AW], ALU.add))
                assert fx[0] == FIX_STEPS[l], fx

                ph = f"N{l}"

                def spread(ap, w):
                    return bc(ap.rearrange("p (b t) -> p b t", b=2).unsqueeze(3), (NP, 2, 2, w))

                def ob(lo, w):
                    v = psO[:, :, 0:2 * NOW[l]].rearrange("p b (t f) -> p b t f", t=2)
                    return v[:, :, :, lo:lo + w]

                def by_bank(t, lo, w):
                    return t[:, :, lo:lo + w].rearrange("p (b t) f -> p b t f", b=2)

                def agn(tr):
                    b = tr.b
                    ve.wait_ge(S2["nld"][b], cnt2(ph, "nld", tr))
                    if tr.has(-1, NTRIPS):
                        ve.wait_ge(S["pe_ring"], cnt(ph, "pe_ring", tr.shift(-1), 2))
                    c = Chain(ve, S, ph, "d_norm", tr)
                    a4 = AG[b][:, :, 0:mw].rearrange("p t (h f) -> p t h f", h=H)
                    c.step(ve.tensor_scalar(rden[:, :].rearrange("p (t h) -> p t h", h=H), a4[:, :, :, HC], 1e-16,
                                            None, ALU.add))
                    c.step(ve.reciprocal(rden[:, :], rden[:, :]))
                    ve.tensor_tensor(AGN[:, :, :].rearrange("p t (h f) -> p t h f", h=H), a4[:, :, :, 0:HC],
                                     bc(rden[:, :].rearrange("p (t h) -> p t h", h=H).unsqueeze(3),
                                        (NP, T, H, HC)), ALU.mult).then_inc(S["agn_done"], 1)
                    c.end()

                if l == 0:
                    agn(Trip(0, 0))

                def node_trip(tr):
                    b = tr.b
                    ve.wait_ge(S2["nld"][b], cnt2(ph, "nld", tr))
                    if l == 0 and tr.has(1, NTRIPS):
                        agn(tr.shift(1))
                    c = Chain(ve, S, ph, "dve", tr)
                    r, x, ag = R[b], X[b], AG[b]
                    if l == 2:
                        c.step(ve.tensor_scalar(rden[:, 0:T], ag[:, :, F + 1], 1.0, None, ALU.max))
                        ve.reciprocal(co[b][:, T:], rden[:, 0:T]).then_inc(S["ang_done"], 1)
                    ve.wait_ge(S["ob_full"], cnt(ph, "ob_full", tr))
                    if l == 0:
                        ve.tensor_copy(by_bank(r, 0, F), ob(0, F)).then_inc(S["ob_used"], 1)
                        ve.wait_ge(S["ob_used"], cnt(ph, "ob_used", tr))
                        ve.scalar_tensor_tensor(r[:, :, 96:F], x[:, :, 0:CS], 2.0, r[:, :, 96:F],
                                                op0=ALU.mult, op1=ALU.add)
                        for j in range(T):
                            rv = r[:, j, 0:96].rearrange("p (d c) -> p d c", d=3)
                            xv = x[:, j, CS:F].rearrange("p (c d) -> p d c", d=3)
                            ins = ve.scalar_tensor_tensor(rv, xv, 2.0, rv, op0=ALU.mult, op1=ALU.add)
                        c.step(ins)
                    elif l in (1, 2):
                        if l == 1:
                            ve.wait_ge(S["coef_done"], cnt(ph, "coef_done", tr))
                            k = co[b][:, 0:T]
                        else:
                            k = x[:, :, ATTR]
                        ins = ve.tensor_tensor(by_bank(r, 0, F), ob(0, F), spread(k, F), ALU.mult)
                        ins.then_inc(S["ob_used"], 1)
                        ve.wait_ge(S["ob_used"], cnt(ph, "ob_used", tr))
                        c.step(ve.tensor_tensor(r[:, :, 0:F], r[:, :, 0:F], x[:, :, 0:F], ALU.add))
                        ve.wait_ge(S["t2_done"], cnt(ph, "t2_done", tr))
                        c.step(ve.tensor_tensor(r[:, :, 0:F], r[:, :, 0:F], T2B[b][:, :, :], ALU.add))
                    else:
                        ve.tensor_tensor(by_bank(R3, 0, 192), ob(0, 192), by_bank(ag, 0, 192), ALU.add)\
                          .then_inc(S["ob_used"], 1)
                        ve.wait_ge(S["ob_used"], cnt(ph, "ob_used", tr))
                        ve.tensor_tensor(R3[:, :, :], R3[:, :, :], bc(x[:, :, ATTR:ATTR + 1], (NP, T, 192)),
                                         ALU.mult).then_inc(S["gate_in"], 1)
                        ve.wait_ge(S["gate_in"], cnt(ph, "gate_in", tr))
                        ve.wait_ge(S["sig_done"], cnt(ph, "sig_done", tr))
                        ve.tensor_tensor(R3[:, :, 96:F], R3[:, :, 96:F], SGN[:, :, 0:CS], ALU.mult)
                        r4 = R3[:, :, 0:96].rearrange("p t (d c) -> p t d c", d=3)
                        c.step(ve.tensor_tensor(r4, r4, bc(SGN[:, :, CS:96].unsqueeze(2), (NP, T, 3, CV)), ALU.mult))
                        ve.tensor_tensor(r[:, :, 0:CS], R3[:, :, 96:F], x[:, :, 96:F], ALU.add)
                        c.step(ve.tensor_tensor(r[:, :, CS:F].rearrange("p t (c d) -> p t d c", d=3), r4,
                                                x[:, :, 0:96].rearrange("p t (d c) -> p t d c", d=3), ALU.add))
                    for j in range(T):
                        ins = ve.bn_stats(nbs[:, j, :], r[:, j, 0:F])
                    c.step(ins)
                    if tr.has(-2, NTRIPS):
                        ve.wait_ge(S["rstd_done"], cnt(ph, "rstd_done", tr.shift(-2)))
                    ve.sem_inc(ve_go, 1)
                    for j in range(T):
                        ins = ve.bn_aggr(nmv[b][:, j, :], nbs[:, j, :])
                    ins.then_inc(S["r_done"], 1)
                    c.end()

                trips(ve, NTRIPS, node_trip)


_INS = [
    "x", "src", "dst", "edge_attr_16", "edge_attr_4", "edge_attr_64", "edge_attr_8", "node_vec1",
    "L0_gnn_gamma_s", "L0_gnn_beta_s", "L0_gnn_gamma_v", "L0_gnn_Ws_src", "L0_gnn_Wv_src", "L0_gnn_Ws_dst",
    "L0_gnn_Wv_dst", "L0_gnn_W_rbf", "L0_gnn_W_alpha", "L0_gnn_alpha_dot", "L0_gnn_Ws_val", "L0_gnn_Wv_val",
    "L0_gnn_Wg", "L0_gnn_w2_ss", "L0_gnn_w2_sv", "L0_gnn_w2_vs", "L0_gnn_w2_vv0", "L0_gnn_w2_vv1",
    "L0_gnn_Ws_vlin", "L0_gnn_Wv_vlin", "L0_gnn_Wps", "L0_gnn_Wpv",
    "L1_gnn_W_sc_s", "L1_gnn_W_sc_v", "L1_gnn_W1_s", "L1_gnn_W1_v", "L1_gnn_W2_s", "L1_gnn_W2_v", "L1_gnn_W3",
    "L1_gnn_fcW1", "L1_gnn_fcW2",
    "L2_gnn_Wfc1", "L2_gnn_Wfc2", "L2_gnn_Wsc0", "L2_gnn_Wsc1", "L2_gnn_Wl1_0", "L2_gnn_Wl1_1", "L2_gnn_Wl2_s",
    "L2_gnn_Wl2_v", "L2_gnn_Wa",
    "L3_gnn_lin1_ws", "L3_gnn_lin1_wv", "L3_gnn_fc_w1", "L3_gnn_fc_w2", "L3_gnn_sc_ws", "L3_gnn_sc_wv",
    "L3_gnn_lin2_ws", "L3_gnn_lin2_wv",
]


def kernel(**inputs):
    import numpy as _np
    import concourse.bacc as _bacc
    from concourse import mybir as _mybir
    from concourse.bass_utils import run_bass_kernel_spmd as _run

    nc = _bacc.Bacc("TRN2", target_bir_lowering=False, num_devices=1)
    arrays, args = {}, {}
    for name in _INS:
        a = _np.ascontiguousarray(inputs[name])
        arrays[f"in_{name}"] = a
        args[name] = nc.dram_tensor(f"in_{name}", a.shape, _mybir.dt.from_np(a.dtype), kind="ExternalInput").ap()
    out = nc.dram_tensor("out_0", (N, F), _mybir.dt.float32, kind="ExternalOutput").ap()
    gnn_kernel(nc, args, out)
    r = _run(nc, [arrays], core_ids=[0])
    return r.results[0]["out_0"]
```

```python
from contextlib import ExitStack

import concourse.bass as bass
from concourse import mybir

N = 50000
E = 25000
CS, CV = 64, 32
F = CS + 3 * CV
H = 4
AS, AV = CS // H, CV // H
HC = AS + 3 * AV

EP = 125
ET = E // EP
T = 4
EC = T * EP
ETRIPS = ET // T
NP = 128
NG = T * NP
NTRIPS = -(-N // NG)
NFULL = N // NG
XW = F + 1
AW = 192
AROWS = 392 * 128
SKIP = 65536
BIG = 1.0e30
ATTR = F
OW = 288

C_VY, C_YV, C_YS, C_S, C_X = 0, 32, 128, 192, 256
EW = 352

LAYERS = [
    dict(rad=16, cross=True, msg=H * (HC + 1) + H),
    dict(rad=8, cross=False, msg=F + 1),
    dict(rad=16, cross=False, msg=F + 2),
    dict(rad=64, cross=True, msg=2 * 96),
]


PI, HALF_PI, INV_2PI = 3.1415925, 1.5707963267948966, 0.15915494309189535
TWO_PI = (6.28125, 1.9350051879882812e-03, 3.0199159819567000e-07)
MAGIC = 12582912.0


class Trip:

    def __init__(self, i, off, turn=2):
        self.i, self.off, self.turn, self.b, self.q = i, off, turn, off % 2, off % 4
        self.g = off if isinstance(i, int) else None

    def shift(self, d):
        return Trip(self.i, self.off + d, self.turn)

    def every(self, m, per, c):
        c = (self.off // m) * per + c
        return c if self.g is not None else self.i * (self.turn // m * per) + c

    def lin(self, per, c):
        return self.every(1, per, c)

    def half(self, per, c):
        return self.every(2, per, c)

    def has(self, d, n):
        return self.g is None or 0 <= self.g + d < n


def trips(eng, n, body, turn=2):
    last = (n - 2) // turn
    for g in range(turn):
        body(Trip(0, g, turn))
    with eng.Fori(1, last) as i:
        for off in range(turn):
            body(Trip(i, off, turn))
    for g in range(last * turn, n):
        body(Trip(0, g, turn))


PHASES = ["E0", "N0", "E1", "N1", "E2", "N2", "E3", "N3"]
RING_E = {0: 10, 1: 6, 2: 6, 3: 8}
CHUNKS = {0: 3, 1: 2, 2: 2, 3: 3}

PER = {}
for _l in range(4):
    PER[f"E{_l}"] = dict(pe_ring=RING_E[_l], act_ring=RING_E[_l], ob_full=4 if _l == 0 else 1,
                         ob_evac=4 if _l == 0 else 1, f_done=CHUNKS[_l], prod_done=CHUNKS[_l], e_done=1,
                         msg_done=1, xn_done=1, e2_done=1, d_ready=1, exp_done=1, tanh_done=1, sq_done=1,
                         stat_done=1, pow_done=1, gp=0, d_norm=0, d_in=0, d_post=0, d_fin=0)
    PER[f"N{_l}"] = dict(pe_ring=2, act_ring=2, ob_full=1, ob_used=1, r_done=1, rstd_done=1, y_done=1, a_done=1,
                         agn_done=int(_l == 0), ang_done=int(_l in (1, 2)), sin_done=int(_l == 1),
                         coef_done=int(_l == 1), t2_done=int(_l in (1, 2)), gate_in=int(_l == 3),
                         sig_done=int(_l == 3), gpn=3)
for _ph, _n in dict(E0=dict(gp=1, d_norm=1, d_in=2, d_post=13, d_fin=10), E1=dict(d_in=2, d_post=5),
                    E2=dict(d_in=2, d_post=5), E3=dict(d_in=2, d_post=5),
                    N0=dict(d_norm=2, dve=1, gp=0), N1=dict(dve=3, gp=11, d_norm=0), N2=dict(dve=3, gp=3, d_norm=1), N3=dict(dve=3, gp=0, d_norm=0)).items():
    PER[_ph].update(_n)
PER2 = {}
for _l in range(4):
    PER2[f"E{_l}"] = dict(gath=16 * T * (2 if _l == 0 else 1), idx=16 * (2 if _l == 0 else 1), lda=48, scid=16,
                          scat=16 * T)
    PER2[f"N{_l}"] = dict(nst=16)
NBUF = 4
PERX = {l: 32 if l == 0 else 16 for l in range(4)}


def node_loads(l, tr, per):
    before = sum(per[k] for k in range(l)) * len(range(tr.q, NTRIPS, NBUF))
    return tr.every(NBUF, per[l], before + per[l])


PERA = {l: 16 for l in range(4)}


def bases(per, ntrips):
    out, at = {}, {}
    for ph in PHASES:
        out[ph] = dict(at)
        for k, v in per[ph].items():
            at[k] = at.get(k, 0) + v * ntrips(ph)
    return out


BASE = bases(PER, lambda ph: ETRIPS if ph[0] == "E" else NTRIPS)
BASE2 = bases(PER2, lambda ph: (ETRIPS if ph[0] == "E" else NTRIPS) // 2)


def cnt(ph, sem, tr, k=1):
    return tr.lin(PER[ph][sem], BASE[ph].get(sem, 0) + k)


def cnt2(ph, sem, tr):
    per = PER2[ph][sem]
    return tr.half(per, BASE2[ph].get(sem, 0) + per)


def total(ph, sem):
    return BASE[ph].get(sem, 0) + PER[ph][sem] * (ETRIPS if ph[0] == "E" else NTRIPS)


def total2(ph, sem):
    return BASE2[ph].get(sem, 0) + PER2[ph][sem] * ((ETRIPS if ph[0] == "E" else NTRIPS) // 2)


class Chain:

    def __init__(self, eng, sems, ph, name, tr, held=None):
        self.eng, self.sem, self.ph, self.name, self.tr, self.n = eng, sems[name], ph, name, tr, 0
        self.held = held

    def step(self, ins):
        self.n += 1
        ins.then_inc(self.sem, 1)
        self.eng.wait_ge(self.sem, cnt(self.ph, self.name, self.tr, self.n))
        if self.held is not None:
            self.eng.sem_inc(self.held, 1)

    def end(self):
        assert self.n == PER[self.ph][self.name], (self.ph, self.name, self.n)


class Chain0:

    def __init__(self, eng, sem, at):
        self.eng, self.sem, self.at = eng, sem, at

    def step(self, ins):
        self.at += 1
        ins.then_inc(self.sem, 1)
        self.eng.wait_ge(self.sem, self.at)


def ring_banks(l):
    return 3 if RING_E[l] % 3 == 0 else 2


def ring_step(l, tr, what):
    if l:
        return 0, {"e": 0, "h": 1, "w": 2, "t": 2 + CHUNKS[l]}[what[0]] + int(what[1:] or 0)
    k = int(what[1:] or 0)
    if what[0] == "n":
        return (None, k) if tr.g == 0 else (-1, 7 + k)
    if what[0] == "t":
        return 0, (7 if tr.g == ETRIPS - 1 else 10) + k
    return 0, (3 if what[0] == "e" else 4) + k


def ring_val(ph, l, tr, what):
    d, k = ring_step(l, tr, what)
    if d is None:
        return BASE[ph].get("pe_ring", 0) + k + 1
    return cnt(ph, "pe_ring", tr.shift(d), k + 1)


def ring_pos(l, tr, what):
    d, k = ring_step(l, tr, what)
    return k if d is None else (tr.off + d) % 2 * RING_E[l] + k


def ob_val(ph, tr, what):
    if what == "M":
        return 1 if tr.g == 0 else cnt(ph, "ob_full", tr.shift(-1), 4)
    if what == "O2":
        return cnt(ph, "ob_full", tr, 4 if tr.g == ETRIPS - 1 else 5)
    return cnt(ph, "ob_full", tr, 2 + int(what[1]))


FIX_STEPS = [5, 6, 7, 8]
GRAPH_STEPS = 34
SETUP_STEPS = 76


def wait(eng, sem, value):
    if isinstance(value, int) and value <= 0:
        return
    eng.wait_ge(sem, value)


def gnn_kernel(nc, A, out):
    f32, i32 = mybir.dt.float32, mybir.dt.int32
    ALU, ACT, AX = mybir.AluOpType, mybir.ActivationFunctionType, mybir.AxisListType

    ctx = ExitStack()
    with ctx:
        def sb(name, shape, dt=f32):
            return ctx.enter_context(nc.sbuf_tensor(name, shape, dt))

        def pair(name, shape, dt=f32):
            return [sb(f"{name}{b}", shape, dt) for b in range(2)]

        def sem(name):
            return ctx.enter_context(nc.semaphore(name))

        tabA = nc.dram_tensor("tab_a", (N, XW), f32).ap()
        tabB = nc.dram_tensor("tab_b", (N, XW), f32).ap()
        agg = nc.dram_tensor("agg", (AROWS, AW), f32).ap()
        runs_d = nc.dram_tensor("runs", (EP, ET, 3), f32).ap()
        scix_d = nc.dram_tensor("scatter_ids", (EP, ET), i32).ap()
        TABLE = [A["x"], tabA, tabB, tabA]
        NEXT = [tabA, tabB, tabA, out]
        ES = [A["edge_attr_16"], A["edge_attr_8"], A["edge_attr_16"], A["edge_attr_64"]]

        ident = sb("ident", [128, 128])
        ones_k = sb("ones_k", [EP, EP])
        zeros = sb("zeros", [128, 3136])
        dst_i = sb("dst_i", [EP, ET], i32)
        dst_f = sb("dst_f", [EP, ET])
        runs = sb("runs_sb", [EP, ET, 3])
        wk_one = sb("wk_one", [EP, ET])
        wk1 = sb("wk1", [EP, ET])
        wk2 = sb("wk2", [EP, ET])
        scix = sb("scix", [EP, ET], i32)
        edge_i = sb("edge_i", [EP, 3], i32)
        edge_f = sb("edge_f", [EP, 3])
        pid = sb("pid", [EP, 1], i32)
        cf = sb("cf", [EP, 8])
        head_i = sb("head_i", [EP, 1], i32)
        fixid = sb("fixid", [EP, 1], i32)
        hrow_i = sb("hrow_i", [EP, EP], i32)
        hrow = sb("hrow", [EP, EP])
        same = sb("same", [EP, EP])
        samen = sb("samen", [EP, EP])

        fc1 = {l: sb(f"fc1_{l}", [LAYERS[l]["rad"], CS]) for l in (1, 2, 3)}
        fc2 = {l: sb(f"fc2_{l}", [16 if l == 0 else CS, EW]) for l in range(4)}
        wf1 = {l: sb(f"wf1_{l}", [128, 128]) for l in (1, 2, 3)}
        wf2 = {l: sb(f"wf2_{l}", [128, 128]) for l in (1, 2, 3)}
        EOW = {0: 288, 1: 193, 2: 193, 3: 224}
        ra = {l: sb(f"ra_{l}", [128, EOW[l] - 96]) for l in range(4)}
        rb = {l: sb(f"rb_{l}", [128, EOW[l]]) for l in range(4)}
        rx = {l: sb(f"rx_{l}", [96, 96]) for l in (0, 3)}
        NOW = {0: 160, 1: 160, 2: 160, 3: 192}
        nw1 = {l: sb(f"nw1_{l}", [96, 96]) for l in range(4)}
        nw2 = {l: sb(f"nw2_{l}", [CS, NOW[l] - 96]) for l in range(4)}
        wm_s = sb("wm_s", [128, F])
        wm_d = sb("wm_d", [128, F])
        wm_t = sb("wm_t", [64, F])
        g1 = sb("g1", [128, 1])
        g3 = sb("g3", [64, 1])
        beta = sb("beta", [CS, 1])
        wsrc = sb("wsrc", [CS, CS])
        wdst = sb("wdst", [CS, CS])
        brow = sb("brow", [1, F])
        onerow = sb("onerow", [1, EP])
        wval = sb("wval", [96, CS])
        wg = sb("wg", [CS, CV])
        wvt = sb("wvt", [CS, 96 + 128])
        adot = sb("adot", [EP, CS])
        r2a = sb("r2a", [128, H * 48])
        r2b = sb("r2b", [128, H * 48])
        r2x = sb("r2x", [96, H * 48])
        cA = sb("cA", [128, 1])
        cB = sb("cB", [128, 1])
        cX = sb("cX", [96, 1])

        gidx = pair("gidx", [EP, T], i32)
        gidx2 = pair("gidx2", [EP, T], i32)
        scid = pair("scid", [EP, T], i32)
        es_in = pair("es_in", [EP, T * 64])
        y_in = pair("y_in", [EP, T, 4])
        k_in = pair("k_in", [EP, T, 3])
        yc = pair("yc", [EP, T, 6])
        kc = pair("kc", [EP, T, 3])
        G = pair("G", [EP, T, XW])
        GS = pair("GS", [EP, T, F])
        GD = pair("GD", [EP, T, F])
        XN = sb("XN", [EP, T, 2, F])
        sqv = sb("sqv", [EP, 2 * T, 96])
        bst = sb("bst", [EP, 2 * T, 6])
        lst = sb("lst", [EP, 2 * T, 3])
        lrs = sb("lrs", [EP, 2 * T, 2])
        mhalf = sb("mhalf", [128, 24])
        epsb = sb("epsb", [128, 1])
        MG = sb("MG", [EP, T, F])
        EE = sb("EE", [EP, T, EW])
        E2 = sb("E2", [EP, T, EW])
        tmp = sb("tmp", [EP, T, 96])
        tmp2 = sb("tmp2", [EP, T, 96])
        tmp3 = sb("tmp3", [EP, T, 96])
        esT = sb("esT", [64, EC])
        hidT = sb("hidT", [64, EC])
        wT = [sb(f"wT{c}", [128, EC]) for c in range(3)]
        ET_ = [sb(f"ET{c}", [128, EC]) for c in range(3)]
        PR = [sb(f"PR{c}", [128, EC]) for c in range(3)]
        O = pair("O", [EP, T, OW])
        MG2 = sb("MG2", [EP, T, F])
        O2 = sb("O2", [EP, T * H, 49])
        SG2 = sb("SG2", [EP, T, CV])
        XT = sb("XT", [EP, T, 64])
        SG = sb("SG", [EP, T, 96])
        LK = sb("LK", [EP, T, CS])
        al = sb("al", [EP, T * H])
        mx = pair("mx", [EP, T * H])
        dd = sb("dd", [EP, 2, T * H])
        pc = sb("pc", [EP, 2, T * H])
        MS = sb("MS", [EP, T * H, HC + 1])
        OUT = pair("OUT", [EP, T, AW])
        FX = sb("FX", [EP, AW])
        FB = sb("FB", [EP, AW])
        FN = sb("FN", [EP, AW])
        fm = sb("fm", [EP, 4, H])
        fdg = sb("fdg", [EP, H * EP])

        X = [sb(f"X{q}", [NP, T, XW]) for q in range(NBUF)]
        AG = [sb(f"AG{q}", [NP, T, AW]) for q in range(NBUF)]
        XA = [sb(f"XA{q}", [NP, T]) for q in range(NBUF)]
        AGN = pair("AGN", [NP, T, F])
        rden = pair("rden", [NP, T * H])
        NT1 = pair("NT1", [96, NG])
        NT2 = pair("NT2", [CS, NG])
        R = pair("R", [NP, T, F])
        T2B = pair("T2B", [NP, T, F])
        R3 = pair("R3", [NP, T, 192])
        SGN = pair("SGN", [NP, T, 96])
        nbs = sb("nbs", [NP, T, 6])
        nmv = pair("nmv", [NP, T, 2])
        nrs = pair("nrs", [NP, T, 2])
        ang = sb("ang", [NP, 2 * T])
        angk = sb("angk", [NP, 2 * T])
        angr = sb("angr", [NP, 2 * T])
        sc8 = sb("sc8", [NP, 2 * T])
        co = pair("co", [NP, 2 * T])
        Y = pair("Y", [NP, T, XW])

        ps = ctx.enter_context(nc.psum_tensor("ps", [128, 8, 512], f32))
        psR, psF, psO = ps[:, 0:3, :], ps[:, 3:6, :], ps[:, 6:8, :]
        NPO = [ps[:, 6:8, :], ps[:, 4:6, :]]

        S = {n: sem(n) for n in (
            "pe_ring", "act_ring", "ob_full", "ob_evac", "ob_used", "f_done", "prod_done", "e_done", "msg_done",
            "xn_done", "e2_done", "d_ready", "exp_done", "tanh_done", "sq_done", "stat_done", "pow_done",
            "r_done", "rstd_done", "y_done", "agn_done", "ang_done", "sin_done", "t2_done", "coef_done",
            "gate_in", "sig_done", "a_done", "dve", "gp", "gpn", "d_norm", "d_in", "d_post",
            "d_fin")}
        S2 = {n: [sem(f"{n}0"), sem(f"{n}1")] for n in ("gath", "idx", "lda", "scid", "scat", "nst")}
        S4 = {n: [sem(f"{n}{q}") for q in range(NBUF)] for n in ("nldx", "nlda")}
        w_zero = sem("w_zero")
        w_load = sem("w_load")
        w_dve = sem("w_dve")
        w_pe = sem("w_pe")
        w_act = sem("w_act")
        g_load = sem("g_load")
        g_store = sem("g_store")
        z_store = sem("z_store")
        go = sem("go")
        sp_go = sem("sp_go")
        pe_go = sem("pe_go")
        ve_go = sem("ve_go")
        ac_go = sem("ac_go")
        fx_rd = sem("fx_rd")
        fx_g = sem("fx_g")
        fx_mm = sem("fx_mm")
        fx_dve = sem("fx_dve")
        fx_act = sem("fx_act")
        fx_st = sem("fx_st")

        loads = []

        def put(tile, r, c, src):
            loads.append((tile[r:r + src.shape[0], c:c + src.shape[1]], src))

        def col(tile, r, src):
            loads.append((tile[r:r + src.shape[0], 0:1], src.rearrange("(a b) -> a b", b=1)))

        L0 = {k[7:]: v for k, v in A.items() if k.startswith("L0_gnn_")}
        L1 = {k[7:]: v for k, v in A.items() if k.startswith("L1_gnn_")}
        L2 = {k[7:]: v for k, v in A.items() if k.startswith("L2_gnn_")}
        L3 = {k[7:]: v for k, v in A.items() if k.startswith("L3_gnn_")}
        for l, w in ((0, L0["W_rbf"]), (1, L1["fcW2"]), (2, L2["Wfc2"]), (3, L3["fc_w2"])):
            put(fc2[l], 0, 0, w[:, 160:192])
            for d in range(3):
                put(fc2[l], 0, 32 + 32 * d, w[:, 128:160])
                if LAYERS[l]["cross"]:
                    put(fc2[l], 0, 256 + 32 * d, w[:, 192:224])
            put(fc2[l], 0, 128, w[:, 0:128])
        for l, w in ((1, L1["fcW1"]), (2, L2["Wfc1"]), (3, L3["fc_w1"])):
            put(fc1[l], 0, 0, w)
        for l, ws, wv in ((1, L1["W1_s"], L1["W1_v"]), (2, L2["Wl1_0"], L2["Wl1_1"]),
                          (3, L3["lin1_ws"], L3["lin1_wv"])):
            for d in range(2):
                put(wf1[l], 64 * d, 64 * d, ws)
            for d in range(4):
                put(wf2[l], 32 * d, 32 * d, wv)
        for l, ws, wv, w1 in ((1, L1["W2_s"], L1["W2_v"], L1["W3"]), (2, L2["Wl2_s"], L2["Wl2_v"], L2["Wa"]),
                              (3, L3["lin2_ws"], L3["lin2_wv"], None), (0, L0["W_alpha"], L0["Wv_val"], None)):
            put(ra[l], 0, 0, ws[0:64])
            put(rb[l], 0, 96, ws[64:96])
            if w1 is not None:
                put(ra[l], 0, 64, w1[0:64])
                put(rb[l], 0, 160, w1[64:96])
            put(ra[l], 64, EOW[l] - 128, wv[0:64])
            for d in range(3):
                put(rb[l], 32 + 32 * d, 32 * d, wv[64:96])
                if l in rx:
                    put(rx[l], 32 * d, 32 * d, wv[96:128])
        put(ra[0], 0, 64, L0["Ws_val"][0:64])
        put(rb[0], 0, 160, L0["Ws_val"][64:96])
        put(wval, 0, 0, L0["Ws_val"])
        put(wg, 0, 0, L0["Wg"])
        for tile, ws, wv in ((wm_s, L0["Ws_src"], L0["Wv_src"]), (wm_d, L0["Ws_dst"], L0["Wv_dst"])):
            for d in range(3):
                put(tile, 32 * d, 32 * d, wv)
            put(tile, 96, 96, ws[0:32])
        put(wm_t, 0, 96, L0["Ws_src"][32:64])
        put(wm_t, 32, 96, L0["Ws_dst"][32:64])
        put(wsrc, 0, 0, L0["Ws_src"])
        put(wdst, 0, 0, L0["Ws_dst"])
        for d in range(3):
            col(g1, 32 * d, L0["gamma_v"])
        col(g1, 96, L0["gamma_s"][0:32])
        for d in range(2):
            col(g3, 32 * d, L0["gamma_s"][32:64])
        col(beta, 0, L0["beta_s"])
        loads.append((adot[:, :], L0["alpha_dot"].rearrange("a h s -> a (h s)").broadcast_to((EP, CS))))
        for h in range(H):
            put(r2a, 0, 48 * h + 8, L0["Ws_vlin"][0:64, AS * h:AS * h + AS])
            put(r2b, 0, 48 * h + 8, L0["Ws_vlin"][64:96, AS * h:AS * h + AS])
            put(r2a, 64, 48 * h, L0["Wv_vlin"][0:64, AV * h:AV * h + AV])
            for d in range(3):
                put(r2b, 32 + 32 * d, 48 * h + 24 + 8 * d, L0["Wv_vlin"][64:96, AV * h:AV * h + AV])
                put(r2x, 32 * d, 48 * h + 24 + 8 * d, L0["Wv_vlin"][96:128, AV * h:AV * h + AV])
        col(cA, 0, L0["w2_ss"])
        col(cA, 64, L0["w2_sv"])
        col(cB, 0, L0["w2_vv0"])
        for d in range(3):
            col(cB, 32 + 32 * d, L0["w2_vs"])
            col(cX, 32 * d, L0["w2_vv1"])
        for l, ws, wv in ((0, L0["Wps"], L0["Wpv"]), (1, L1["W_sc_s"], L1["W_sc_v"]), (2, L2["Wsc0"], L2["Wsc1"]),
                          (3, L3["sc_ws"], L3["sc_wv"])):
            for d in range(3):
                put(nw1[l], 32 * d, 32 * d, wv)
            put(nw2[l], 0, 0, ws)

        cleared = ([fc2[l] for l in range(4)] + [wf1[l] for l in (1, 2, 3)] + [wf2[l] for l in (1, 2, 3)]
                   + [t[l] for t in (ra, rb, nw1) for l in range(4)] + [rx[0], rx[3]]
                   + [wm_s, wm_d, wm_t, r2a, r2b, r2x, brow, wvt])

        r3, r2 = 3.0 ** -0.5, 2.0 ** -0.5
        s64, s32, s96, s128 = 64 ** -0.5, 32 ** -0.5, 96 ** -0.5, 128 ** -0.5
        c1, c2, c3 = 10 ** -0.5 * s96, s96, 0.25 * s96
        scales = [(fc1[1][:, :], 8 ** -0.5), (fc1[2][:, :], 0.25), (fc1[3][:, :], 0.125)]
        for l in (1, 2, 3):
            scales += [(fc2[l][:, 0:(352 if l == 3 else 256)], s64), (wf1[l][:, :], s64), (wf2[l][:, :], s32)]
        scales += [(ra[1][:, 0:64], c1), (ra[1][:, 64:65], 0.1 * c1), (ra[1][:, 65:97], c1),
                   (rb[1][0:32, 96:160], c1 * r3), (rb[1][0:32, 160:161], 0.1 * c1 * r3), (rb[1][:, 0:96], c1),
                   (ra[2][:, :], c2), (rb[2][0:32, 96:161], c2 * r3), (rb[2][:, 0:96], c2),
                   (ra[3][:, 0:96], c3), (ra[3][:, 96:128], 0.25 * s128),
                   (rb[3][0:32, 96:192], c3 * r3), (rb[3][:, 0:96], 0.25 * s128), (rx[3][:, :], 0.25 * s128 * r2),
                   (rx[0][:, :], r2)]
        for l in (1, 2, 3):
            scales += [(nw1[l][:, :], s32), (nw2[l][:, :], s64)]

        N_CLEAR = len(cleared)
        N_LOAD = 16 * len(loads)

        def tab_rows(tab, tr, width):
            if tr.g is not None and tr.g == NTRIPS - 1:
                return tab[N - NG:N, :].rearrange("(p j) f -> p j f", j=T)[:, :, 0:width]
            v = tab[0:NFULL * NG, :].rearrange("(g p j) f -> g p j f", p=NP, j=T)
            return v[tr.lin(1, 0)][:, :, 0:width]

        block = ctx.enter_context(nc.Block())

        @block.sync
        def _(sp):
            sp.dma_start(dst_i[:, :], A["dst"].rearrange("(p t) -> p t", t=ET)).then_inc(g_load, 16)
            sp.dma_start(hrow_i[:, :], A["dst"].rearrange("(a p t) -> t a p", a=1, t=ET)[0]
                         .broadcast_to((EP, EP)), allow_slow_non_contiguous=True).then_inc(g_load, 16)
            dcol = A["dst"].rearrange("(p t) -> p t", t=ET)
            sp.wait_ge(w_zero, 1)
            sp.dma_start(edge_i[1:EP, 0:1], dcol[0:EP - 1, 0:1],
                         allow_slow_non_contiguous=True).then_inc(g_load, 16)
            sp.dma_start(edge_i[1:EP, 1:2], dcol[0:EP - 1, ET - 1:ET],
                         allow_slow_non_contiguous=True).then_inc(g_load, 16)
            sp.dma_start(edge_i[2:EP, 2:3], dcol[0:EP - 2, ET - 1:ET],
                         allow_slow_non_contiguous=True).then_inc(g_load, 16)
            sp.wait_ge(w_zero, 1 + N_CLEAR)
            for dst, src in loads:
                sp.dma_start(dst, src, allow_slow_non_contiguous=True).then_inc(w_load, 16)
            sp.wait_ge(w_dve, GRAPH_STEPS)
            sp.dma_start(runs_d[:, :, :], runs[:, :, :]).then_inc(g_store, 16)
            sp.dma_start(scix_d[:, :], scix[:, :]).then_inc(g_store, 16)
            sp.wait_ge(g_store, 32)

            for l in range(4):
                ph, rad = f"E{l}", LAYERS[l]["rad"]
                es_v = ES[l].rearrange("(p g t) k -> g p (t k)", p=EP, t=T)
                y_v = A["edge_attr_4"].rearrange("(p g t) k -> g p t k", p=EP, t=T)
                k_v = runs_d.rearrange("p (g t) k -> g p t k", t=T)
                s_v = A["src"].rearrange("(p g t) -> g p t", p=EP, t=T)
                d_v = A["dst"].rearrange("(p g t) -> g p t", p=EP, t=T)
                sc_v = scix_d.rearrange("p (g t) -> g p t", t=T)

                def load_idx(tr):
                    sp.dma_start(gidx[tr.b][:, :], s_v[tr.lin(1, 0)]).then_inc(S2["idx"][tr.b], 16)
                    if l == 0:
                        sp.dma_start(gidx2[tr.b][:, :], d_v[tr.lin(1, 0)]).then_inc(S2["idx"][tr.b], 16)

                def load_attrs(tr):
                    sp.dma_start(es_in[tr.b][:, 0:T * rad], es_v[tr.lin(1, 0)]).then_inc(S2["lda"][tr.b], 16)
                    sp.dma_start(y_in[tr.b][:, :, :], y_v[tr.lin(1, 0)]).then_inc(S2["lda"][tr.b], 16)
                    sp.dma_start(k_in[tr.b][:, :, :], k_v[tr.lin(1, 0)]).then_inc(S2["lda"][tr.b], 16)

                for g in range(2):
                    load_idx(Trip(0, g))
                    load_attrs(Trip(0, g))

                def edge_trip(tr):
                    if tr.has(2, ETRIPS):
                        wait(sp, S2["gath"][tr.b], cnt2(ph, "gath", tr))
                        sp.sem_inc(sp_go, 1)
                        load_idx(tr.shift(2))
                        wait(sp, S["e_done"], cnt(ph, "e_done", tr))
                        sp.sem_inc(sp_go, 1)
                        wait(sp, S["pe_ring"], cnt(ph, "pe_ring", tr, (3 if l == 0 else 0) + 1))
                        sp.sem_inc(sp_go, 1)
                        load_attrs(tr.shift(2))
                    if tr.has(-2, ETRIPS):
                        wait(sp, S2["scat"][tr.b], cnt2(ph, "scat", tr.shift(-2)))
                        sp.sem_inc(sp_go, 1)
                    sp.dma_start(scid[tr.b][:, :], sc_v[tr.lin(1, 0)]).then_inc(S2["scid"][tr.b], 16)

                trips(sp, ETRIPS, edge_trip)

                for b in range(2):
                    sp.wait_ge(S2["scat"][b], total2(ph, "scat"))
                sp.dma_start(FX[:, :], agg[N:N + EP, :]).then_inc(fx_rd, 16)
                sp.wait_ge(fx_st, 16 * (l + 1))

                ph = f"N{l}"
                aw = H * (HC + 1) if l == 0 else LAYERS[l]["msg"]
                xw = F if l == 0 else XW

                def node_trip(tr):
                    q = tr.q
                    if tr.has(-NBUF, NTRIPS):
                        wait(sp, S["r_done"], cnt(ph, "r_done", tr.shift(-NBUF)))
                        wait(sp, S["a_done"], cnt(ph, "a_done", tr.shift(-NBUF)))
                        sp.sem_inc(sp_go, 1)
                    sp.dma_start(AG[q][:, :, 0:aw], tab_rows(agg[0:N, :], tr, aw)).then_inc(S4["nlda"][q], 16)
                    sp.dma_start(X[q][:, :, 0:xw], tab_rows(TABLE[l], tr, xw)).then_inc(S4["nldx"][q], 16)
                    if l == 0:
                        sp.dma_start(XA[q][:, :], tab_rows(A["node_vec1"], tr, 1)
                                     .rearrange("p j f -> p (j f)")).then_inc(S4["nldx"][q], 16)

                trips(sp, NTRIPS, node_trip, NBUF)

            for b in range(2):
                sp.wait_ge(S2["nst"][b], total2("N3", "nst"))

        @block.gpsimd
        def _(gp):
            gp.memset(edge_i[:, :], -1).then_inc(w_zero, 1)
            for t in cleared:
                gp.memset(t[:, :], 0.0).then_inc(w_zero, 1)
            gp.memset(zeros[:, :], 0.0).then_inc(w_zero, 1)
            gp.memset(ident[:, :], 0.0).then_inc(w_zero, 1)
            gp.memset(ones_k[:, :], 1.0).then_inc(w_zero, 1)
            gp.memset(onerow[:, :], 1.0).then_inc(w_zero, 1)
            gp.memset(mhalf[:, :], -0.5).then_inc(w_zero, 1)
            gp.iota(pid[:, :], [[0, 1]], base=N, channel_multiplier=1).then_inc(w_zero, 1)
            gp.memset(O2[:, :, 48], 1.0).then_inc(w_zero, 1)
            gp.memset(wk_one[:, :], 1.0).then_inc(w_zero, 1)
            for b in range(2):
                gp.memset(OUT[b][:, :, :], 0.0).then_inc(w_zero, 1)
                gp.memset(mx[b][:, :], 0.0).then_inc(w_zero, 1)
            gp.wait_ge(w_zero, N_CLEAR + 13)
            gp.affine_select(out=ident[:, :], in_=ident[:, :], compare_op=ALU.not_equal, fill=1.0, base=0,
                             pattern=[[-1, 128]], channel_multiplier=1).then_inc(w_zero, 1)
            for l in range(4):
                ph = f"E{l}"
                if l:
                    for b in range(2):
                        gp.wait_ge(S2["nst"][b], total2(f"N{l - 1}", "nst"))

                def rows(dst, j, ids):
                    return gp.indirect_dma_start(dst[:, j, :], None, TABLE[l][:, :],
                                                 bass.IndirectOffsetOnAxis(ap=ids[:, j:j + 1], axis=0))

                def gathers(tr):
                    b = tr.b
                    wait(gp, S2["idx"][b], cnt2(ph, "idx", tr))
                    gp.sem_inc(go, 1)
                    if tr.has(-2, ETRIPS):
                        s = "xn_done" if l == 0 else "e_done"
                        wait(gp, S[s], cnt(ph, s, tr.shift(-2)))
                        gp.sem_inc(go, 1)
                    for j in range(T):
                        if l == 0:
                            rows(GS[b], j, gidx[b]).then_inc(S2["gath"][b], 16)
                            rows(GD[b], j, gidx2[b]).then_inc(S2["gath"][b], 16)
                        else:
                            rows(G[b], j, gidx[b]).then_inc(S2["gath"][b], 16)

                def scatters(tr):
                    b = tr.b
                    wait(gp, S2["scid"][b], cnt2(ph, "scid", tr))
                    gp.sem_inc(go, 1)
                    wait(gp, S["msg_done"], cnt(ph, "msg_done", tr))
                    gp.sem_inc(go, 1)
                    if tr.g == 0 and l == 0:
                        gp.wait_ge(z_store, 16 * 24)
                        gp.sem_inc(go, 1)
                    for j in range(T):
                        gp.indirect_dma_start(agg[:, :], bass.IndirectOffsetOnAxis(ap=scid[b][:, j:j + 1], axis=0),
                                              OUT[b][:, j, :], None, bounds_check=AROWS - 1, oob_is_err=False)\
                          .then_inc(S2["scat"][b], 16)

                def inv_norms(tr):
                    gp.wait_ge(S["stat_done"], cnt(ph, "stat_done", tr))
                    gp.sem_inc(go, 1)
                    c = Chain(gp, S, ph, "gp", tr, go)
                    c.step(gp.tensor_scalar(lrs[:, :, :], lst[:, :, 1:3], 1e-5, None, ALU.add))
                    gp.tensor_tensor(lrs[:, :, :].rearrange("p a b -> p (a b)"),
                                     lrs[:, :, :].rearrange("p a b -> p (a b)"),
                                     mhalf[0:EP, 0:4 * T], ALU.pow).then_inc(S["pow_done"], 1)
                    c.end()

                gathers(Trip(0, 0))
                gathers(Trip(0, 1))
                if l == 0:
                    inv_norms(Trip(0, 0))

                def edge_trip(tr):
                    if l == 0 and tr.has(1, ETRIPS):
                        inv_norms(tr.shift(1))
                    if tr.has(2, ETRIPS):
                        gathers(tr.shift(2))
                    if tr.has(-1, ETRIPS):
                        scatters(tr.shift(-1))

                trips(gp, ETRIPS, edge_trip)
                scatters(Trip(0, ETRIPS - 1))

                for b in range(2):
                    gp.wait_ge(S2["scat"][b], total2(ph, "scat"))
                gp.indirect_dma_start(FB[:, :], None, agg[:, :],
                                      bass.IndirectOffsetOnAxis(ap=head_i[:, 0:1], axis=0)).then_inc(fx_g, 16)
                gp.wait_ge(fx_dve, FIX_STEPS[l])
                gp.indirect_dma_start(agg[:, :], bass.IndirectOffsetOnAxis(ap=fixid[:, 0:1], axis=0),
                                      FN[:, :], None, bounds_check=AROWS - 1, oob_is_err=False).then_inc(fx_st, 16)

                ph = f"N{l}"

                def node_rstd(tr):
                    b = tr.b
                    gp.wait_ge(S["r_done"], cnt(ph, "r_done", tr))
                    if tr.has(-2, NTRIPS):
                        wait(gp, S["y_done"], cnt(ph, "y_done", tr.shift(-2)))
                    gp.sem_inc(go, 1)
                    c = Chain(gp, S, ph, "gpn", tr, go)
                    c.step(gp.tensor_scalar(nrs[b][:, :, 0], nmv[b][:, :, 1], 1e-5, None, ALU.add))
                    c.step(gp.tensor_tensor(nrs[b][:, :, 0], nrs[b][:, :, 0], mhalf[:, 0:T], ALU.pow))
                    c.step(gp.tensor_scalar(nrs[b][:, :, 1], nmv[b][:, :, 0], -1.0, None, ALU.mult))
                    gp.tensor_tensor(nrs[b][:, :, 1], nrs[b][:, :, 1], nrs[b][:, :, 0], ALU.mult)\
                      .then_inc(S["rstd_done"], 1)
                    c.end()

                def attr_out(tr):
                    b, q = tr.b, tr.q
                    gp.wait_ge(S4["nldx"][q], node_loads(l, tr, PERX))
                    if tr.has(-2, NTRIPS):
                        wait(gp, S2["nst"][b], cnt2(ph, "nst", tr.shift(-2)))
                    gp.sem_inc(go, 1)
                    src = XA[q][:, :] if l == 0 else X[q][:, :, ATTR]
                    gp.tensor_copy(Y[b][:, :, ATTR], src).then_inc(S["a_done"], 1)

                def coefs(tr):
                    b, q = tr.b, tr.q
                    gp.wait_ge(S4["nldx"][q], node_loads(l, tr, PERX))
                    gp.wait_ge(S4["nlda"][q], node_loads(l, tr, PERA))
                    att = X[q][:, :, ATTR]
                    c = Chain(gp, S, ph, "gp", tr, go)
                    if l == 1:
                        if tr.has(-1, NTRIPS):
                            gp.wait_ge(S["sin_done"], cnt(ph, "sin_done", tr.shift(-1)))
                        c.step(gp.tensor_tensor(ang[:, 0:T], AG[q][:, :, F], att, ALU.mult))
                        c.step(gp.tensor_scalar(ang[:, T:], ang[:, 0:T], HALF_PI, None, ALU.add))
                        c.step(gp.tensor_scalar(angk[:, :], ang[:, :], INV_2PI, MAGIC, ALU.mult, ALU.add))
                        c.step(gp.tensor_scalar(angk[:, :], angk[:, :], -MAGIC, None, ALU.add))
                        for part in TWO_PI:
                            c.step(gp.tensor_scalar(angr[:, :], angk[:, :], -part, None, ALU.mult))
                            c.step(gp.tensor_tensor(ang[:, :], ang[:, :], angr[:, :], ALU.add))
                        gp.tensor_scalar(angr[:, :], ang[:, :], PI, -PI, ALU.min, ALU.max)\
                          .then_inc(S["ang_done"], 1)
                        gp.wait_ge(S["sin_done"], cnt(ph, "sin_done", tr))
                    if tr.has(-2, NTRIPS):
                        wait(gp, S["r_done"], cnt(ph, "r_done", tr.shift(-2)))
                    if l == 1:
                        gp.tensor_tensor(co[b][:, 0:T], sc8[:, T:], att, ALU.mult).then_inc(S["coef_done"], 1)
                        c.step(gp.tensor_tensor(co[b][:, T:], sc8[:, 0:T], att, ALU.mult))
                    if l == 2:
                        gp.wait_ge(S["ang_done"], cnt(ph, "ang_done", tr))
                        c.step(gp.tensor_tensor(co[b][:, T:], co[b][:, T:], att, ALU.mult))
                        c.step(gp.tensor_tensor(co[b][:, 0:T], co[b][:, T:], co[b][:, T:], ALU.mult))
                        c.step(gp.tensor_tensor(co[b][:, T:], co[b][:, 0:T], AG[q][:, :, F], ALU.mult))
                    gp.tensor_tensor(T2B[b][:, :, :], AG[q][:, :, 0:F],
                                     co[b][:, T:].unsqueeze(2).broadcast_to((NP, T, F)), ALU.mult)\
                      .then_inc(S["t2_done"], 1)
                    c.end()

                if l in (1, 2):
                    coefs(Trip(0, 0))

                def node_trip(tr):
                    if l in (1, 2) and tr.has(1, NTRIPS):
                        coefs(tr.shift(1))
                    attr_out(tr)
                    if tr.has(-1, NTRIPS):
                        node_rstd(tr.shift(-1))

                trips(gp, NTRIPS, node_trip, NBUF)
                node_rstd(Trip(0, NTRIPS - 1))

        @block.scalar
        def _(ac):
            ac.wait_ge(w_zero, N_CLEAR + 2)
            az = agg.rearrange("(p r) f -> p (r f)", p=128)
            for i in range(24):
                ac.dma_start(az[:, 3136 * i:3136 * (i + 1)], zeros[:, :]).then_inc(z_store, 16)
            ac.wait_ge(w_zero, N_CLEAR + 1)
            ac.wait_ge(w_pe, 1)
            ac.copy(wvt[:, 0:96], psR[0:CS, 0, 0:96]).then_inc(w_act, 1)
            ac.copy(wvt[:, 192:224], psR[0:CS, 0, 64:96]).then_inc(w_act, 1)
            ac.wait_ge(w_pe, 2)
            ac.wait_ge(w_load, N_LOAD)
            ac.copy(ra[0][0:64, 128:160], psR[0:64, 1, 0:32]).then_inc(w_act, 1)
            ac.copy(rb[0][0:32, 224:256], psR[0:32, 2, 0:32]).then_inc(w_act, 1)
            ac.wait_ge(w_pe, 3)
            ac.copy(brow[0:1, 96:160], psF[0:1, 0, 0:64]).then_inc(w_act, 1)

            for l in range(4):
                ph, rad, R_ = f"E{l}", LAYERS[l]["rad"], ring_banks(l)

                def evac(tr, k, dst, rows, cols, func=ACT.Copy, scale=1.0):
                    pos = ring_pos(l, tr, k)
                    ac.wait_ge(S["pe_ring"], ring_val(ph, l, tr, k))
                    ac.activation(dst, psR[0:rows, pos % R_, 0:cols], func, scale=scale)\
                      .then_inc(S["act_ring"], 1)

                def squares(tr):
                    ac.wait_ge(S2["gath"][tr.b], cnt2(ph, "gath", tr))
                    if tr.has(-1, ETRIPS):
                        ac.wait_ge(S["stat_done"], cnt(ph, "stat_done", tr.shift(-1)))
                    ac.activation(sqv[:, 0:T, :], GS[tr.b][:, :, CS:F], ACT.Square, scale=CV ** -0.5)
                    ac.activation(sqv[:, T:, :], GD[tr.b][:, :, CS:F], ACT.Square, scale=CV ** -0.5)\
                      .then_inc(S["sq_done"], 1)

                def norm_and_messages(tr):
                    for c in range(3):
                        evac(tr, f"n{c}", ET_[c][0:(64 if c == 2 else 128), :], 64 if c == 2 else 128, EC)
                    ac.wait_ge(S["ob_full"], ob_val(ph, tr, "M"))
                    ac.copy(MG[:, :, :].rearrange("p (b t) f -> p b (t f)", b=2), psO[0:EP, :, 0:2 * F])\
                      .then_inc(S["ob_evac"], 1)

                if l == 0:
                    squares(Trip(0, 0))
                    norm_and_messages(Trip(0, 0))

                def edge_trip(tr):
                    nc_ = CHUNKS[l]
                    if l == 0:
                        if tr.has(1, ETRIPS):
                            squares(tr.shift(1))
                        evac(tr, "e", esT[0:16, :], 16, EC)
                    else:
                        evac(tr, "e", esT[0:rad, :], rad, EC)
                        evac(tr, "h", hidT[:, :], CS, EC, ACT.Silu)
                    for c in range(nc_):
                        w = 96 if c == 2 else 128
                        evac(tr, f"w{c}", wT[c][0:w, :], w, EC)
                    if l == 0:
                        for h in range(2):
                            ac.wait_ge(S["ob_full"], ob_val(ph, tr, f"o{h}"))
                            ac.copy(O[0][:, 2 * h:2 * h + 2, :], psO[0:EP, :, 0:288]).then_inc(S["ob_evac"], 1)
                        ac.wait_ge(S["ob_evac"], ob_val(ph, tr, "o1"))
                        ac.activation(SG[:, :, :], O[0][:, :, 160:256], ACT.Tanh, scale=0.5)\
                          .then_inc(S["tanh_done"], 1)
                        if tr.has(1, ETRIPS):
                            norm_and_messages(tr.shift(1))
                        ac.wait_ge(S["d_ready"], cnt(ph, "d_ready", tr))
                        ac.activation(pc[:, :, :], dd[:, :, :], ACT.Exp).then_inc(S["exp_done"], 1)
                    for c in range(nc_):
                        w = 96 if c == 2 else 128
                        evac(tr, f"t{c}", ET_[c][0:w, :], w, EC)
                    if l == 0:
                        ac.wait_ge(S["ob_full"], ob_val(ph, tr, "O2"))
                        ac.copy(O2[:, :, 0:48].rearrange("p (b t) f -> p b t f", b=2),
                                psO[0:EP, :, 0:384].rearrange("p b (t f) -> p b t f", t=2 * H))\
                          .then_inc(S["ob_evac"], 1)
                    else:
                        w = EOW[l]
                        ac.wait_ge(S["ob_full"], cnt(ph, "ob_full", tr))
                        ac.copy(O[tr.b][:, :, 0:w].rearrange("p (b t) f -> p b t f", b=2),
                                psO[0:EP, :, 0:2 * w].rearrange("p b (t f) -> p b t f", t=2))\
                          .then_inc(S["ob_evac"], 1)

                trips(ac, ETRIPS, edge_trip)
                if l == 0:
                    ac.wait_ge(fx_dve, 3)
                    ac.activation(fm[:, 2:4, :], fm[:, 2:4, :], ACT.Exp).then_inc(fx_act, 1)

                ph = f"N{l}"

                def normed(tr):
                    b = tr.b
                    ac.wait_ge(S["rstd_done"], cnt(ph, "rstd_done", tr))
                    if tr.has(-2, NTRIPS):
                        wait(ac, S2["nst"][b], cnt2(ph, "nst", tr.shift(-2)))
                    ac.wait_ge(S["a_done"], cnt(ph, "a_done", tr))
                    for j in range(T):
                        last = ac.activation(Y[b][:, j, 0:F], R[b][:, j, 0:F], ACT.Identity,
                                             bias=nrs[b][:, j, 1:2], scale=nrs[b][:, j, 0:1])
                    last.then_inc(S["y_done"], 1)
                    ac.wait_ge(S["y_done"], cnt(ph, "y_done", tr))
                    ac.sem_inc(ac_go, 1)
                    if tr.g == NTRIPS - 1:
                        ac.wait_ge(S2["nst"][1 - b], cnt2(ph, "nst", tr.shift(-1)))
                        ac.sem_inc(ac_go, 1)
                    ac.dma_start(tab_rows(NEXT[l], tr, XW if l < 3 else F),
                                 Y[b][:, :, 0:XW if l < 3 else F]).then_inc(S2["nst"][b], 16)

                def rows_t(tr):
                    b = tr.b
                    if tr.has(-2, NTRIPS):
                        ac.wait_ge(S["ob_full"], cnt(ph, "ob_full", tr.shift(-2)))
                    for k, dst, rows in ((0, NT1[b], 96), (1, NT2[b], CS)):
                        ac.wait_ge(S["pe_ring"], cnt(ph, "pe_ring", tr, k + 1))
                        ac.copy(dst[:, :], ps[0:rows, 2 * b + k, :]).then_inc(S["act_ring"], 1)

                def sines(tr):
                    ac.wait_ge(S["ang_done"], cnt(ph, "ang_done", tr))
                    if tr.has(-1, NTRIPS):
                        ac.wait_ge(S["t2_done"], cnt(ph, "t2_done", tr.shift(-1)))
                    ac.activation(sc8[:, :], angr[:, :], ACT.Sin).then_inc(S["sin_done"], 1)

                rows_t(Trip(0, 0))
                if l == 1:
                    sines(Trip(0, 0))

                def node_trip(tr):
                    if tr.has(1, NTRIPS):
                        rows_t(tr.shift(1))
                        if l == 1:
                            sines(tr.shift(1))
                    if l == 3:
                        ac.wait_ge(S["gate_in"], cnt(ph, "gate_in", tr))
                        ac.activation(SGN[tr.b][:, :, :], R3[tr.b][:, :, 96:192], ACT.Sigmoid)\
                          .then_inc(S["sig_done"], 1)
                    if tr.has(-1, NTRIPS):
                        normed(tr.shift(-1))

                trips(ac, NTRIPS, node_trip, NBUF)
                normed(Trip(0, NTRIPS - 1))

        @block.tensor
        def _(pe):
            def tr_(dst, src, parts):
                return pe.transpose(dst, src, ident[0:parts, 0:parts])

            pe.wait_ge(w_zero, N_CLEAR + 14)
            pe.wait_ge(w_load, N_LOAD)
            tr_(psR[0:CS, 0, 0:96], wval[:, :], 96).then_inc(w_pe, 1)
            pe.wait_ge(w_act, 2)
            pe.matmul(psR[0:64, 1, 0:32], wvt[:, 0:64], wg[:, :], start=True, stop=True)
            pe.matmul(psR[0:32, 2, 0:32], wvt[:, 192:224], wg[:, :], start=True, stop=True).then_inc(w_pe, 1)
            pe.matmul(psF[0:1, 0, 0:64], beta[:, :], wsrc[:, :], start=True, stop=False)
            pe.matmul(psF[0:1, 0, 0:64], beta[:, :], wdst[:, :], start=False, stop=True).then_inc(w_pe, 1)
            pe.wait_ge(w_act, 5)
            pe.wait_ge(w_dve, SETUP_STEPS)

            for l in range(4):
                ph, rad, R_ = f"E{l}", LAYERS[l]["rad"], ring_banks(l)
                nc_ = CHUNKS[l]
                if l:
                    pe.wait_ge(S["act_ring"], total(f"N{l - 1}", "act_ring"))
                    pe.wait_ge(S["ob_used"], total(f"N{l - 1}", "ob_used"))

                def slot(tr, k):
                    pos = ring_pos(l, tr, k)
                    v = ring_val(ph, l, tr, k)
                    base = BASE[ph].get("act_ring", 0)
                    if not isinstance(v, int) or v - base > R_:
                        pe.wait_ge(S["act_ring"], v - R_)
                        pe.sem_inc(pe_go, 1)
                    return psR[:, pos % R_, :]

                def out_of_ring(tr, k):
                    pe.wait_ge(S["act_ring"], ring_val(ph, l, tr, k))

                def ob_free(v):
                    if not isinstance(v, int) or v > BASE[ph].get("ob_evac", 0) + 1:
                        pe.wait_ge(S["ob_evac"], v - 1)

                def norm_and_messages(tr):
                    pe.wait_ge(S["xn_done"], cnt(ph, "xn_done", tr))
                    for c in range(3):
                        bank = slot(tr, f"n{c}")
                        for j in range(T):
                            if c < 2:
                                last = tr_(bank[:, j * EP:(j + 1) * EP], XN[:, j, c, 0:128], EP)
                            else:
                                last = tr_(bank[0:64, j * EP:(j + 1) * EP], XT[:, j, :], EP)
                        last.then_inc(S["pe_ring"], 1)
                    out_of_ring(tr, "n2")
                    ob_free(ob_val(ph, tr, "M"))
                    for j in range(T):
                        dst, at = psO[0:EP, j // 2, F * (j % 2):F * (j % 2) + F], slice(j * EP, (j + 1) * EP)
                        pe.matmul(dst, onerow[:, :], brow[:, :], start=True, stop=False)
                        pe.matmul(dst, ET_[0][:, at], wm_s[:, :], start=False, stop=False)
                        pe.matmul(dst, ET_[1][:, at], wm_d[:, :], start=False, stop=False)
                        last = pe.matmul(dst, ET_[2][0:64, at], wm_t[:, :], start=False, stop=True)
                    last.then_inc(S["ob_full"], 1)

                if l == 0:
                    norm_and_messages(Trip(0, 0))

                def edge_trip(tr):
                    b = tr.b
                    pe.wait_ge(S2["lda"][b], cnt2(ph, "lda", tr))
                    bank = slot(tr, "e")
                    for j in range(T):
                        last = tr_(bank[0:rad, j * EP:(j + 1) * EP], es_in[b][:, j * rad:(j + 1) * rad], EP)
                    last.then_inc(S["pe_ring"], 1)
                    out_of_ring(tr, "e")
                    pe.sem_inc(pe_go, 1)
                    src = esT[0:rad, :]
                    if l:
                        bank = slot(tr, "h")
                        pe.matmul(bank[0:CS, 0:EC], fc1[l][:, :], src, start=True, stop=True)\
                          .then_inc(S["pe_ring"], 1)
                        out_of_ring(tr, "h")
                        pe.sem_inc(pe_go, 1)
                        src = hidT[:, :]
                    for c in range(nc_):
                        w = 96 if c == 2 else 128
                        bank = slot(tr, f"w{c}")
                        pe.matmul(bank[0:w, 0:EC], fc2[l][:, 128 * c:128 * c + w], src, start=True, stop=True)\
                          .then_inc(S["pe_ring"], 1)
                    pe.wait_ge(S["e_done"], cnt(ph, "e_done", tr))
                    if l == 0:
                        for c in range(3):
                            w = 96 if c == 2 else 128
                            for j in range(T):
                                last = tr_(psF[0:w, c, j * EP:(j + 1) * EP], EE[:, j, 128 * c:128 * c + w], EP)
                            last.then_inc(S["f_done"], 1)
                    else:
                        for c in range(nc_):
                            w = 96 if c == 2 else 128
                            bank = slot(tr, f"t{c}")
                            for j in range(T):
                                last = tr_(bank[0:w, j * EP:(j + 1) * EP], EE[:, j, 128 * c:128 * c + w], EP)
                            last.then_inc(S["pe_ring"], 1)
                        for c in range(nc_):
                            w = 96 if c == 2 else 128
                            out_of_ring(tr, f"t{c}")
                            wf = wf1[l] if c == 1 else wf2[l]
                            pe.matmul(psF[0:w, c, 0:EC], wf[0:w, 0:w], ET_[c][0:w, :], start=True, stop=True)\
                              .then_inc(S["f_done"], 1)
                    pe.wait_ge(S["prod_done"], cnt(ph, "prod_done", tr, nc_))
                    w = EOW[l]
                    per_bank = 1 if l == 0 else 2
                    for j in range(T):
                        if j % (2 * per_bank) == 0:
                            if l == 0:
                                ob_free(ob_val(ph, tr, f"o{j // 2}"))
                            else:
                                ob_free(cnt(ph, "ob_evac", tr))
                        o = w * (j % per_bank)
                        dst = psO[0:EP, (j // per_bank) % 2, :]
                        at = slice(j * EP, (j + 1) * EP)
                        pe.matmul(dst[:, o:o + w], PR[0][:, at], rb[l][:, :], start=True, stop=True)
                        if nc_ == 3:
                            pe.matmul(dst[:, o:o + 96], PR[2][0:96, at], rx[l][:, :], start=False, stop=True,
                                      skip_group_check=True)
                        last = pe.matmul(dst[:, o + 96:o + w], PR[1][:, at], ra[l][:, :], start=False, stop=True,
                                         skip_group_check=True)
                        if j % (2 * per_bank) == 2 * per_bank - 1:
                            last.then_inc(S["ob_full"], 1)
                    if l == 0:
                        if tr.has(1, ETRIPS):
                            norm_and_messages(tr.shift(1))
                        pe.wait_ge(S["e2_done"], cnt(ph, "e2_done", tr))
                        for c in range(3):
                            w = 96 if c == 2 else 128
                            bank = slot(tr, f"t{c}")
                            for j in range(T):
                                last = tr_(bank[0:w, j * EP:(j + 1) * EP], E2[:, j, 128 * c:128 * c + w], EP)
                            last.then_inc(S["pe_ring"], 1)
                        out_of_ring(tr, "t2")
                        ob_free(ob_val(ph, tr, "O2"))
                        for j in range(T):
                            dst, at = psO[0:EP, j // 2, 192 * (j % 2):192 * (j % 2) + 192], slice(j * EP, (j + 1) * EP)
                            pe.matmul(dst, ET_[1][:, at], r2a[:, :], start=True, stop=False)
                            pe.matmul(dst, ET_[0][:, at], r2b[:, :], start=False, stop=False)
                            last = pe.matmul(dst, ET_[2][0:96, at], r2x[:, :], start=False, stop=True)
                        last.then_inc(S["ob_full"], 1)

                trips(pe, ETRIPS, edge_trip)

                pe.wait_ge(S["ob_evac"], total(ph, "ob_evac"))
                if l == 0:
                    pe.wait_ge(fx_dve, 1)
                    pe.matmul(psF[0:EP, 0, 0:H * EP], ones_k[:, :], fdg[:, :], start=True, stop=True)\
                      .then_inc(fx_mm, 1)
                    pe.wait_ge(fx_dve, 4)
                else:
                    pe.wait_ge(fx_rd, 16 * (l + 1))
                pe.matmul(psO[0:EP, 0, 0:AW], same[:, :], FX[:, :], start=True, stop=True).then_inc(fx_mm, 1)

                ph = f"N{l}"
                pe.wait_ge(fx_dve, FIX_STEPS[l])
                pe.wait_ge(S["act_ring"], total(f"E{l}", "act_ring"))

                def transposes(tr):
                    b, q = tr.b, tr.q
                    if l == 0:
                        pe.wait_ge(S["agn_done"], cnt(ph, "agn_done", tr))
                        src = AGN[b]
                    else:
                        pe.wait_ge(S4["nldx"][q], node_loads(l, tr, PERX))
                        src = X[q]
                    pe.sem_inc(pe_go, 1)
                    for k, lo, hi in ((0, 0, 96), (1, 96, F)):
                        if tr.has(-2, NTRIPS):
                            pe.wait_ge(S["act_ring"], cnt(ph, "act_ring", tr.shift(-2), k + 1))
                            pe.sem_inc(pe_go, 1)
                        for j in range(T):
                            last = tr_(ps[0:hi - lo, 2 * b + k, j * NP:(j + 1) * NP], src[:, j, lo:hi], NP)
                        last.then_inc(S["pe_ring"], 1)

                transposes(Trip(0, 0))

                def node_trip(tr):
                    b, w = tr.b, NOW[l]
                    pe.wait_ge(S["act_ring"], cnt(ph, "act_ring", tr, 2))
                    if tr.has(-2, NTRIPS):
                        pe.wait_ge(S["ob_used"], cnt(ph, "ob_used", tr.shift(-2)))
                    for j in range(T):
                        dst, o, at = NPO[b][:, j // 2, :], w * (j % 2), slice(j * NP, (j + 1) * NP)
                        pe.matmul(dst[:, o:o + 96], NT1[b][:, at], nw1[l][:, :], start=True, stop=True)
                        last = pe.matmul(dst[:, o + 96:o + w], NT2[b][:, at], nw2[l][:, :], start=True, stop=True)
                    last.then_inc(S["ob_full"], 1)
                    if tr.has(1, NTRIPS):
                        transposes(tr.shift(1))

                trips(pe, NTRIPS, node_trip, NBUF)

        @block.vector
        def _(ve):
            n = [0]

            def step(ins):
                n[0] += 1
                ins.then_inc(w_dve, 1)
                ve.wait_ge(w_dve, n[0])

            def bc(ap, shape):
                return ap.broadcast_to(shape)

            ve.wait_ge(w_zero, N_CLEAR + 14)
            ve.wait_ge(g_load, 80)
            step(ve.tensor_copy(dst_f[:, :], dst_i[:, :]))
            step(ve.tensor_copy(edge_f[:, :], edge_i[:, :]))
            step(ve.tensor_copy(hrow[:, :], hrow_i[:, :]))
            step(ve.tensor_copy(cf[:, 0:1], pid[:, :]))
            step(ve.tensor_copy(head_i[:, :], dst_i[:, 0:1]))
            step(ve.tensor_scalar(cf[:, 1:2], cf[:, 0:1], float(SKIP - N), None, ALU.add))
            keep, mask = runs[:, :, 0], runs[:, :, 1]
            step(ve.memset(wk1[:, :], 0.0))
            step(ve.tensor_tensor(wk1[:, 1:ET], dst_f[:, 1:ET], dst_f[:, 0:ET - 1], ALU.is_equal))
            step(ve.tensor_copy(keep, wk1[:, :]))
            step(ve.tensor_scalar(mask, wk1[:, :], -1.0, BIG, ALU.add, ALU.mult))
            step(ve.tensor_tensor_scan(wk2[:, :], wk1[:, :], wk_one[:, :], 0.0, ALU.mult, ALU.add))
            step(ve.tensor_copy(runs[:, :, 2], wk2[:, :]))
            step(ve.tensor_tensor(cf[:, 2:3], dst_f[:, 0:1], edge_f[:, 1:2], ALU.is_equal))
            step(ve.tensor_tensor(cf[:, 4:5], dst_f[:, 0:1], edge_f[:, 0:1], ALU.is_equal))
            step(ve.tensor_tensor(cf[:, 5:6], edge_f[:, 0:1], edge_f[:, 2:3], ALU.is_equal))
            step(ve.tensor_tensor(cf[:, 4:5], cf[:, 4:5], cf[:, 5:6], ALU.mult))
            step(ve.tensor_scalar(cf[:, 4:5], cf[:, 4:5], -1.0, 1.0, ALU.mult, ALU.add))
            step(ve.tensor_tensor(cf[:, 3:4], cf[:, 2:3], cf[:, 4:5], ALU.mult))
            step(ve.tensor_tensor(cf[:, 6:7], dst_f[:, 0:1], cf[:, 1:2], ALU.subtract))
            step(ve.tensor_tensor(cf[:, 6:7], cf[:, 6:7], cf[:, 3:4], ALU.mult))
            step(ve.tensor_tensor(cf[:, 6:7], cf[:, 6:7], cf[:, 1:2], ALU.add))
            step(ve.tensor_copy(fixid[:, :], cf[:, 6:7]))
            step(ve.tensor_scalar(wk2[:, :], dst_f[:, :], dst_f[:, 0:1], cf[:, 2:3], ALU.is_equal, ALU.mult))
            step(ve.tensor_scalar(wk1[:, :], dst_f[:, :], cf[:, 0:1], -1.0, ALU.subtract, ALU.mult))
            step(ve.tensor_tensor(wk1[:, :], wk1[:, :], wk2[:, :], ALU.mult))
            step(ve.tensor_tensor(wk1[:, :], wk1[:, :], dst_f[:, :], ALU.add))
            step(ve.tensor_scalar(wk1[:, :], wk1[:, :], cf[:, 1:2], None, ALU.subtract))
            step(ve.memset(wk2[:, :], 1.0))
            step(ve.tensor_scalar(wk2[:, 0:ET - 1], runs[:, 1:ET, 0], -1.0, 1.0, ALU.mult, ALU.add))
            step(ve.tensor_tensor(wk1[:, :], wk1[:, :], wk2[:, :], ALU.mult))
            step(ve.tensor_scalar(wk1[:, :], wk1[:, :], cf[:, 1:2], None, ALU.add))
            step(ve.tensor_copy(scix[:, :], wk1[:, :]))
            step(ve.tensor_scalar(same[:, :], hrow[:, :], dst_f[:, 0:1], None, ALU.is_equal))
            step(ve.tensor_scalar(samen[:, :], same[:, :], -1.0, BIG, ALU.add, ALU.mult))
            assert n[0] == GRAPH_STEPS, n
            ve.wait_ge(w_load, N_LOAD)
            ve.wait_ge(w_act, 5)
            for region, factor in scales:
                step(ve.tensor_scalar(region, region, factor, None, ALU.mult))
            step(ve.tensor_scalar(rb[0][0:32, 96:256], rb[0][0:32, 96:256], r3, None, ALU.mult))
            for t, g in ((wm_s, g1), (wm_d, g1), (wm_t, g3), (r2a, cA), (r2b, cB), (r2x, cX)):
                step(ve.tensor_scalar(t[:, :], t[:, :], g[:, 0:1], None, ALU.mult))
            step(ve.tensor_scalar(r2b[0:32, :], r2b[0:32, :], r3, None, ALU.mult))
            step(ve.tensor_scalar(r2x[:, :], r2x[:, :], r2, None, ALU.mult))
            assert n[0] == SETUP_STEPS, n

            fx = [0]

            def fstep(ins, own=False):
                fx[0] += 1
                ins.then_inc(fx_dve, 1)
                ve.wait_ge(fx_dve, fx[0])

            for l in range(4):
                ph, nc_, cross = f"E{l}", CHUNKS[l], LAYERS[l]["cross"]

                def attrs(tr, c):
                    b = tr.b
                    wait(ve, S2["lda"][b], cnt2(ph, "lda", tr))
                    if l == 0:
                        ve.tensor_copy(yc[b][:, :, 0:4], y_in[b][:, :, :])
                        ve.tensor_copy(yc[b][:, :, 4:6], y_in[b][:, :, 1:3])
                    else:
                        att = G[b][:, :, ATTR:ATTR + 1]
                        ve.tensor_tensor(yc[b][:, :, 0:4], y_in[b][:, :, :], bc(att, (EP, T, 4)), ALU.mult)
                        ve.tensor_tensor(yc[b][:, :, 4:6], y_in[b][:, :, 1:3], bc(att, (EP, T, 2)), ALU.mult)
                    c.step(ve.tensor_copy(kc[b][:, :, :], k_in[b][:, :, :]))

                def tp_inputs(src, y, dst, c, done):
                    v = src[:, :, 0:96].rearrange("p t (d c) -> p t d c", d=3)
                    sh = (EP, T, 3, CV)

                    def times(out, vd, yd, m):
                        return ve.tensor_tensor(out, v[:, :, vd:vd + m, :],
                                                bc(y[:, :, yd:yd + m].unsqueeze(3), (EP, T, m, CV)), ALU.mult)

                    t4 = tmp[:, :, :].rearrange("p t (d c) -> p t d c", d=3)
                    t5 = tmp2[:, :, :].rearrange("p t (d c) -> p t d c", d=3)
                    times(t4, 0, 1, 3)
                    if cross:
                        x4 = dst[:, :, C_X:C_X + 96].rearrange("p t (d c) -> p t d c", d=3)
                        times(x4[:, :, 0:2, :], 1, 3, 2)
                        times(x4[:, :, 2:3, :], 0, 5, 1)
                        times(t5[:, :, 0:1, :], 2, 2, 1)
                        times(t5[:, :, 1:3, :], 0, 3, 2)
                    ve.tensor_copy(dst[:, :, C_S:C_S + CS], src[:, :, 96:F])
                    c.step(ve.tensor_tensor(dst[:, :, C_YV:C_YV + F], src[:, :, 0:F],
                                            bc(y[:, :, 0:1], (EP, T, F)), ALU.mult))
                    if cross:
                        xs = dst[:, :, C_X:C_X + 96]
                        ve.tensor_tensor(xs, xs, tmp2[:, :, :], ALU.subtract)
                    ve.tensor_reduce(dst[:, :, C_VY:C_VY + CV], tmp[:, :, :].rearrange("p t (d c) -> p t c d", d=3),
                                     AX.X, ALU.add).then_inc(S[done], 1)

                def inputs(tr):
                    b = tr.b
                    c = Chain(ve, S, ph, "d_in", tr)
                    if l == 0:
                        ve.wait_ge(S["ob_evac"], ob_val(ph, tr, "M"))
                        src = MG
                    else:
                        ve.wait_ge(S2["gath"][b], cnt2(ph, "gath", tr))
                        src = G[b]
                    attrs(tr, c)
                    tp_inputs(src, yc[b], EE, c, "e_done")
                    c.end()

                def products(tr):
                    for c in range(nc_):
                        w = 96 if c == 2 else 128
                        ve.wait_ge(S["f_done"], cnt(ph, "f_done", tr, c + 1))
                        if c == 0:
                            ve.wait_ge(S["act_ring"], ring_val(ph, l, tr, f"w{nc_ - 1}"))
                        ve.tensor_tensor(PR[c][0:w, :], psF[0:w, c, 0:EC], wT[c][0:w, :], ALU.mult)\
                          .then_inc(S["prod_done"], 1)

                def times_u(o, uo, y, c):
                    u = o[:, :, uo:uo + CV].unsqueeze(2)
                    t4 = tmp3[:, :, :].rearrange("p t (d c) -> p t d c", d=3)
                    c.step(ve.tensor_tensor(t4, bc(u, (EP, T, 3, CV)), bc(y[:, :, 1:4].unsqueeze(3), (EP, T, 3, CV)),
                                            ALU.mult))
                    c.step(ve.tensor_tensor(o[:, :, 0:96], o[:, :, 0:96], tmp3[:, :, :], ALU.add))

                def out_free(tr):
                    if tr.has(-2, ETRIPS):
                        wait(ve, S2["scat"][tr.b], cnt2(ph, "scat", tr.shift(-2)))

                def messages(tr):
                    b = tr.b
                    c = Chain(ve, S, ph, "d_post", tr)
                    w = EOW[l] - 32
                    ve.wait_ge(S["ob_evac"], cnt(ph, "ob_evac", tr))
                    times_u(O[b], w, yc[b], c)
                    out_free(tr)
                    if l == 2:
                        ve.tensor_copy(OUT[b][:, :, w], kc[b][:, :, 2])
                    for t in range(T):
                        prev = OUT[b][:, t - 1, 0:w] if t else OUT[1 - b][:, T - 1, 0:w]
                        ins = ve.scalar_tensor_tensor(OUT[b][:, t, 0:w], prev, kc[b][:, t, 0:1], O[b][:, t, 0:w],
                                                      op0=ALU.mult, op1=ALU.add)
                        if t < T - 1:
                            c.step(ins)
                    ins.then_inc(S["msg_done"], 1)
                    ve.wait_ge(S["msg_done"], cnt(ph, "msg_done", tr))
                    c.end()

                def norm_stats(tr):
                    b = tr.b
                    c = Chain(ve, S, ph, "d_norm", tr)
                    ve.wait_ge(S2["gath"][b], cnt2(ph, "gath", tr))
                    for i in range(2 * T):
                        src = (GS, GD)[i // T][b]
                        ins = ve.bn_stats(bst[:, i, :], src[:, i % T, 0:CS])
                    c.step(ins)
                    ve.sem_inc(ve_go, 1)
                    for i in range(2 * T):
                        ve.bn_aggr(lst[:, i, 0:2], bst[:, i, :])
                    ve.wait_ge(S["sq_done"], cnt(ph, "sq_done", tr))
                    ve.tensor_reduce(lst[:, :, 2], sqv[:, :, :], AX.X, ALU.add).then_inc(S["stat_done"], 1)
                    ve.wait_ge(S["stat_done"], cnt(ph, "stat_done", tr))
                    c.end()

                def norm_rows(tr):
                    b = tr.b
                    ve.wait_ge(S["pow_done"], cnt(ph, "pow_done", tr))
                    for i in range(2 * T):
                        src = (GS, GD)[i // T][b]
                        o = XN[:, i % T, i // T, 96:F]
                        ve.tensor_scalar(o, src[:, i % T, 0:CS], lst[:, i, 0:1], lrs[:, i, 0:1],
                                         ALU.subtract, ALU.mult)
                        ve.tensor_scalar(XT[:, i % T, 32 * (i // T):32 * (i // T) + 32], src[:, i % T, 32:CS],
                                         lst[:, i, 0:1], lrs[:, i, 0:1], ALU.subtract, ALU.mult)
                    for side in range(2):
                        src = (GS, GD)[side][b][:, :, CS:F].rearrange("p t (c d) -> p t d c", d=3)
                        ins = ve.tensor_tensor(XN[:, :, side, 0:96].rearrange("p t (d c) -> p t d c", d=3), src,
                                               bc(lrs[:, side * T:side * T + T, 1:2].unsqueeze(3), (EP, T, 3, CV)),
                                               ALU.mult)
                    ins.then_inc(S["xn_done"], 1)

                def first_outputs(tr):
                    b = tr.b
                    c = Chain(ve, S, ph, "d_post", tr)
                    o = O[0]
                    ve.wait_ge(S["ob_evac"], ob_val(ph, tr, "o1"))
                    c.step(ve.scalar_tensor_tensor(LK[:, :, :], o[:, :, 96:160], 0.2, o[:, :, 96:160],
                                                   op0=ALU.mult, op1=ALU.max))
                    c.step(ve.tensor_tensor(LK[:, :, :], LK[:, :, :], bc(adot[:, :].unsqueeze(1), (EP, T, CS)), ALU.mult))
                    c.step(ve.tensor_reduce(al[:, :], LK[:, :, :].rearrange("p t (h s) -> p (t h) s", s=AS),
                                            AX.X, ALU.add))
                    for t in range(T):
                        prev = mx[b][:, H * (t - 1):H * t] if t else mx[1 - b][:, H * (T - 1):]
                        c.step(ve.scalar_tensor_tensor(mx[b][:, H * t:H * t + H], prev, kc[b][:, t, 1:2],
                                                       al[:, H * t:H * t + H], op0=ALU.add, op1=ALU.max))
                    ve.tensor_tensor(dd[:, 0, :], al[:, :], mx[b][:, :], ALU.subtract)
                    ve.tensor_tensor(dd[:, 1, 0:H], mx[1 - b][:, H * (T - 1):], mx[b][:, 0:H], ALU.subtract)
                    c.step(ve.tensor_tensor(dd[:, 1, H:], mx[b][:, 0:H * (T - 1)], mx[b][:, H:], ALU.subtract))
                    d1 = dd[:, 1, :].rearrange("p (t h) -> p t h", h=H)
                    ve.tensor_tensor(d1, d1, bc(kc[b][:, :, 1:2], (EP, T, H)), ALU.add).then_inc(S["d_ready"], 1)
                    times_u(o, 256, yc[b], c)
                    ve.wait_ge(S["tanh_done"], cnt(ph, "tanh_done", tr))
                    ve.tensor_scalar(MG2[:, :, 96:F], SG[:, :, 0:CS], 0.5, 0.5, ALU.mult, ALU.add)
                    c.step(ve.tensor_scalar(SG2[:, :, :], SG[:, :, CS:96], 0.5, 0.5, ALU.mult, ALU.add))
                    c.step(ve.tensor_tensor(MG2[:, :, 0:96].rearrange("p t (d c) -> p t d c", d=3),
                                            o[:, :, 0:96].rearrange("p t (d c) -> p t d c", d=3),
                                            bc(SG2[:, :, :].unsqueeze(2), (EP, T, 3, CV)), ALU.mult))
                    tp_inputs(MG2, yc[b], E2, c, "e2_done")
                    c.end()

                def attention(tr):
                    b = tr.b
                    c = Chain(ve, S, ph, "d_fin", tr)
                    ve.wait_ge(S["ob_evac"], ob_val(ph, tr, "O2"))
                    o4 = O2[:, :, :].rearrange("p (t h) f -> p t h f", h=H)
                    y = yc[b]
                    for d in range(3):
                        ins = ve.tensor_tensor(tmp[:, :, 32 * d:32 * d + 32].rearrange("p t (h f) -> p t h f", h=H),
                                               o4[:, :, :, 0:AV],
                                               bc(y[:, :, 1 + d:2 + d].unsqueeze(3), (EP, T, H, AV)), ALU.mult)
                    c.step(ins)
                    for d in range(3):
                        hv = o4[:, :, :, 24 + AV * d:24 + AV * d + AV]
                        ins = ve.tensor_tensor(hv, hv,
                                               tmp[:, :, 32 * d:32 * d + 32].rearrange("p t (h f) -> p t h f", h=H),
                                               ALU.add)
                    c.step(ins)
                    ve.wait_ge(S["exp_done"], cnt(ph, "exp_done", tr))
                    c.step(ve.tensor_tensor(MS[:, :, :], O2[:, :, 8:49],
                                            bc(pc[:, 0, :].unsqueeze(2), (EP, T * H, HC + 1)), ALU.mult))
                    out_free(tr)
                    mw = H * (HC + 1)
                    ve.tensor_copy(OUT[b][:, :, mw:mw + H], mx[b][:, :].rearrange("p (t h) -> p t h", h=H))
                    for t in range(T):
                        prev = OUT[b][:, t - 1, 0:mw] if t else OUT[1 - b][:, T - 1, 0:mw]
                        c.step(ve.tensor_tensor(OUT[b][:, t, 0:mw].rearrange("p (h f) -> p h f", h=H),
                                                prev.rearrange("p (h f) -> p h f", h=H),
                                                bc(pc[:, 1, H * t:H * t + H].unsqueeze(2), (EP, H, HC + 1)), ALU.mult))
                        ins = ve.tensor_tensor(OUT[b][:, t, 0:mw], OUT[b][:, t, 0:mw],
                                               MS[:, H * t:H * t + H, :].rearrange("p h f -> p (h f)"), ALU.add)
                        if t < T - 1:
                            c.step(ins)
                    ins.then_inc(S["msg_done"], 1)
                    ve.wait_ge(S["msg_done"], cnt(ph, "msg_done", tr))
                    c.end()

                if l == 0:
                    norm_stats(Trip(0, 0))
                    norm_rows(Trip(0, 0))

                    def edge_trip(tr):
                        inputs(tr)
                        if tr.has(1, ETRIPS):
                            norm_stats(tr.shift(1))
                        products(tr)
                        if tr.has(1, ETRIPS):
                            norm_rows(tr.shift(1))
                        if tr.has(-1, ETRIPS):
                            attention(tr.shift(-1))
                        first_outputs(tr)

                    trips(ve, ETRIPS, edge_trip)
                    attention(Trip(0, ETRIPS - 1))
                else:
                    inputs(Trip(0, 0))

                    def edge_trip(tr):
                        if tr.has(-1, ETRIPS):
                            messages(tr.shift(-1))
                        products(tr)
                        if tr.has(1, ETRIPS):
                            inputs(tr.shift(1))

                    trips(ve, ETRIPS, edge_trip)
                    messages(Trip(0, ETRIPS - 1))

                ve.wait_ge(fx_rd, 16 * (l + 1))
                mw = H * (HC + 1)
                if l == 0:
                    cn, mrow = cf[:, 2:3], FX[:, mw:mw + H]
                    fxx = Chain0(ve, w_dve, SETUP_STEPS)
                    fxx.step(ve.tensor_scalar(fm[:, 0, :], mrow, cn, None, ALU.mult))
                    fxx.step(ve.tensor_scalar(cf[:, 7:8], cn, -1.0, BIG, ALU.add, ALU.mult))
                    fxx.step(ve.tensor_scalar(fm[:, 0, :], fm[:, 0, :], cf[:, 7:8], None, ALU.add))
                    for h in range(H):
                        ins = ve.tensor_scalar(fdg[:, h * EP:(h + 1) * EP], ident[0:EP, 0:EP], fm[:, 0, h:h + 1],
                                               None, ALU.mult)
                    fstep(ins)
                    ve.wait_ge(fx_mm, 1)
                    f3 = fdg[:, :].rearrange("p (h q) -> p h q", h=H)
                    fxx.step(ve.tensor_tensor(f3, psF[0:EP, 0, 0:H * EP].rearrange("p (h q) -> p h q", h=H),
                                              bc(samen[:, :].unsqueeze(1), (EP, H, EP)), ALU.add))
                    fxx.step(ve.tensor_reduce(fm[:, 1, :], f3, AX.X, ALU.max))
                    ve.wait_ge(fx_g, 16)
                    fstep(ve.tensor_tensor(fm[:, 1, :], fm[:, 1, :], FB[:, mw:mw + H], ALU.max))
                    ve.tensor_tensor(fm[:, 2, :], fm[:, 0, :], fm[:, 1, :], ALU.subtract)
                    fstep(ve.tensor_tensor(fm[:, 3, :], FB[:, mw:mw + H], fm[:, 1, :], ALU.subtract))
                    ve.wait_ge(fx_act, 1)
                    for row, k in ((FX, 2), (FB, 3)):
                        r4 = row[:, 0:mw].rearrange("p (h f) -> p h f", h=H)
                        ins = ve.tensor_tensor(r4, r4, bc(fm[:, k, :].unsqueeze(2), (EP, H, HC + 1)), ALU.mult)
                    fstep(ins)
                    ve.wait_ge(fx_mm, 2)
                    ve.tensor_copy(FN[:, mw + H:AW], FB[:, mw + H:AW])
                    ve.tensor_copy(FN[:, mw:mw + H], fm[:, 1, :])
                    fstep(ve.tensor_tensor(FN[:, 0:mw], FB[:, 0:mw], psO[0:EP, 0, 0:mw], ALU.add))
                else:
                    ve.wait_ge(fx_g, 16 * (l + 1))
                    ve.wait_ge(fx_mm, l + 2)
                    fstep(ve.tensor_tensor(FN[:, :], FB[:, :], psO[0:EP, 0, 0:AW], ALU.add))
                assert fx[0] == FIX_STEPS[l], fx

                ph = f"N{l}"

                def ob(b, lo, w):
                    v = NPO[b][:, :, 0:2 * NOW[l]].rearrange("p b (t f) -> p b t f", t=2)
                    return v[:, :, :, lo:lo + w]

                def by_bank(t, lo, w):
                    return t[:, :, lo:lo + w].rearrange("p (b t) f -> p b t f", b=2)

                def agn(tr):
                    b, q = tr.b, tr.q
                    ve.wait_ge(S4["nlda"][q], node_loads(l, tr, PERA))
                    if tr.has(-2, NTRIPS):
                        ve.wait_ge(S["pe_ring"], cnt(ph, "pe_ring", tr.shift(-2), 2))
                    c = Chain(ve, S, ph, "d_norm", tr)
                    a4 = AG[q][:, :, 0:mw].rearrange("p t (h f) -> p t h f", h=H)
                    den = rden[b][:, :].rearrange("p (t h) -> p t h", h=H)
                    c.step(ve.tensor_scalar(den, a4[:, :, :, HC], 1e-16, None, ALU.add))
                    c.step(ve.reciprocal(rden[b][:, :], rden[b][:, :]))
                    ve.tensor_tensor(AGN[b][:, :, 96:F].rearrange("p t (h f) -> p t h f", h=H), a4[:, :, :, 0:AS],
                                     bc(den.unsqueeze(3), (NP, T, H, AS)), ALU.mult)
                    for j in range(T):
                        r4 = a4[:, j, :, AS:HC].rearrange("p h (d c) -> p d h c", d=3)
                        last = ve.tensor_tensor(AGN[b][:, j, 0:96].rearrange("p (d h c) -> p d h c", d=3, h=H), r4,
                                                bc(den[:, j, :].unsqueeze(1).unsqueeze(3), (NP, 3, H, AV)), ALU.mult)
                    last.then_inc(S["agn_done"], 1)
                    c.end()

                def counts(tr):
                    b, q = tr.b, tr.q
                    ve.wait_ge(S4["nlda"][q], node_loads(l, tr, PERA))
                    if tr.has(-2, NTRIPS):
                        ve.wait_ge(S["t2_done"], cnt(ph, "t2_done", tr.shift(-2)))
                    c = Chain(ve, S, ph, "d_norm", tr)
                    c.step(ve.tensor_scalar(rden[b][:, 0:T], AG[q][:, :, F + 1], 1.0, None, ALU.max))
                    ve.reciprocal(co[b][:, T:], rden[b][:, 0:T]).then_inc(S["ang_done"], 1)
                    c.end()

                def before_gates(tr):
                    b, q = tr.b, tr.q
                    ve.wait_ge(S4["nlda"][q], node_loads(l, tr, PERA))
                    ve.wait_ge(S["ob_full"], cnt(ph, "ob_full", tr))
                    ve.tensor_tensor(by_bank(R3[b], 0, 192), ob(b, 0, 192), by_bank(AG[q], 0, 192), ALU.add)\
                      .then_inc(S["ob_used"], 1)
                    ve.wait_ge(S["ob_used"], cnt(ph, "ob_used", tr))
                    ve.wait_ge(S4["nldx"][q], node_loads(l, tr, PERX))
                    ve.tensor_tensor(R3[b][:, :, :], R3[b][:, :, :], bc(X[q][:, :, ATTR:ATTR + 1], (NP, T, 192)),
                                     ALU.mult).then_inc(S["gate_in"], 1)

                def update(tr):
                    b, q = tr.b, tr.q
                    ve.wait_ge(S4["nldx"][q], node_loads(l, tr, PERX))
                    c = Chain(ve, S, ph, "dve", tr)
                    r, x = R[b], X[q]
                    if l < 3:
                        ve.wait_ge(S["ob_full"], cnt(ph, "ob_full", tr))
                    if tr.has(-2, NTRIPS):
                        ve.wait_ge(S["y_done"], cnt(ph, "y_done", tr.shift(-2)))
                    if l == 0:
                        for k in range(2):
                            ve.scalar_tensor_tensor(r[:, 2 * k:2 * k + 2, 96:F], x[:, 2 * k:2 * k + 2, 0:CS], 2.0,
                                                    ob(b, 96, CS)[:, k], op0=ALU.mult, op1=ALU.add)
                        for j in range(T):
                            ins = ve.scalar_tensor_tensor(
                                r[:, j, 0:96].rearrange("p (d c) -> p d c", d=3),
                                x[:, j, CS:F].rearrange("p (c d) -> p d c", d=3), 2.0,
                                NPO[b][:, j // 2, F * (j % 2):F * (j % 2) + 96].rearrange("p (d c) -> p d c", d=3),
                                op0=ALU.mult, op1=ALU.add)
                        ins.then_inc(S["ob_used"], 1)
                        ve.wait_ge(S["ob_used"], cnt(ph, "ob_used", tr))
                    elif l in (1, 2):
                        if l == 1:
                            ve.wait_ge(S["coef_done"], cnt(ph, "coef_done", tr))
                            k = co[b][:, 0:T]
                        else:
                            k = x[:, :, ATTR]
                        k4 = bc(k.rearrange("p (b t) -> p b t", b=2).unsqueeze(3), (NP, 2, 2, F))
                        ve.tensor_tensor(by_bank(r, 0, F), ob(b, 0, F), k4, ALU.mult).then_inc(S["ob_used"], 1)
                        ve.wait_ge(S["ob_used"], cnt(ph, "ob_used", tr))
                        c.step(ve.tensor_tensor(r[:, :, 0:F], r[:, :, 0:F], x[:, :, 0:F], ALU.add))
                        ve.wait_ge(S["t2_done"], cnt(ph, "t2_done", tr))
                        c.step(ve.tensor_tensor(r[:, :, 0:F], r[:, :, 0:F], T2B[b][:, :, :], ALU.add))
                    else:
                        ve.wait_ge(S["sig_done"], cnt(ph, "sig_done", tr))
                        r3 = R3[b]
                        ve.tensor_tensor(r3[:, :, 96:F], r3[:, :, 96:F], SGN[b][:, :, 0:CS], ALU.mult)
                        r4 = r3[:, :, 0:96].rearrange("p t (d c) -> p t d c", d=3)
                        c.step(ve.tensor_tensor(r4, r4, bc(SGN[b][:, :, CS:96].unsqueeze(2), (NP, T, 3, CV)),
                                                ALU.mult))
                        ve.tensor_tensor(r[:, :, 0:CS], r3[:, :, 96:F], x[:, :, 96:F], ALU.add)
                        c.step(ve.tensor_tensor(r[:, :, CS:F].rearrange("p t (c d) -> p t d c", d=3), r4,
                                                x[:, :, 0:96].rearrange("p t (d c) -> p t d c", d=3), ALU.add))
                    for j in range(T):
                        ins = ve.bn_stats(nbs[:, j, :], r[:, j, 0:F])
                    c.step(ins)
                    if tr.has(-2, NTRIPS):
                        ve.wait_ge(S["rstd_done"], cnt(ph, "rstd_done", tr.shift(-2)))
                    ve.sem_inc(ve_go, 1)
                    for j in range(T):
                        ins = ve.bn_aggr(nmv[b][:, j, :], nbs[:, j, :])
                    ins.then_inc(S["r_done"], 1)
                    c.end()

                if l == 0:
                    agn(Trip(0, 0))
                    agn(Trip(0, 1))
                if l == 2:
                    counts(Trip(0, 0))
                    counts(Trip(0, 1))
                if l == 3:
                    before_gates(Trip(0, 0))

                def node_trip(tr):
                    if l == 0 and tr.has(2, NTRIPS):
                        agn(tr.shift(2))
                    if l == 3 and tr.has(1, NTRIPS):
                        before_gates(tr.shift(1))
                    update(tr)
                    if l == 2 and tr.has(2, NTRIPS):
                        counts(tr.shift(2))

                trips(ve, NTRIPS, node_trip, NBUF)


_INS = [
    "x", "src", "dst", "edge_attr_16", "edge_attr_4", "edge_attr_64", "edge_attr_8", "node_vec1",
    "L0_gnn_gamma_s", "L0_gnn_beta_s", "L0_gnn_gamma_v", "L0_gnn_Ws_src", "L0_gnn_Wv_src", "L0_gnn_Ws_dst",
    "L0_gnn_Wv_dst", "L0_gnn_W_rbf", "L0_gnn_W_alpha", "L0_gnn_alpha_dot", "L0_gnn_Ws_val", "L0_gnn_Wv_val",
    "L0_gnn_Wg", "L0_gnn_w2_ss", "L0_gnn_w2_sv", "L0_gnn_w2_vs", "L0_gnn_w2_vv0", "L0_gnn_w2_vv1",
    "L0_gnn_Ws_vlin", "L0_gnn_Wv_vlin", "L0_gnn_Wps", "L0_gnn_Wpv",
    "L1_gnn_W_sc_s", "L1_gnn_W_sc_v", "L1_gnn_W1_s", "L1_gnn_W1_v", "L1_gnn_W2_s", "L1_gnn_W2_v", "L1_gnn_W3",
    "L1_gnn_fcW1", "L1_gnn_fcW2",
    "L2_gnn_Wfc1", "L2_gnn_Wfc2", "L2_gnn_Wsc0", "L2_gnn_Wsc1", "L2_gnn_Wl1_0", "L2_gnn_Wl1_1", "L2_gnn_Wl2_s",
    "L2_gnn_Wl2_v", "L2_gnn_Wa",
    "L3_gnn_lin1_ws", "L3_gnn_lin1_wv", "L3_gnn_fc_w1", "L3_gnn_fc_w2", "L3_gnn_sc_ws", "L3_gnn_sc_wv",
    "L3_gnn_lin2_ws", "L3_gnn_lin2_wv",
]


def kernel(**inputs):
    import numpy as _np
    import concourse.bacc as _bacc
    from concourse import mybir as _mybir
    from concourse.bass_utils import run_bass_kernel_spmd as _run

    nc = _bacc.Bacc("TRN2", target_bir_lowering=False, num_devices=1)
    arrays, args = {}, {}
    for name in _INS:
        a = _np.ascontiguousarray(inputs[name])
        arrays[f"in_{name}"] = a
        args[name] = nc.dram_tensor(f"in_{name}", a.shape, _mybir.dt.from_np(a.dtype), kind="ExternalInput").ap()
    out = nc.dram_tensor("out_0", (N, F), _mybir.dt.float32, kind="ExternalOutput").ap()
    gnn_kernel(nc, args, out)
    r = _run(nc, [arrays], core_ids=[0])
    return r.results[0]["out_0"]
```

```python
from contextlib import ExitStack

import concourse.bass as bass
from concourse import mybir

N = 50000
E = 25000
CS, CV = 64, 32
F = CS + 3 * CV
H = 4
AS, AV = CS // H, CV // H
HC = AS + 3 * AV

EP = 125
ET = E // EP
T = 4
EC = T * EP
ETRIPS = ET // T
NP = 128
NG = T * NP
NTRIPS = -(-N // NG)
NFULL = N // NG
XW = F + 1
AW = 192
AROWS = 392 * 128
SKIP = 65536
BIG = 1.0e30
ATTR = F
OW = 288

C_VY, C_YV, C_YS, C_S, C_X = 0, 32, 128, 192, 256
EW = 352

LAYERS = [
    dict(rad=16, cross=True, msg=H * (HC + 1) + H),
    dict(rad=8, cross=False, msg=F + 1),
    dict(rad=16, cross=False, msg=F + 2),
    dict(rad=64, cross=True, msg=2 * 96),
]


PI, HALF_PI, INV_2PI = 3.1415925, 1.5707963267948966, 0.15915494309189535
TWO_PI = (6.28125, 1.9350051879882812e-03, 3.0199159819567000e-07)
MAGIC = 12582912.0


EBUF = 4
NBUF = 6
YBUF = 3


class Trip:

    def __init__(self, i, off, turn=2):
        self.i, self.off, self.turn, self.b = i, off, turn, off % 2
        self.q, self.m, self.y = off % EBUF, off % NBUF, off % YBUF
        self.g = off if isinstance(i, int) else None

    def shift(self, d):
        return Trip(self.i, self.off + d, self.turn)

    def every(self, m, per, c):
        c = (self.off // m) * per + c
        return c if self.g is not None else self.i * (self.turn // m * per) + c

    def lin(self, per, c):
        return self.every(1, per, c)

    def half(self, per, c):
        return self.every(2, per, c)

    def has(self, d, n):
        return self.g is None or 0 <= self.g + d < n


def trips(eng, n, body, turn=2, tail=2):
    last = (n - tail) // turn
    for g in range(turn):
        body(Trip(0, g, turn))
    with eng.Fori(1, last) as i:
        for off in range(turn):
            body(Trip(i, off, turn))
    for g in range(last * turn, n):
        body(Trip(0, g, turn))


PHASES = ["E0", "N0", "E1", "N1", "E2", "N2", "E3", "N3"]
RING_E = {0: 10, 1: 6, 2: 6, 3: 9}
CHUNKS = {0: 3, 1: 2, 2: 2, 3: 3}

PER = {}
for _l in range(4):
    PER[f"E{_l}"] = dict(pe_ring=RING_E[_l], act_ring=RING_E[_l], ob_full=4 if _l == 0 else 1,
                         ob_evac=4 if _l == 0 else 1, f_done=CHUNKS[_l], prod_done=CHUNKS[_l], e_done=1,
                         msg_done=1, xn_done=1, e2_done=1, d_ready=1, exp_done=1, tanh_done=1, sq_done=1,
                         stat_done=1, pow_done=1, gp=0, d_norm=0, d_in=0, d_post=0, d_fin=0)
    PER[f"N{_l}"] = dict(pe_ring=2, act_ring=2, ob_full=1, ob_used=1, r_done=1, rstd_done=1, y_done=1, a_done=1,
                         agn_done=int(_l == 0), ang_done=int(_l in (1, 2)), sin_done=int(_l == 1),
                         coef_done=int(_l == 1), co_done=int(_l in (1, 2)), ag_done=int(_l in (1, 2)),
                         t2_done=int(_l in (1, 2)), gate_in=int(_l == 3),
                         sig_done=int(_l == 3), gpn=3)
for _ph, _n in dict(E0=dict(gp=1, d_norm=1, d_in=2, d_post=13, d_fin=10), E1=dict(d_in=2, d_post=5),
                    E2=dict(d_in=2, d_post=5), E3=dict(d_in=2, d_post=5),
                    N0=dict(d_norm=2, dve=1, gp=0), N1=dict(dve=2, gp=0, d_norm=7), N2=dict(dve=2, gp=2, d_norm=1),
                    N3=dict(dve=3, gp=0, d_norm=0)).items():
    PER[_ph].update(_n)
PER2 = {}
for _l in range(4):
    PER2[f"E{_l}"] = dict(gath=16 * T * (2 if _l == 0 else 1), idx=16 * (2 if _l == 0 else 1), ldr=16, scid=16,
                          scat=16 * T)
    PER2[f"N{_l}"] = {}
AHEAD = {0: 2, 1: 2, 2: 2, 3: 2}
PERX = {l: 32 if l == 0 else 16 for l in range(4)}
PERA = {l: 16 for l in range(4)}
PERY = {l: 16 for l in range(4)}


PERYK = {l: 32 for l in range(4)}


def buf_dma(l, tr, per, q, nbuf, n):
    return tr.every(nbuf, per[l], sum(per[k] for k in range(l)) * len(range(q, n, nbuf)) + per[l])


def node_dma(l, tr, per):
    return buf_dma(l, tr, per, tr.m, NBUF, NTRIPS)


def row_dma(l, tr):
    return buf_dma(l, tr, PERY, tr.m, NBUF, NTRIPS)


def row_dma_total(l, q):
    return sum(PERY[k] for k in range(l + 1)) * len(range(q, NTRIPS, NBUF))


def edge_dma(l, tr):
    return buf_dma(l, tr, PERYK, tr.q, EBUF, ETRIPS)


def bases(per, ntrips):
    out, at = {}, {}
    for ph in PHASES:
        out[ph] = dict(at)
        for k, v in per[ph].items():
            at[k] = at.get(k, 0) + v * ntrips(ph)
    return out


BASE = bases(PER, lambda ph: ETRIPS if ph[0] == "E" else NTRIPS)
BASE2 = bases(PER2, lambda ph: (ETRIPS if ph[0] == "E" else NTRIPS) // 2)


def cnt(ph, sem, tr, k=1):
    return tr.lin(PER[ph][sem], BASE[ph].get(sem, 0) + k)


def cnt2(ph, sem, tr):
    per = PER2[ph][sem]
    return tr.half(per, BASE2[ph].get(sem, 0) + per)


def total(ph, sem):
    return BASE[ph].get(sem, 0) + PER[ph][sem] * (ETRIPS if ph[0] == "E" else NTRIPS)


def total2(ph, sem):
    return BASE2[ph].get(sem, 0) + PER2[ph][sem] * ((ETRIPS if ph[0] == "E" else NTRIPS) // 2)


class Chain:

    def __init__(self, eng, sems, ph, name, tr, held=None):
        self.eng, self.sem, self.ph, self.name, self.tr, self.n = eng, sems[name], ph, name, tr, 0
        self.held = held

    def step(self, ins):
        self.n += 1
        ins.then_inc(self.sem, 1)
        self.eng.wait_ge(self.sem, cnt(self.ph, self.name, self.tr, self.n))
        if self.held is not None:
            self.eng.sem_inc(self.held, 1)

    def end(self):
        assert self.n == PER[self.ph][self.name], (self.ph, self.name, self.n)


class Chain0:

    def __init__(self, eng, sem, at):
        self.eng, self.sem, self.at = eng, sem, at

    def step(self, ins):
        self.at += 1
        ins.then_inc(self.sem, 1)
        self.eng.wait_ge(self.sem, self.at)


def ring_banks(l):
    return 3 if RING_E[l] % 3 == 0 else 2


def ring_step(l, tr, what):
    k, n = int(what[1:] or 0), CHUNKS[l]
    if l == 0:
        lead = 7
        if what[0] == "t":
            return 0, lead + (0 if tr.g == ETRIPS - 1 else 7) + k
        if tr.g == 0:
            return None, {"n": 0, "e": 3, "w": 4}[what[0]] + k
        return -1, lead + {"e": 0, "n": 1, "w": 4}[what[0]] + k
    eh = 3 if l == 3 else 2
    lead = 2 * eh + n
    if what[0] == "t":
        return 0, lead + k
    if what[0] == "w":
        if tr.g == 0:
            return None, eh + k
        return -1, lead + n + k
    k = {"e": 0, "h": eh - 1}[what[0]]
    if tr.g in (0, 1):
        return None, k + (eh + n if tr.g == 1 else 0)
    return -2, lead + 2 * n + k


def ring_gone(l, tr, what):
    return (3 if l == 3 else 2) if l and what[0] == "t" and tr.g == ETRIPS - 1 else 0


def ring_val(ph, l, tr, what):
    d, k = ring_step(l, tr, what)
    if d is None:
        return BASE[ph].get("pe_ring", 0) + k + 1
    return cnt(ph, "pe_ring", tr.shift(d), k + 1 - ring_gone(l, tr, what))


def ring_pos(l, tr, what):
    d, k = ring_step(l, tr, what)
    return k if d is None else (tr.off + d) * RING_E[l] + k - ring_gone(l, tr, what)


def ring_inc(l, what):
    return 2 if l == 3 and what == "h" else 1


def ob_val(ph, tr, what):
    if what == "M":
        return 1 if tr.g == 0 else cnt(ph, "ob_full", tr.shift(-1), 4)
    if what == "O2":
        return cnt(ph, "ob_full", tr, 4 if tr.g == ETRIPS - 1 else 5)
    return cnt(ph, "ob_full", tr, 2 + int(what[1]))


FIX_STEPS = [5, 6, 7, 8]
GRAPH_STEPS = 34
FIRST_STEPS = GRAPH_STEPS + 7
SETUP_STEPS = 73


def wait(eng, sem, value):
    if isinstance(value, int) and value <= 0:
        return
    eng.wait_ge(sem, value)


def gnn_kernel(nc, A, out):
    f32, i32 = mybir.dt.float32, mybir.dt.int32
    ALU, ACT, AX = mybir.AluOpType, mybir.ActivationFunctionType, mybir.AxisListType

    ctx = ExitStack()
    with ctx:
        def sb(name, shape, dt=f32):
            return ctx.enter_context(nc.sbuf_tensor(name, shape, dt))

        def pair(name, shape, dt=f32):
            return [sb(f"{name}{b}", shape, dt) for b in range(2)]

        def sem(name):
            return ctx.enter_context(nc.semaphore(name))

        tabA = nc.dram_tensor("tab_a", (N, XW), f32).ap()
        tabB = nc.dram_tensor("tab_b", (N, XW), f32).ap()
        agg = nc.dram_tensor("agg", (AROWS, AW), f32).ap()
        runs_d = nc.dram_tensor("runs", (EP, ET, 3), f32).ap()
        scix_d = nc.dram_tensor("scatter_ids", (EP, ET), i32).ap()
        TABLE = [A["x"], tabA, tabB, tabA]
        NEXT = [tabA, tabB, tabA, out]
        ES = [A["edge_attr_16"], A["edge_attr_8"], A["edge_attr_16"], A["edge_attr_64"]]

        ident = sb("ident", [128, 128])
        ones_k = sb("ones_k", [EP, EP])
        zeros = sb("zeros", [128, 1, 784])
        dst_i = sb("dst_i", [EP, ET], i32)
        dst_f = sb("dst_f", [EP, ET])
        runs = sb("runs_sb", [EP, ET, 3])
        wk_one = sb("wk_one", [EP, ET])
        wk1 = sb("wk1", [EP, ET])
        wk2 = sb("wk2", [EP, ET])
        scix = sb("scix", [EP, ET], i32)
        edge_i = sb("edge_i", [EP, 3], i32)
        edge_f = sb("edge_f", [EP, 3])
        pid = sb("pid", [EP, 1], i32)
        cf = sb("cf", [EP, 8])
        head_i = sb("head_i", [EP, 1], i32)
        fixid = sb("fixid", [EP, 1], i32)
        hrow_i = sb("hrow_i", [EP, EP], i32)
        hrow = sb("hrow", [EP, EP])
        same = sb("same", [EP, EP])
        samen = sb("samen", [EP, EP])

        fc1 = {l: sb(f"fc1_{l}", [LAYERS[l]["rad"], CS]) for l in (1, 2, 3)}
        fc2 = {l: sb(f"fc2_{l}", [16 if l == 0 else CS, EW]) for l in range(4)}
        wf1 = {l: sb(f"wf1_{l}", [128, 128]) for l in (1, 2, 3)}
        wf2 = {l: sb(f"wf2_{l}", [128, 128]) for l in (1, 2, 3)}
        EOW = {0: 288, 1: 193, 2: 193, 3: 224}
        ra = {l: sb(f"ra_{l}", [128, EOW[l] - 96]) for l in range(4)}
        rb = {l: sb(f"rb_{l}", [128, EOW[l]]) for l in range(4)}
        rx = {l: sb(f"rx_{l}", [96, 96]) for l in (0, 3)}
        NOW = {0: 160, 1: 160, 2: 160, 3: 192}
        nw1 = {l: sb(f"nw1_{l}", [96, 96]) for l in range(4)}
        nw2 = {l: sb(f"nw2_{l}", [CS, NOW[l] - 96]) for l in range(4)}
        wm = [sb("wm_vs", [96, 96]), sb("wm_vd", [96, 96]), sb("wm_s", [2 * CS, CS])]
        gv = sb("gamma_v3", [96, 1])
        gs = sb("gamma_s2", [2 * CS, 1])
        bs = sb("beta_s2", [2 * CS, 1])
        wval = sb("wval", [96, CS])
        wg = sb("wg", [CS, CV])
        wvt = sb("wvt", [CS, 96 + 128])
        adot = sb("adot", [EP, CS])
        r2a = sb("r2a", [128, H * 48])
        r2b = sb("r2b", [128, H * 48])
        r2x = sb("r2x", [96, H * 48])
        cA = sb("cA", [128, 1])
        cB = sb("cB", [128, 1])
        cX = sb("cX", [96, 1])

        gidx = pair("gidx", [EP, T], i32)
        gidx2 = pair("gidx2", [EP, T], i32)
        scid = pair("scid", [EP, T], i32)
        es_in = pair("es_in", [EP, T * 64])
        y_in = [sb(f"y_in{q}", [EP, T, 4]) for q in range(EBUF)]
        kc = [sb(f"kc{q}", [EP, T, 3]) for q in range(EBUF)]
        yc = [sb(f"yc{q}", [EP, T, 6]) for q in range(EBUF)]
        G = pair("G", [EP, T, XW])
        Y = [sb(f"Y{y}", [NP, T, XW]) for y in range(3)]
        GS = [Y[0][0:EP, :, 0:F], Y[1][0:EP, :, 0:F]]
        GD = [Y[2][0:EP, :, 0:F], sb("GD1", [EP, T, F])[:, :, :]]
        XN = sb("XN", [EP, T, 2 * F])
        sqv = sb("sqv", [EP, 2 * T, 96])
        bst = sb("bst", [EP, 2 * T, 6])
        lst = sb("lst", [EP, 2 * T, 3])
        lrs = sb("lrs", [EP, 2 * T, 2])
        mhalf = sb("mhalf", [128, 4 * T])
        MG = sb("MG", [EP, T, F])
        EE = sb("EE", [EP, T, EW])
        E2_ = sb("E2", [NP, T, EW])
        E2 = E2_[0:EP, :, :]
        EEs = [EE, E2]
        tmp = sb("tmp", [EP, T, 96])
        tmp2 = sb("tmp2", [EP, T, 96])
        tmp3 = sb("tmp3", [EP, T, 96])
        esT = sb("esT", [64, EC])
        hidT = sb("hidT", [64, EC])
        ET_ = [sb(f"ET{c}", [128, EC]) for c in range(3)]
        PR = [sb(f"PR{c}", [128, EC]) for c in range(3)]
        O_ = pair("O", [NP, T, OW])
        O = [o[0:EP, :, :] for o in O_]
        Y += [t[:, :, 0:XW] for t in (E2_, O_[0], O_[1])]
        MG2 = sb("MG2", [EP, T, F])
        O2 = sb("O2", [EP, T * H, 49])
        SG2 = sb("SG2", [EP, T, CV])
        SG = sb("SG", [EP, T, 96])
        LK = sb("LK", [EP, T, CS])
        al = sb("al", [EP, T * H])
        mx = pair("mx", [EP, T * H])
        dd = sb("dd", [EP, 2, T * H])
        pc = sb("pc", [EP, 2, T * H])
        MS = sb("MS", [EP, T * H, HC + 1])
        OUT = pair("OUT", [EP, T, AW])
        FX = sb("FX", [EP, AW])
        FB = sb("FB", [EP, AW])
        FN = sb("FN", [EP, AW])
        fm = sb("fm", [EP, 4, H])
        fdg = sb("fdg", [EP, H * EP])

        X = [sb(f"X{q}", [NP, T, XW]) for q in range(NBUF)]
        AG = [sb(f"AG{q}", [NP, T, AW]) for q in range(NBUF)]
        XA = [sb(f"XA{q}", [NP, T]) for q in range(NBUF)]
        AGN = pair("AGN", [NP, T, F])
        rden = pair("rden", [NP, T * H])
        WT = [sb(f"WT{k}", [128, NG]) for k in range(6)]
        NT1, NT2 = [WT[0], WT[1]], [WT[2], WT[3]]
        wT = [WT[0:3], WT[3:6]]
        R = [sb(f"R{q}", [NP, T, F]) for q in range(YBUF)]
        T2B = AGN
        R3 = pair("R3", [NP, T, 192])
        SGN = pair("SGN", [NP, T, 96])
        nbs = sb("nbs", [NP, T, 6])
        nmv = pair("nmv", [NP, T, 2])
        nrs = [sb(f"nrs{q}", [NP, T, 2]) for q in range(YBUF)]
        ang = sb("ang", [NP, 2 * T])
        angk = sb("angk", [NP, 2 * T])
        angr = pair("angr", [NP, 2 * T])
        sc8 = pair("sc8", [NP, 2 * T])
        co = pair("co", [NP, 2 * T])

        ps = ctx.enter_context(nc.psum_tensor("ps", [128, 8, 512], f32))
        psR, psF, psO = ps[:, 0:3, :], ps[:, 3:6, :], ps[:, 6:8, :]
        NPO = [ps[:, 6:8, :], ps[:, 4:6, :]]

        S = {n: sem(n) for n in (
            "pe_ring", "act_ring", "ob_full", "ob_evac", "ob_used", "f_done", "prod_done", "e_done", "msg_done",
            "xn_done", "e2_done", "d_ready", "exp_done", "tanh_done", "sq_done", "stat_done", "pow_done",
            "r_done", "rstd_done", "y_done", "agn_done", "ang_done", "sin_done", "t2_done", "coef_done", "co_done",
            "ag_done",
            "gate_in", "sig_done", "a_done", "dve", "gp", "gpn", "d_norm", "d_in", "d_post",
            "d_fin")}
        S2 = {n: [sem(f"{n}0"), sem(f"{n}1")] for n in ("gath", "idx", "ldr", "scid", "scat")}
        S4 = {n: [sem(f"{n}{q}") for q in range(k)]
              for n, k in (("nldx", NBUF), ("nlda", NBUF), ("nst", NBUF), ("ldy", EBUF))}
        w_zero = sem("w_zero")
        w_load = sem("w_load")
        w_late = sem("w_late")
        w_dve = sem("w_dve")
        w_pe = sem("w_pe")
        w_act = sem("w_act")
        g_load = sem("g_load")
        g_store = sem("g_store")
        z_store = sem("z_store")
        go = sem("go")
        sp_go = sem("sp_go")
        pe_go = sem("pe_go")
        ve_go = sem("ve_go")
        fx_rd = sem("fx_rd")
        fx_g = sem("fx_g")
        fx_mm = sem("fx_mm")
        fx_dve = sem("fx_dve")
        fx_act = sem("fx_act")
        fx_st = sem("fx_st")

        loads, later = [], []
        late_tiles = [t[l] for t in (fc1, fc2, wf1, wf2, ra, rb, rx, nw1, nw2) for l in (1, 2, 3) if l in t]

        def put(tile, r, c, src):
            to = later if any(tile is t for t in late_tiles) else loads
            to.append((tile[r:r + src.shape[0], c:c + src.shape[1]], src))

        def col(tile, r, src):
            loads.append((tile[r:r + src.shape[0], 0:1], src.rearrange("(a b) -> a b", b=1)))

        L0 = {k[7:]: v for k, v in A.items() if k.startswith("L0_gnn_")}
        L1 = {k[7:]: v for k, v in A.items() if k.startswith("L1_gnn_")}
        L2 = {k[7:]: v for k, v in A.items() if k.startswith("L2_gnn_")}
        L3 = {k[7:]: v for k, v in A.items() if k.startswith("L3_gnn_")}
        for l, w in ((0, L0["W_rbf"]), (1, L1["fcW2"]), (2, L2["Wfc2"]), (3, L3["fc_w2"])):
            put(fc2[l], 0, 0, w[:, 160:192])
            for d in range(3):
                put(fc2[l], 0, 32 + 32 * d, w[:, 128:160])
                if LAYERS[l]["cross"]:
                    put(fc2[l], 0, 256 + 32 * d, w[:, 192:224])
            put(fc2[l], 0, 128, w[:, 0:128])
        for l, w in ((1, L1["fcW1"]), (2, L2["Wfc1"]), (3, L3["fc_w1"])):
            put(fc1[l], 0, 0, w)
        for l, ws, wv in ((1, L1["W1_s"], L1["W1_v"]), (2, L2["Wl1_0"], L2["Wl1_1"]),
                          (3, L3["lin1_ws"], L3["lin1_wv"])):
            for d in range(2):
                put(wf1[l], 64 * d, 64 * d, ws)
            for d in range(4):
                put(wf2[l], 32 * d, 32 * d, wv)
        for l, ws, wv, w1 in ((1, L1["W2_s"], L1["W2_v"], L1["W3"]), (2, L2["Wl2_s"], L2["Wl2_v"], L2["Wa"]),
                              (3, L3["lin2_ws"], L3["lin2_wv"], None), (0, L0["W_alpha"], L0["Wv_val"], None)):
            put(ra[l], 0, 0, ws[0:64])
            put(rb[l], 0, 96, ws[64:96])
            if w1 is not None:
                put(ra[l], 0, 64, w1[0:64])
                put(rb[l], 0, 160, w1[64:96])
            put(ra[l], 64, EOW[l] - 128, wv[0:64])
            for d in range(3):
                put(rb[l], 32 + 32 * d, 32 * d, wv[64:96])
                if l in rx:
                    put(rx[l], 32 * d, 32 * d, wv[96:128])
        put(ra[0], 0, 64, L0["Ws_val"][0:64])
        put(rb[0], 0, 160, L0["Ws_val"][64:96])
        put(wval, 0, 0, L0["Ws_val"])
        put(wg, 0, 0, L0["Wg"])
        for k, ws, wv in ((0, L0["Ws_src"], L0["Wv_src"]), (1, L0["Ws_dst"], L0["Wv_dst"])):
            for d in range(3):
                put(wm[k], 32 * d, 32 * d, wv)
            put(wm[2], CS * k, 0, ws)
            col(gs, CS * k, L0["gamma_s"])
            col(bs, CS * k, L0["beta_s"])
        for d in range(3):
            col(gv, 32 * d, L0["gamma_v"])
        loads.append((adot[:, :], L0["alpha_dot"].rearrange("a h s -> a (h s)").broadcast_to((EP, CS))))
        for h in range(H):
            put(r2a, 0, 48 * h + 8, L0["Ws_vlin"][0:64, AS * h:AS * h + AS])
            put(r2b, 0, 48 * h + 8, L0["Ws_vlin"][64:96, AS * h:AS * h + AS])
            put(r2a, 64, 48 * h, L0["Wv_vlin"][0:64, AV * h:AV * h + AV])
            for d in range(3):
                put(r2b, 32 + 32 * d, 48 * h + 24 + 8 * d, L0["Wv_vlin"][64:96, AV * h:AV * h + AV])
                put(r2x, 32 * d, 48 * h + 24 + 8 * d, L0["Wv_vlin"][96:128, AV * h:AV * h + AV])
        col(cA, 0, L0["w2_ss"])
        col(cA, 64, L0["w2_sv"])
        col(cB, 0, L0["w2_vv0"])
        for d in range(3):
            col(cB, 32 + 32 * d, L0["w2_vs"])
            col(cX, 32 * d, L0["w2_vv1"])
        for l, ws, wv in ((0, L0["Wps"], L0["Wpv"]), (1, L1["W_sc_s"], L1["W_sc_v"]), (2, L2["Wsc0"], L2["Wsc1"]),
                          (3, L3["sc_ws"], L3["sc_wv"])):
            for d in range(3):
                put(nw1[l], 32 * d, 32 * d, wv)
            put(nw2[l], 0, 0, ws)

        cleared = ([fc2[l] for l in range(4)] + [wf1[l] for l in (1, 2, 3)] + [wf2[l] for l in (1, 2, 3)]
                   + [t[l] for t in (ra, rb, nw1) for l in range(4)] + [rx[0], rx[3]]
                   + [wm[0], wm[1], r2a, r2b, r2x, wvt])

        r3, r2 = 3.0 ** -0.5, 2.0 ** -0.5
        s64, s32, s96, s128 = 64 ** -0.5, 32 ** -0.5, 96 ** -0.5, 128 ** -0.5
        c1, c2, c3 = 10 ** -0.5 * s96, s96, 0.25 * s96
        scales = [(fc1[1][:, :], 8 ** -0.5), (fc1[2][:, :], 0.25), (fc1[3][:, :], 0.125)]
        for l in (1, 2, 3):
            scales += [(fc2[l][:, 0:(352 if l == 3 else 256)], s64), (wf1[l][:, :], s64), (wf2[l][:, :], s32)]
        scales += [(ra[1][:, 0:64], c1), (ra[1][:, 64:65], 0.1 * c1), (ra[1][:, 65:97], c1),
                   (rb[1][0:32, 96:160], c1 * r3), (rb[1][0:32, 160:161], 0.1 * c1 * r3), (rb[1][:, 0:96], c1),
                   (ra[2][:, :], c2), (rb[2][0:32, 96:161], c2 * r3), (rb[2][:, 0:96], c2),
                   (ra[3][:, 0:96], c3), (ra[3][:, 96:128], 0.25 * s128),
                   (rb[3][0:32, 96:192], c3 * r3), (rb[3][:, 0:96], 0.25 * s128), (rx[3][:, :], 0.25 * s128 * r2)]
        for l in (1, 2, 3):
            scales += [(nw1[l][:, :], s32), (nw2[l][:, :], s64)]

        N_CLEAR = len(cleared)
        N_LOAD = 16 * len(loads)
        PART = -(-len(later) // EBUF)

        def tab_rows(tab, tr, width):
            if tr.g is not None and tr.g == NTRIPS - 1:
                return tab[N - NG:N, :].rearrange("(p j) f -> p j f", j=T)[:, :, 0:width]
            v = tab[0:NFULL * NG, :].rearrange("(g p j) f -> g p j f", p=NP, j=T)
            return v[tr.lin(1, 0)][:, :, 0:width]

        block = ctx.enter_context(nc.Block())

        @block.sync
        def _(sp):
            sp.dma_start(dst_i[:, :], A["dst"].rearrange("(p t) -> p t", t=ET)).then_inc(g_load, 16)
            sp.dma_start(hrow_i[:, :], A["dst"].rearrange("(a p t) -> t a p", a=1, t=ET)[0]
                         .broadcast_to((EP, EP)), allow_slow_non_contiguous=True).then_inc(g_load, 16)
            dcol = A["dst"].rearrange("(p t) -> p t", t=ET)
            sp.wait_ge(w_zero, 1)
            sp.dma_start(edge_i[1:EP, 0:1], dcol[0:EP - 1, 0:1],
                         allow_slow_non_contiguous=True).then_inc(g_load, 16)
            sp.dma_start(edge_i[1:EP, 1:2], dcol[0:EP - 1, ET - 1:ET],
                         allow_slow_non_contiguous=True).then_inc(g_load, 16)
            sp.dma_start(edge_i[2:EP, 2:3], dcol[0:EP - 2, ET - 1:ET],
                         allow_slow_non_contiguous=True).then_inc(g_load, 16)
            sp.wait_ge(w_zero, 1 + N_CLEAR)
            for dst, src in loads:
                sp.dma_start(dst, src, allow_slow_non_contiguous=True).then_inc(w_load, 16)
            sp.wait_ge(w_dve, GRAPH_STEPS)
            sp.dma_start(runs_d[:, :, :], runs[:, :, :]).then_inc(g_store, 16)
            sp.dma_start(scix_d[:, :], scix[:, :]).then_inc(g_store, 16)
            sp.wait_ge(g_store, 32)

            for l in range(4):
                ph, rad = f"E{l}", LAYERS[l]["rad"]
                es_v = ES[l].rearrange("(p g t) k -> g p (t k)", p=EP, t=T)
                y_v = A["edge_attr_4"].rearrange("(p g t) k -> g p t k", p=EP, t=T)
                k_v = runs_d.rearrange("p (g t) k -> g p t k", t=T)
                s_v = A["src"].rearrange("(p g t) -> g p t", p=EP, t=T)
                d_v = A["dst"].rearrange("(p g t) -> g p t", p=EP, t=T)
                sc_v = scix_d.rearrange("p (g t) -> g p t", t=T)

                def load_idx(tr):
                    sp.dma_start(gidx[tr.b][:, :], s_v[tr.lin(1, 0)]).then_inc(S2["idx"][tr.b], 16)
                    if l == 0:
                        sp.dma_start(gidx2[tr.b][:, :], d_v[tr.lin(1, 0)]).then_inc(S2["idx"][tr.b], 16)

                def next_idx(tr):
                    wait(sp, S2["gath"][tr.b], cnt2(ph, "gath", tr.shift(-2)))
                    sp.sem_inc(sp_go, 1)
                    load_idx(tr)

                def load_radial(tr):
                    sp.dma_start(es_in[tr.b][:, 0:T * rad], es_v[tr.lin(1, 0)]).then_inc(S2["ldr"][tr.b], 16)

                def load_attrs(tr):
                    q = tr.q
                    sp.dma_start(y_in[q][:, :, :], y_v[tr.lin(1, 0)]).then_inc(S4["ldy"][q], 16)
                    sp.dma_start(kc[q][:, :, :], k_v[tr.lin(1, 0)]).then_inc(S4["ldy"][q], 16)

                for g in range(2):
                    load_idx(Trip(0, g))
                    load_radial(Trip(0, g))
                    load_attrs(Trip(0, g))
                if l == 0:
                    sp.wait_ge(w_load, N_LOAD)
                    az = agg.rearrange("(p i) f -> p (i f)", p=128).rearrange("p (i k f) -> i p k f", k=4, f=784)
                    for i in range(24):
                        sp.dma_start(az[i], zeros[:, :, :].broadcast_to((128, 4, 784))).then_inc(z_store, 16)
                next_idx(Trip(0, 2))
                sp.wait_ge(S["pe_ring"], ring_val(ph, l, Trip(0, 0), "e"))
                load_radial(Trip(0, 2))

                def edge_trip(tr):
                    if tr.has(3, ETRIPS):
                        next_idx(tr.shift(3))
                    if tr.has(2, ETRIPS):
                        if tr.has(-2, ETRIPS):
                            wait(sp, S["msg_done"], cnt(ph, "msg_done", tr.shift(-2)))
                            sp.sem_inc(sp_go, 1)
                        load_attrs(tr.shift(2))
                    if tr.has(-2, ETRIPS):
                        wait(sp, S2["scat"][tr.b], cnt2(ph, "scat", tr.shift(-2)))
                        sp.sem_inc(sp_go, 1)
                    sp.dma_start(scid[tr.b][:, :], sc_v[tr.lin(1, 0)]).then_inc(S2["scid"][tr.b], 16)
                    if tr.has(3, ETRIPS):
                        wait(sp, S["pe_ring"], ring_val(ph, l, tr.shift(1), "e"))
                        sp.sem_inc(sp_go, 1)
                        load_radial(tr.shift(3))

                def edge_trip_0(tr):
                    edge_trip(tr)
                    if tr.g is not None and tr.g < EBUF:
                        for dst, src in later[PART * tr.g:PART * (tr.g + 1)]:
                            sp.dma_start(dst, src, allow_slow_non_contiguous=True).then_inc(w_late, 16)

                trips(sp, ETRIPS, edge_trip if l else edge_trip_0, EBUF, 3)

                for b in range(2):
                    sp.wait_ge(S2["scat"][b], total2(ph, "scat"))
                sp.dma_start(FX[:, :], agg[N:N + EP, :]).then_inc(fx_rd, 16)
                sp.wait_ge(fx_st, 16 * (l + 1))

                ph = f"N{l}"
                aw = H * (HC + 1) if l == 0 else LAYERS[l]["msg"]
                xw = F if l == 0 else XW

                def load_nodes(tr):
                    q = tr.m
                    if tr.has(-NBUF, NTRIPS):
                        wait(sp, S["r_done"], cnt(ph, "r_done", tr.shift(-NBUF)))
                        wait(sp, S["a_done"], cnt(ph, "a_done", tr.shift(-NBUF)))
                        sp.sem_inc(sp_go, 1)
                    sp.dma_start(AG[q][:, :, 0:aw], tab_rows(agg[0:N, :], tr, aw)).then_inc(S4["nlda"][q], 16)
                    sp.dma_start(X[q][:, :, 0:xw], tab_rows(TABLE[l], tr, xw)).then_inc(S4["nldx"][q], 16)
                    if l == 0:
                        sp.dma_start(XA[q][:, :], tab_rows(A["node_vec1"], tr, 1)
                                     .rearrange("p j f -> p (j f)")).then_inc(S4["nldx"][q], 16)

                def store_nodes(tr):
                    q = tr.m
                    wait(sp, S["y_done"], cnt(ph, "y_done", tr))
                    sp.sem_inc(sp_go, 1)
                    if tr.g == NTRIPS - 1:
                        before = tr.shift(-1)
                        wait(sp, S4["nst"][before.m], row_dma(l, before))
                        sp.sem_inc(sp_go, 1)
                    sp.dma_start(tab_rows(NEXT[l], tr, XW if l < 3 else F),
                                 Y[q][:, :, 0:XW if l < 3 else F]).then_inc(S4["nst"][q], 16)

                for g in range(NBUF - 1):
                    load_nodes(Trip(0, g))

                def node_trip(tr):
                    if tr.has(NBUF - 1, NTRIPS):
                        load_nodes(tr.shift(NBUF - 1))
                    if tr.has(-3, NTRIPS):
                        store_nodes(tr.shift(-3))

                trips(sp, NTRIPS, node_trip, NBUF, NBUF - 1)
                for g in range(NTRIPS - 3, NTRIPS):
                    store_nodes(Trip(0, g))

            for q in range(NBUF):
                sp.wait_ge(S4["nst"][q], row_dma_total(3, q))

        @block.gpsimd
        def _(gp):
            gp.memset(edge_i[:, :], -1).then_inc(w_zero, 1)
            for t in cleared:
                gp.memset(t[:, :], 0.0).then_inc(w_zero, 1)
            gp.memset(zeros[:, :, :], 0.0).then_inc(w_zero, 1)
            gp.memset(ident[:, :], 0.0).then_inc(w_zero, 1)
            gp.memset(ones_k[:, :], 1.0).then_inc(w_zero, 1)
            gp.memset(mhalf[:, :], -0.5).then_inc(w_zero, 1)
            gp.iota(pid[:, :], [[0, 1]], base=N, channel_multiplier=1).then_inc(w_zero, 1)
            gp.memset(O2[:, :, 48], 1.0).then_inc(w_zero, 1)
            gp.memset(wk_one[:, :], 1.0).then_inc(w_zero, 1)
            for b in range(2):
                gp.memset(OUT[b][:, :, :], 0.0).then_inc(w_zero, 1)
                gp.memset(mx[b][:, :], 0.0).then_inc(w_zero, 1)
            gp.wait_ge(w_zero, N_CLEAR + 12)
            gp.affine_select(out=ident[:, :], in_=ident[:, :], compare_op=ALU.not_equal, fill=1.0, base=0,
                             pattern=[[-1, 128]], channel_multiplier=1).then_inc(w_zero, 1)
            for l in range(4):
                ph = f"E{l}"
                if l:
                    for q in range(NBUF):
                        gp.wait_ge(S4["nst"][q], row_dma_total(l - 1, q))

                def rows(dst, j, ids):
                    return gp.indirect_dma_start(dst[:, j, :], None, TABLE[l][:, :],
                                                 bass.IndirectOffsetOnAxis(ap=ids[:, j:j + 1], axis=0))

                def gathers(tr):
                    b = tr.b
                    wait(gp, S2["idx"][b], cnt2(ph, "idx", tr))
                    gp.sem_inc(go, 1)
                    if tr.has(-2, ETRIPS):
                        s = "xn_done" if l == 0 else "e_done"
                        wait(gp, S[s], cnt(ph, s, tr.shift(-2)))
                        gp.sem_inc(go, 1)
                    for j in range(T):
                        if l == 0:
                            rows(GS[b], j, gidx[b]).then_inc(S2["gath"][b], 16)
                            rows(GD[b], j, gidx2[b]).then_inc(S2["gath"][b], 16)
                        else:
                            rows(G[b], j, gidx[b]).then_inc(S2["gath"][b], 16)

                def scatters(tr):
                    b = tr.b
                    wait(gp, S2["scid"][b], cnt2(ph, "scid", tr))
                    gp.sem_inc(go, 1)
                    wait(gp, S["msg_done"], cnt(ph, "msg_done", tr))
                    gp.sem_inc(go, 1)
                    if tr.g == 0 and l == 0:
                        gp.wait_ge(z_store, 16 * 24)
                        gp.sem_inc(go, 1)
                    for j in range(T):
                        gp.indirect_dma_start(agg[:, :], bass.IndirectOffsetOnAxis(ap=scid[b][:, j:j + 1], axis=0),
                                              OUT[b][:, j, :], None, bounds_check=AROWS - 1, oob_is_err=False)\
                          .then_inc(S2["scat"][b], 16)

                def inv_norms(tr):
                    gp.wait_ge(S["stat_done"], cnt(ph, "stat_done", tr))
                    gp.sem_inc(go, 1)
                    c = Chain(gp, S, ph, "gp", tr, go)
                    c.step(gp.tensor_scalar(lrs[:, :, :], lst[:, :, 1:3], 1e-5, None, ALU.add))
                    gp.tensor_tensor(lrs[:, :, :].rearrange("p a b -> p (a b)"),
                                     lrs[:, :, :].rearrange("p a b -> p (a b)"),
                                     mhalf[0:EP, 0:4 * T], ALU.pow).then_inc(S["pow_done"], 1)
                    c.end()

                ahead = 3 if l else 2
                for g in range(ahead):
                    gathers(Trip(0, g))
                if l == 0:
                    inv_norms(Trip(0, 0))

                def edge_trip(tr):
                    if l == 0 and tr.has(1, ETRIPS):
                        inv_norms(tr.shift(1))
                    if tr.has(ahead, ETRIPS):
                        gathers(tr.shift(ahead))
                    if tr.has(-1, ETRIPS):
                        scatters(tr.shift(-1))

                trips(gp, ETRIPS, edge_trip, EBUF, 3)
                scatters(Trip(0, ETRIPS - 1))

                for b in range(2):
                    gp.wait_ge(S2["scat"][b], total2(ph, "scat"))
                gp.indirect_dma_start(FB[:, :], None, agg[:, :],
                                      bass.IndirectOffsetOnAxis(ap=head_i[:, 0:1], axis=0)).then_inc(fx_g, 16)
                gp.wait_ge(fx_dve, FIX_STEPS[l])
                gp.indirect_dma_start(agg[:, :], bass.IndirectOffsetOnAxis(ap=fixid[:, 0:1], axis=0),
                                      FN[:, :], None, bounds_check=AROWS - 1, oob_is_err=False).then_inc(fx_st, 16)

                ph = f"N{l}"

                def node_rstd(tr):
                    b, y = tr.b, tr.y
                    gp.wait_ge(S["r_done"], cnt(ph, "r_done", tr))
                    if tr.has(-YBUF, NTRIPS):
                        wait(gp, S["y_done"], cnt(ph, "y_done", tr.shift(-YBUF)))
                    gp.sem_inc(go, 1)
                    c = Chain(gp, S, ph, "gpn", tr, go)
                    c.step(gp.tensor_scalar(nrs[y][:, :, 0], nmv[b][:, :, 1], 1e-5, None, ALU.add))
                    c.step(gp.tensor_tensor(nrs[y][:, :, 0], nrs[y][:, :, 0], mhalf[:, 0:T], ALU.pow))
                    c.step(gp.tensor_scalar(nrs[y][:, :, 1], nmv[b][:, :, 0], -1.0, None, ALU.mult))
                    gp.tensor_tensor(nrs[y][:, :, 1], nrs[y][:, :, 1], nrs[y][:, :, 0], ALU.mult)\
                      .then_inc(S["rstd_done"], 1)
                    c.end()

                def attr_out(tr):
                    q = tr.m
                    gp.wait_ge(S4["nldx"][q], node_dma(l, tr, PERX))
                    if tr.has(-NBUF, NTRIPS):
                        wait(gp, S4["nst"][q], row_dma(l, tr.shift(-NBUF)))
                    gp.sem_inc(go, 1)
                    src = XA[q][:, :] if l == 0 else X[q][:, :, ATTR]
                    gp.tensor_copy(Y[q][:, :, ATTR], src).then_inc(S["a_done"], 1)

                def times_attr(tr):
                    b, q = tr.b, tr.m
                    gp.wait_ge(S4["nldx"][q], node_dma(l, tr, PERX))
                    gp.sem_inc(go, 1)
                    gp.wait_ge(S["ob_used"], cnt(ph, "ob_used", tr))
                    gp.sem_inc(go, 1)
                    gp.tensor_tensor(R3[b][:, :, :], R3[b][:, :, :],
                                     X[q][:, :, ATTR:ATTR + 1].broadcast_to((NP, T, 192)), ALU.mult)\
                      .then_inc(S["gate_in"], 1)

                def coefs(tr):
                    b, q = tr.b, tr.m
                    gp.wait_ge(S4["nldx"][q], node_dma(l, tr, PERX))
                    gp.wait_ge(S4["nlda"][q], node_dma(l, tr, PERA))
                    att = X[q][:, :, ATTR]
                    c = Chain(gp, S, ph, "gp", tr, go)
                    if l == 1:
                        gp.wait_ge(S["sin_done"], cnt(ph, "sin_done", tr))
                    if tr.has(-2, NTRIPS):
                        wait(gp, S["r_done"], cnt(ph, "r_done", tr.shift(-2)))
                    if l == 1:
                        gp.tensor_tensor(co[b][:, 0:T], sc8[b][:, T:], att, ALU.mult).then_inc(S["coef_done"], 1)
                        gp.tensor_tensor(co[b][:, T:], sc8[b][:, 0:T], att, ALU.mult).then_inc(S["co_done"], 1)
                    if l == 2:
                        gp.wait_ge(S["ang_done"], cnt(ph, "ang_done", tr))
                        c.step(gp.tensor_tensor(co[b][:, T:], co[b][:, T:], att, ALU.mult))
                        c.step(gp.tensor_tensor(co[b][:, 0:T], co[b][:, T:], co[b][:, T:], ALU.mult))
                        gp.tensor_tensor(co[b][:, T:], co[b][:, 0:T], AG[q][:, :, F], ALU.mult)\
                          .then_inc(S["co_done"], 1)
                    c.end()

                def plus_row(tr):
                    b, q = tr.b, tr.m
                    gp.wait_ge(S["ag_done"], cnt(ph, "ag_done", tr))
                    gp.tensor_tensor(T2B[b][:, :, :], T2B[b][:, :, :], X[q][:, :, 0:F], ALU.add)\
                      .then_inc(S["t2_done"], 1)

                if l in (1, 2):
                    coefs(Trip(0, 0))
                    plus_row(Trip(0, 0))
                if l == 3:
                    times_attr(Trip(0, 0))

                def node_trip(tr):
                    if l == 3 and tr.has(1, NTRIPS):
                        times_attr(tr.shift(1))
                    if l in (1, 2) and tr.has(1, NTRIPS):
                        coefs(tr.shift(1))
                    if tr.has(-1, NTRIPS):
                        attr_out(tr.shift(-1))
                        node_rstd(tr.shift(-1))
                    if l in (1, 2) and tr.has(1, NTRIPS):
                        plus_row(tr.shift(1))

                trips(gp, NTRIPS, node_trip, NBUF)
                attr_out(Trip(0, NTRIPS - 1))
                node_rstd(Trip(0, NTRIPS - 1))

        @block.scalar
        def _(ac):
            ac.wait_ge(w_zero, N_CLEAR + 1)
            ac.wait_ge(w_pe, 1)
            ac.copy(wvt[:, 0:96], psR[0:CS, 0, 0:96]).then_inc(w_act, 1)
            ac.copy(wvt[:, 192:224], psR[0:CS, 0, 64:96]).then_inc(w_act, 1)
            ac.wait_ge(w_pe, 2)
            ac.wait_ge(w_load, N_LOAD)
            ac.copy(ra[0][0:64, 128:160], psR[0:64, 1, 0:32]).then_inc(w_act, 1)
            ac.copy(rb[0][0:32, 224:256], psR[0:32, 2, 0:32]).then_inc(w_act, 1)

            for l in range(4):
                ph, rad, R_ = f"E{l}", LAYERS[l]["rad"], ring_banks(l)

                def evac(tr, k, dst, rows, cols, func=ACT.Copy, **kw):
                    pos = ring_pos(l, tr, k)
                    ac.wait_ge(S["pe_ring"], ring_val(ph, l, tr, k))
                    ac.activation(dst, psR[0:rows, pos % R_, 0:cols], func, **kw)\
                      .then_inc(S["act_ring"], ring_inc(l, k))

                def squares(tr):
                    ac.wait_ge(S2["gath"][tr.b], cnt2(ph, "gath", tr))
                    if tr.has(-1, ETRIPS):
                        ac.wait_ge(S["stat_done"], cnt(ph, "stat_done", tr.shift(-1)))
                    ac.activation(sqv[:, 0:T, :], GS[tr.b][:, :, CS:F], ACT.Square, scale=CV ** -0.5)
                    ac.activation(sqv[:, T:, :], GD[tr.b][:, :, CS:F], ACT.Square, scale=CV ** -0.5)\
                      .then_inc(S["sq_done"], 1)

                def norm_and_messages(tr):
                    for c in range(2):
                        evac(tr, f"n{c}", ET_[c][0:96, :], 96, EC, scale=gv[:, 0:1])
                    evac(tr, "n2", ET_[2][:, :], 2 * CS, EC, ACT.Identity, scale=gs[:, 0:1], bias=bs[:, 0:1])
                    ac.wait_ge(S["ob_full"], ob_val(ph, tr, "M"))
                    ac.copy(MG[:, :, :].rearrange("p (b t) f -> p b (t f)", b=2), psO[0:EP, :, 0:2 * F])\
                      .then_inc(S["ob_evac"], 1)

                def radial_in(tr):
                    evac(tr, "e", esT[0:rad, :], rad, EC)

                def radial_hidden(tr):
                    evac(tr, "h", hidT[:, :], CS, EC, ACT.Silu)

                def radial_out(tr):
                    if tr.has(-2, ETRIPS):
                        wait(ac, S["prod_done"], cnt(ph, "prod_done", tr.shift(-2), nc_))
                    for c in range(nc_):
                        w = 96 if c == 2 else 128
                        evac(tr, f"w{c}", wT[tr.b][c][0:w, 0:EC], w, EC)

                def inputs_t(tr):
                    for c in range(nc_):
                        w = 96 if c == 2 else 128
                        evac(tr, f"t{c}", ET_[c][0:w, :], w, EC)

                def outputs(tr):
                    w = EOW[l]
                    ac.wait_ge(S["ob_full"], cnt(ph, "ob_full", tr))
                    ac.copy(O[tr.b][:, :, 0:w].rearrange("p (b t) f -> p b t f", b=2),
                            psO[0:EP, :, 0:2 * w].rearrange("p b (t f) -> p b t f", t=2))\
                      .then_inc(S["ob_evac"], 1)

                nc_ = CHUNKS[l]
                if l == 0:
                    squares(Trip(0, 0))
                    norm_and_messages(Trip(0, 0))
                    radial_in(Trip(0, 0))
                    radial_out(Trip(0, 0))
                    squares(Trip(0, 1))
                else:
                    radial_in(Trip(0, 0))
                    radial_hidden(Trip(0, 0))
                    radial_out(Trip(0, 0))
                    radial_in(Trip(0, 1))
                    radial_hidden(Trip(0, 1))

                def second_outputs(tr):
                    ac.wait_ge(S["ob_full"], ob_val(ph, tr, "O2"))
                    ac.copy(O2[:, :, 0:48].rearrange("p (b t) f -> p b t f", b=2),
                            psO[0:EP, :, 0:384].rearrange("p b (t f) -> p b t f", t=2 * H))\
                      .then_inc(S["ob_evac"], 1)

                def first_trip(tr):
                    if tr.has(1, ETRIPS):
                        radial_in(tr.shift(1))
                    if tr.has(-1, ETRIPS):
                        second_outputs(tr.shift(-1))
                    for h in range(2):
                        ac.wait_ge(S["ob_full"], ob_val(ph, tr, f"o{h}"))
                        ac.copy(O[0][:, 2 * h:2 * h + 2, :], psO[0:EP, :, 0:288]).then_inc(S["ob_evac"], 1)
                    ac.wait_ge(S["ob_evac"], ob_val(ph, tr, "o1"))
                    ac.activation(SG[:, :, :], O[0][:, :, 160:256], ACT.Tanh, scale=0.5)\
                      .then_inc(S["tanh_done"], 1)
                    if tr.has(1, ETRIPS):
                        norm_and_messages(tr.shift(1))
                        radial_out(tr.shift(1))
                    ac.wait_ge(S["d_ready"], cnt(ph, "d_ready", tr))
                    ac.activation(pc[:, :, :], dd[:, :, :], ACT.Exp).then_inc(S["exp_done"], 1)
                    inputs_t(tr)
                    if tr.has(2, ETRIPS):
                        squares(tr.shift(2))

                def edge_trip(tr):
                    if l == 0:
                        first_trip(tr)
                        return
                    inputs_t(tr)
                    if tr.has(1, ETRIPS):
                        radial_out(tr.shift(1))
                    if tr.has(2, ETRIPS):
                        radial_in(tr.shift(2))
                    if tr.has(-1, ETRIPS):
                        outputs(tr.shift(-1))
                    if tr.has(2, ETRIPS):
                        radial_hidden(tr.shift(2))

                trips(ac, ETRIPS, edge_trip, EBUF)
                (outputs if l else second_outputs)(Trip(0, ETRIPS - 1))
                if l == 0:
                    ac.wait_ge(fx_dve, 3)
                    ac.activation(fm[:, 2:4, :], fm[:, 2:4, :], ACT.Exp).then_inc(fx_act, 1)

                ph = f"N{l}"

                def normed(tr):
                    y = tr.y
                    ac.wait_ge(S["rstd_done"], cnt(ph, "rstd_done", tr))
                    ac.wait_ge(S["a_done"], cnt(ph, "a_done", tr))
                    for j in range(T):
                        last = ac.activation(Y[tr.m][:, j, 0:F], R[y][:, j, 0:F], ACT.Identity,
                                             bias=nrs[y][:, j, 1:2], scale=nrs[y][:, j, 0:1])
                    last.then_inc(S["y_done"], 1)

                def rows_t(tr):
                    b = tr.b
                    if tr.has(-2, NTRIPS):
                        ac.wait_ge(S["ob_full"], cnt(ph, "ob_full", tr.shift(-2)))
                    for k, dst, rows in ((0, NT1[b], 96), (1, NT2[b], CS)):
                        ac.wait_ge(S["pe_ring"], cnt(ph, "pe_ring", tr, k + 1))
                        ac.copy(dst[0:rows, :], ps[0:rows, 2 * b + k, :]).then_inc(S["act_ring"], 1)

                def sines(tr):
                    b = tr.b
                    ac.wait_ge(S["ang_done"], cnt(ph, "ang_done", tr))
                    if tr.has(-2, NTRIPS):
                        ac.wait_ge(S["t2_done"], cnt(ph, "t2_done", tr.shift(-2)))
                    ac.activation(sc8[b][:, :], angr[b][:, :], ACT.Sin).then_inc(S["sin_done"], 1)

                def scaled_aggregate(tr):
                    b, q = tr.b, tr.m
                    ac.wait_ge(S["co_done"], cnt(ph, "co_done", tr))
                    for j in range(T):
                        last = ac.activation(T2B[b][:, j, :], AG[q][:, j, 0:F], ACT.Copy,
                                             scale=co[b][:, T + j:T + j + 1])
                    last.then_inc(S["ag_done"], 1)

                def gates(tr):
                    ac.wait_ge(S["gate_in"], cnt(ph, "gate_in", tr))
                    ac.activation(SGN[tr.b][:, :, :], R3[tr.b][:, :, 96:192], ACT.Sigmoid).then_inc(S["sig_done"], 1)

                for g in range(AHEAD[l]):
                    rows_t(Trip(0, g))
                if l == 1:
                    sines(Trip(0, 0))
                if l in (1, 2):
                    scaled_aggregate(Trip(0, 0))
                if l == 3:
                    gates(Trip(0, 0))

                def node_trip(tr):
                    if l == 1 and tr.has(1, NTRIPS):
                        sines(tr.shift(1))
                    if tr.has(AHEAD[l], NTRIPS):
                        rows_t(tr.shift(AHEAD[l]))
                    if l == 3 and tr.has(1, NTRIPS):
                        gates(tr.shift(1))
                    if l in (1, 2) and tr.has(1, NTRIPS):
                        scaled_aggregate(tr.shift(1))
                    if tr.has(-2, NTRIPS):
                        normed(tr.shift(-2))

                trips(ac, NTRIPS, node_trip, NBUF)
                normed(Trip(0, NTRIPS - 2))
                normed(Trip(0, NTRIPS - 1))

        @block.tensor
        def _(pe):
            def tr_(dst, src, parts):
                return pe.transpose(dst, src, ident[0:parts, 0:parts])

            pe.wait_ge(w_zero, N_CLEAR + 13)
            pe.wait_ge(w_load, N_LOAD)
            tr_(psR[0:CS, 0, 0:96], wval[:, :], 96).then_inc(w_pe, 1)
            pe.wait_ge(w_act, 2)
            pe.matmul(psR[0:64, 1, 0:32], wvt[:, 0:64], wg[:, :], start=True, stop=True)
            pe.matmul(psR[0:32, 2, 0:32], wvt[:, 192:224], wg[:, :], start=True, stop=True).then_inc(w_pe, 1)
            pe.wait_ge(w_act, 4)
            pe.wait_ge(w_dve, FIRST_STEPS)

            for l in range(4):
                ph, rad, R_ = f"E{l}", LAYERS[l]["rad"], ring_banks(l)
                nc_ = CHUNKS[l]
                if l == 1:
                    pe.wait_ge(w_dve, SETUP_STEPS)
                if l:
                    pe.wait_ge(S["act_ring"], total(f"N{l - 1}", "act_ring"))
                    pe.wait_ge(S["ob_used"], total(f"N{l - 1}", "ob_used"))

                def slot(tr, k):
                    pos = ring_pos(l, tr, k)
                    v = ring_val(ph, l, tr, k)
                    base = BASE[ph].get("act_ring", 0)
                    if not isinstance(v, int) or v - base > R_:
                        pe.wait_ge(S["act_ring"], v - R_)
                        pe.sem_inc(pe_go, 1)
                    return psR[:, pos % R_, :]

                def out_of_ring(tr, k):
                    pe.wait_ge(S["act_ring"], ring_val(ph, l, tr, k))

                def ob_free(v):
                    if not isinstance(v, int) or v > BASE[ph].get("ob_evac", 0) + 1:
                        pe.wait_ge(S["ob_evac"], v - 1)

                def norm_and_messages(tr):
                    pe.wait_ge(S["xn_done"], cnt(ph, "xn_done", tr))
                    for c in range(3):
                        bank = slot(tr, f"n{c}")
                        w = 2 * CS if c == 2 else 96
                        for j in range(T):
                            last = tr_(bank[0:w, j * EP:(j + 1) * EP], XN[:, j, 96 * c:96 * c + w], EP)
                        last.then_inc(S["pe_ring"], 1)
                    out_of_ring(tr, "n2")
                    ob_free(ob_val(ph, tr, "M"))
                    for j in range(T):
                        dst, at = psO[0:EP, j // 2, F * (j % 2):F * (j % 2) + F], slice(j * EP, (j + 1) * EP)
                        pe.matmul(dst[:, 0:96], ET_[0][0:96, at], wm[0][:, :], start=True, stop=False)
                        pe.matmul(dst[:, 0:96], ET_[1][0:96, at], wm[1][:, :], start=False, stop=True)
                        last = pe.matmul(dst[:, 96:F], ET_[2][:, at], wm[2][:, :], start=True, stop=True)
                    last.then_inc(S["ob_full"], 1)

                def radial_in(tr):
                    b = tr.b
                    pe.wait_ge(S2["ldr"][b], cnt2(ph, "ldr", tr))
                    bank = slot(tr, "e")
                    for j in range(T):
                        last = tr_(bank[0:rad, j * EP:(j + 1) * EP], es_in[b][:, j * rad:(j + 1) * rad], EP)
                    last.then_inc(S["pe_ring"], 1)

                def radial_hidden(tr):
                    out_of_ring(tr, "e")
                    pe.sem_inc(pe_go, 1)
                    bank = slot(tr, "h")
                    pe.matmul(bank[0:CS, 0:EC], fc1[l][:, :], esT[0:rad, :], start=True, stop=True)\
                      .then_inc(S["pe_ring"], ring_inc(l, "h"))

                def radial_out(tr):
                    out_of_ring(tr, "h" if l else "e")
                    pe.sem_inc(pe_go, 1)
                    src = hidT[:, :] if l else esT[0:rad, :]
                    for c in range(nc_):
                        w = 96 if c == 2 else 128
                        bank = slot(tr, f"w{c}")
                        pe.matmul(bank[0:w, 0:EC], fc2[l][:, 128 * c:128 * c + w], src, start=True, stop=True)\
                          .then_inc(S["pe_ring"], 1)

                def inputs_t(tr, E_, what):
                    for c in range(nc_):
                        w = 96 if c == 2 else 128
                        bank = psF[:, c, :] if what is None else slot(tr, f"t{c}")
                        for j in range(T):
                            last = tr_(bank[0:w, j * EP:(j + 1) * EP], E_[:, j, 128 * c:128 * c + w], EP)
                        last.then_inc(S["f_done" if what is None else "pe_ring"], 1)

                def outputs(tr):
                    pe.wait_ge(S["prod_done"], cnt(ph, "prod_done", tr, nc_))
                    w = EOW[l]
                    per_bank = 1 if l == 0 else 2
                    for j in range(T):
                        if j % (2 * per_bank) == 0:
                            if l == 0:
                                ob_free(ob_val(ph, tr, f"o{j // 2}"))
                            else:
                                ob_free(cnt(ph, "ob_evac", tr))
                        o = w * (j % per_bank)
                        dst = psO[0:EP, (j // per_bank) % 2, :]
                        at = slice(j * EP, (j + 1) * EP)
                        pe.matmul(dst[:, o:o + w], PR[0][:, at], rb[l][:, :], start=True, stop=True)
                        if nc_ == 3:
                            pe.matmul(dst[:, o:o + 96], PR[2][0:96, at], rx[l][:, :], start=False, stop=True,
                                      skip_group_check=True)
                        last = pe.matmul(dst[:, o + 96:o + w], PR[1][:, at], ra[l][:, :], start=False, stop=True,
                                         skip_group_check=True)
                        if j % (2 * per_bank) == 2 * per_bank - 1:
                            last.then_inc(S["ob_full"], 1)

                if l == 0:
                    norm_and_messages(Trip(0, 0))
                radial_in(Trip(0, 0))
                if l:
                    radial_hidden(Trip(0, 0))
                radial_out(Trip(0, 0))
                if l:
                    radial_in(Trip(0, 1))
                    radial_hidden(Trip(0, 1))

                def second_outputs(tr):
                    out_of_ring(tr, "t2")
                    ob_free(ob_val(ph, tr, "O2"))
                    for j in range(T):
                        dst, at = psO[0:EP, j // 2, 192 * (j % 2):192 * (j % 2) + 192], slice(j * EP, (j + 1) * EP)
                        pe.matmul(dst, ET_[1][:, at], r2a[:, :], start=True, stop=False)
                        pe.matmul(dst, ET_[0][:, at], r2b[:, :], start=False, stop=False)
                        last = pe.matmul(dst, ET_[2][0:96, at], r2x[:, :], start=False, stop=True)
                    last.then_inc(S["ob_full"], 1)

                def first_trip(tr):
                    pe.wait_ge(S["e_done"], cnt(ph, "e_done", tr))
                    inputs_t(tr, EE, None)
                    if tr.has(1, ETRIPS):
                        radial_in(tr.shift(1))
                    if tr.has(-1, ETRIPS):
                        second_outputs(tr.shift(-1))
                    outputs(tr)
                    if tr.has(1, ETRIPS):
                        norm_and_messages(tr.shift(1))
                        radial_out(tr.shift(1))
                    pe.wait_ge(S["e2_done"], cnt(ph, "e2_done", tr))
                    inputs_t(tr, E2, "t")

                def edge_trip(tr):
                    if l == 0:
                        first_trip(tr)
                        return
                    pe.wait_ge(S["e_done"], cnt(ph, "e_done", tr))
                    inputs_t(tr, EEs[tr.b], "t")
                    if tr.has(1, ETRIPS):
                        radial_out(tr.shift(1))
                    if tr.has(2, ETRIPS):
                        radial_in(tr.shift(2))
                    if tr.has(-1, ETRIPS):
                        outputs(tr.shift(-1))
                    for c in range(nc_):
                        w = 96 if c == 2 else 128
                        out_of_ring(tr, f"t{c}")
                        wf = wf1[l] if c == 1 else wf2[l]
                        pe.matmul(psF[0:w, c, 0:EC], wf[0:w, 0:w], ET_[c][0:w, :], start=True, stop=True)\
                          .then_inc(S["f_done"], 1)
                    if tr.has(2, ETRIPS):
                        radial_hidden(tr.shift(2))

                trips(pe, ETRIPS, edge_trip, EBUF)
                (outputs if l else second_outputs)(Trip(0, ETRIPS - 1))

                pe.wait_ge(S["ob_evac"], total(ph, "ob_evac"))
                if l == 0:
                    pe.wait_ge(fx_dve, 1)
                    pe.matmul(psF[0:EP, 0, 0:H * EP], ones_k[:, :], fdg[:, :], start=True, stop=True)\
                      .then_inc(fx_mm, 1)
                    pe.wait_ge(fx_dve, 4)
                else:
                    pe.wait_ge(fx_rd, 16 * (l + 1))
                pe.matmul(psO[0:EP, 0, 0:AW], same[:, :], FX[:, :], start=True, stop=True).then_inc(fx_mm, 1)

                ph = f"N{l}"
                pe.wait_ge(fx_dve, FIX_STEPS[l])
                pe.wait_ge(S["act_ring"], total(f"E{l}", "act_ring"))

                def transposes(tr):
                    b, q = tr.b, tr.m
                    if l == 0:
                        pe.wait_ge(S["agn_done"], cnt(ph, "agn_done", tr))
                        src = AGN[b]
                    else:
                        pe.wait_ge(S4["nldx"][q], node_dma(l, tr, PERX))
                        src = X[q]
                    pe.sem_inc(pe_go, 1)
                    for k, lo, hi in ((0, 0, 96), (1, 96, F)):
                        if tr.has(-2, NTRIPS):
                            pe.wait_ge(S["act_ring"], cnt(ph, "act_ring", tr.shift(-2), k + 1))
                            pe.sem_inc(pe_go, 1)
                        for j in range(T):
                            last = tr_(ps[0:hi - lo, 2 * b + k, j * NP:(j + 1) * NP], src[:, j, lo:hi], NP)
                        last.then_inc(S["pe_ring"], 1)

                for g in range(AHEAD[l]):
                    transposes(Trip(0, g))

                def node_trip(tr):
                    b, w = tr.b, NOW[l]
                    pe.wait_ge(S["act_ring"], cnt(ph, "act_ring", tr, 2))
                    if tr.has(-2, NTRIPS):
                        pe.wait_ge(S["ob_used"], cnt(ph, "ob_used", tr.shift(-2)))
                    for j in range(T):
                        dst, o, at = NPO[b][:, j // 2, :], w * (j % 2), slice(j * NP, (j + 1) * NP)
                        pe.matmul(dst[:, o:o + 96], NT1[b][0:96, at], nw1[l][:, :], start=True, stop=True)
                        last = pe.matmul(dst[:, o + 96:o + w], NT2[b][0:CS, at], nw2[l][:, :], start=True, stop=True)
                    last.then_inc(S["ob_full"], 1)
                    if tr.has(AHEAD[l], NTRIPS):
                        transposes(tr.shift(AHEAD[l]))

                trips(pe, NTRIPS, node_trip, NBUF)

        @block.vector
        def _(ve):
            n = [0]

            def step(ins):
                n[0] += 1
                ins.then_inc(w_dve, 1)
                ve.wait_ge(w_dve, n[0])

            def bc(ap, shape):
                return ap.broadcast_to(shape)

            ve.wait_ge(w_zero, N_CLEAR + 13)
            ve.wait_ge(g_load, 80)
            step(ve.tensor_copy(dst_f[:, :], dst_i[:, :]))
            step(ve.tensor_copy(edge_f[:, :], edge_i[:, :]))
            step(ve.tensor_copy(hrow[:, :], hrow_i[:, :]))
            step(ve.tensor_copy(cf[:, 0:1], pid[:, :]))
            step(ve.tensor_copy(head_i[:, :], dst_i[:, 0:1]))
            step(ve.tensor_scalar(cf[:, 1:2], cf[:, 0:1], float(SKIP - N), None, ALU.add))
            keep, mask = runs[:, :, 0], runs[:, :, 1]
            step(ve.memset(wk1[:, :], 0.0))
            step(ve.tensor_tensor(wk1[:, 1:ET], dst_f[:, 1:ET], dst_f[:, 0:ET - 1], ALU.is_equal))
            step(ve.tensor_copy(keep, wk1[:, :]))
            step(ve.tensor_scalar(mask, wk1[:, :], -1.0, BIG, ALU.add, ALU.mult))
            step(ve.tensor_tensor_scan(wk2[:, :], wk1[:, :], wk_one[:, :], 0.0, ALU.mult, ALU.add))
            step(ve.tensor_copy(runs[:, :, 2], wk2[:, :]))
            step(ve.tensor_tensor(cf[:, 2:3], dst_f[:, 0:1], edge_f[:, 1:2], ALU.is_equal))
            step(ve.tensor_tensor(cf[:, 4:5], dst_f[:, 0:1], edge_f[:, 0:1], ALU.is_equal))
            step(ve.tensor_tensor(cf[:, 5:6], edge_f[:, 0:1], edge_f[:, 2:3], ALU.is_equal))
            step(ve.tensor_tensor(cf[:, 4:5], cf[:, 4:5], cf[:, 5:6], ALU.mult))
            step(ve.tensor_scalar(cf[:, 4:5], cf[:, 4:5], -1.0, 1.0, ALU.mult, ALU.add))
            step(ve.tensor_tensor(cf[:, 3:4], cf[:, 2:3], cf[:, 4:5], ALU.mult))
            step(ve.tensor_tensor(cf[:, 6:7], dst_f[:, 0:1], cf[:, 1:2], ALU.subtract))
            step(ve.tensor_tensor(cf[:, 6:7], cf[:, 6:7], cf[:, 3:4], ALU.mult))
            step(ve.tensor_tensor(cf[:, 6:7], cf[:, 6:7], cf[:, 1:2], ALU.add))
            step(ve.tensor_copy(fixid[:, :], cf[:, 6:7]))
            step(ve.tensor_scalar(wk2[:, :], dst_f[:, :], dst_f[:, 0:1], cf[:, 2:3], ALU.is_equal, ALU.mult))
            step(ve.tensor_scalar(wk1[:, :], dst_f[:, :], cf[:, 0:1], -1.0, ALU.subtract, ALU.mult))
            step(ve.tensor_tensor(wk1[:, :], wk1[:, :], wk2[:, :], ALU.mult))
            step(ve.tensor_tensor(wk1[:, :], wk1[:, :], dst_f[:, :], ALU.add))
            step(ve.tensor_scalar(wk1[:, :], wk1[:, :], cf[:, 1:2], None, ALU.subtract))
            step(ve.memset(wk2[:, :], 1.0))
            step(ve.tensor_scalar(wk2[:, 0:ET - 1], runs[:, 1:ET, 0], -1.0, 1.0, ALU.mult, ALU.add))
            step(ve.tensor_tensor(wk1[:, :], wk1[:, :], wk2[:, :], ALU.mult))
            step(ve.tensor_scalar(wk1[:, :], wk1[:, :], cf[:, 1:2], None, ALU.add))
            step(ve.tensor_copy(scix[:, :], wk1[:, :]))
            step(ve.tensor_scalar(same[:, :], hrow[:, :], dst_f[:, 0:1], None, ALU.is_equal))
            step(ve.tensor_scalar(samen[:, :], same[:, :], -1.0, BIG, ALU.add, ALU.mult))
            assert n[0] == GRAPH_STEPS, n
            ve.wait_ge(w_load, N_LOAD)
            ve.wait_ge(w_act, 4)
            for region, factor in ((rx[0][:, :], r2), (rb[0][0:32, 96:256], r3)):
                ve.tensor_scalar(region, region, factor, None, ALU.mult).then_inc(w_dve, 1)
            n[0] += 2
            for t, g in ((r2a, cA), (r2b, cB), (r2x, cX)):
                step(ve.tensor_scalar(t[:, :], t[:, :], g[:, 0:1], None, ALU.mult))
            step(ve.tensor_scalar(r2b[0:32, :], r2b[0:32, :], r3, None, ALU.mult))
            step(ve.tensor_scalar(r2x[:, :], r2x[:, :], r2, None, ALU.mult))
            assert n[0] == FIRST_STEPS, n

            def later_weights():
                ve.wait_ge(w_late, 16 * len(later))
                for region, factor in scales:
                    ve.tensor_scalar(region, region, factor, None, ALU.mult).then_inc(w_dve, 1)
                assert FIRST_STEPS + len(scales) == SETUP_STEPS, len(scales)

            fx = [0]

            def fstep(ins):
                fx[0] += 1
                ins.then_inc(fx_dve, 1)
                ve.wait_ge(fx_dve, fx[0])

            for l in range(4):
                ph, nc_, cross = f"E{l}", CHUNKS[l], LAYERS[l]["cross"]

                def attrs(tr):
                    b, q = tr.b, tr.q
                    wait(ve, S4["ldy"][q], edge_dma(l, tr))
                    if l == 0:
                        ve.tensor_copy(yc[q][:, :, 0:4], y_in[q][:, :, :])
                        return ve.tensor_copy(yc[q][:, :, 4:6], y_in[q][:, :, 1:3])
                    att = G[b][:, :, ATTR:ATTR + 1]
                    ve.tensor_tensor(yc[q][:, :, 0:4], y_in[q][:, :, :], bc(att, (EP, T, 4)), ALU.mult)
                    return ve.tensor_tensor(yc[q][:, :, 4:6], y_in[q][:, :, 1:3], bc(att, (EP, T, 2)), ALU.mult)

                def tp_inputs(src, y, dst, c, done):
                    v = src[:, :, 0:96].rearrange("p t (d c) -> p t d c", d=3)
                    sh = (EP, T, 3, CV)

                    def times(out, vd, yd, m):
                        return ve.tensor_tensor(out, v[:, :, vd:vd + m, :],
                                                bc(y[:, :, yd:yd + m].unsqueeze(3), (EP, T, m, CV)), ALU.mult)

                    t4 = tmp[:, :, :].rearrange("p t (d c) -> p t d c", d=3)
                    t5 = tmp2[:, :, :].rearrange("p t (d c) -> p t d c", d=3)
                    times(t4, 0, 1, 3)
                    if cross:
                        x4 = dst[:, :, C_X:C_X + 96].rearrange("p t (d c) -> p t d c", d=3)
                        times(x4[:, :, 0:2, :], 1, 3, 2)
                        times(x4[:, :, 2:3, :], 0, 5, 1)
                        times(t5[:, :, 0:1, :], 2, 2, 1)
                        times(t5[:, :, 1:3, :], 0, 3, 2)
                    ve.tensor_copy(dst[:, :, C_S:C_S + CS], src[:, :, 96:F])
                    c.step(ve.tensor_tensor(dst[:, :, C_YV:C_YV + F], src[:, :, 0:F],
                                            bc(y[:, :, 0:1], (EP, T, F)), ALU.mult))
                    if cross:
                        xs = dst[:, :, C_X:C_X + 96]
                        ve.tensor_tensor(xs, xs, tmp2[:, :, :], ALU.subtract)
                    ve.tensor_reduce(dst[:, :, C_VY:C_VY + CV], tmp[:, :, :].rearrange("p t (d c) -> p t c d", d=3),
                                     AX.X, ALU.add).then_inc(S[done], 1)

                def inputs(tr):
                    b = tr.b
                    c = Chain(ve, S, ph, "d_in", tr)
                    if l == 0:
                        ve.wait_ge(S["ob_evac"], ob_val(ph, tr, "M"))
                        src = MG
                    else:
                        ve.wait_ge(S2["gath"][b], cnt2(ph, "gath", tr))
                        src = G[b]
                    c.step(attrs(tr))
                    if l and tr.has(-2, ETRIPS):
                        ve.wait_ge(S["pe_ring"], ring_val(ph, l, tr.shift(-2), f"t{nc_ - 1}"))
                    if l and tr.has(-1, ETRIPS):
                        ve.wait_ge(S["e_done"], cnt(ph, "e_done", tr.shift(-1)))
                    tp_inputs(src, yc[tr.q], EEs[tr.b] if l else EE, c, "e_done")
                    c.end()

                def products(tr):
                    for c in range(nc_):
                        w = 96 if c == 2 else 128
                        ve.wait_ge(S["f_done"], cnt(ph, "f_done", tr, c + 1))
                        if c == 0:
                            ve.wait_ge(S["act_ring"], ring_val(ph, l, tr, f"w{nc_ - 1}"))
                        ve.tensor_tensor(PR[c][0:w, :], psF[0:w, c, 0:EC], wT[tr.b][c][0:w, 0:EC],
                                         ALU.mult)\
                          .then_inc(S["prod_done"], 1)

                def times_u(o, uo, y, c):
                    u = o[:, :, uo:uo + CV].unsqueeze(2)
                    t4 = tmp3[:, :, :].rearrange("p t (d c) -> p t d c", d=3)
                    c.step(ve.tensor_tensor(t4, bc(u, (EP, T, 3, CV)), bc(y[:, :, 1:4].unsqueeze(3), (EP, T, 3, CV)),
                                            ALU.mult))
                    c.step(ve.tensor_tensor(o[:, :, 0:96], o[:, :, 0:96], tmp3[:, :, :], ALU.add))

                def out_free(tr):
                    if tr.has(-2, ETRIPS):
                        wait(ve, S2["scat"][tr.b], cnt2(ph, "scat", tr.shift(-2)))

                def messages(tr):
                    b = tr.b
                    c = Chain(ve, S, ph, "d_post", tr)
                    w = EOW[l] - 32
                    ve.wait_ge(S["ob_evac"], cnt(ph, "ob_evac", tr))
                    times_u(O[b], w, yc[tr.q], c)
                    out_free(tr)
                    if l == 2:
                        ve.tensor_copy(OUT[b][:, :, w], kc[tr.q][:, :, 2])
                    for t in range(T):
                        prev = OUT[b][:, t - 1, 0:w] if t else OUT[1 - b][:, T - 1, 0:w]
                        ins = ve.scalar_tensor_tensor(OUT[b][:, t, 0:w], prev, kc[tr.q][:, t, 0:1], O[b][:, t, 0:w],
                                                      op0=ALU.mult, op1=ALU.add)
                        if t < T - 1:
                            c.step(ins)
                    ins.then_inc(S["msg_done"], 1)
                    ve.wait_ge(S["msg_done"], cnt(ph, "msg_done", tr))
                    c.end()

                def norm_stats(tr):
                    b = tr.b
                    c = Chain(ve, S, ph, "d_norm", tr)
                    ve.wait_ge(S2["gath"][b], cnt2(ph, "gath", tr))
                    for i in range(2 * T):
                        src = (GS, GD)[i // T][b]
                        ins = ve.bn_stats(bst[:, i, :], src[:, i % T, 0:CS])
                    c.step(ins)
                    ve.sem_inc(ve_go, 1)
                    for i in range(2 * T):
                        ve.bn_aggr(lst[:, i, 0:2], bst[:, i, :])
                    ve.wait_ge(S["sq_done"], cnt(ph, "sq_done", tr))
                    ve.tensor_reduce(lst[:, :, 2], sqv[:, :, :], AX.X, ALU.add).then_inc(S["stat_done"], 1)
                    ve.wait_ge(S["stat_done"], cnt(ph, "stat_done", tr))
                    c.end()

                def norm_rows(tr):
                    b = tr.b
                    ve.wait_ge(S["pow_done"], cnt(ph, "pow_done", tr))
                    for i in range(2 * T):
                        src = (GS, GD)[i // T][b]
                        o = XN[:, i % T, 192 + CS * (i // T):192 + CS * (i // T) + CS]
                        ve.tensor_scalar(o, src[:, i % T, 0:CS], lst[:, i, 0:1], lrs[:, i, 0:1],
                                         ALU.subtract, ALU.mult)
                    for side in range(2):
                        src = (GS, GD)[side][b][:, :, CS:F].rearrange("p t (c d) -> p t d c", d=3)
                        o = XN[:, :, 96 * side:96 * side + 96].rearrange("p t (d c) -> p t d c", d=3)
                        ins = ve.tensor_tensor(o, src,
                                               bc(lrs[:, side * T:side * T + T, 1:2].unsqueeze(3), (EP, T, 3, CV)),
                                               ALU.mult)
                    ins.then_inc(S["xn_done"], 1)

                def first_outputs(tr):
                    b = tr.b
                    c = Chain(ve, S, ph, "d_post", tr)
                    o = O[0]
                    ve.wait_ge(S["ob_evac"], ob_val(ph, tr, "o1"))
                    c.step(ve.scalar_tensor_tensor(LK[:, :, :], o[:, :, 96:160], 0.2, o[:, :, 96:160],
                                                   op0=ALU.mult, op1=ALU.max))
                    c.step(ve.tensor_tensor(LK[:, :, :], LK[:, :, :], bc(adot[:, :].unsqueeze(1), (EP, T, CS)),
                                            ALU.mult))
                    c.step(ve.tensor_reduce(al[:, :], LK[:, :, :].rearrange("p t (h s) -> p (t h) s", s=AS),
                                            AX.X, ALU.add))
                    for t in range(T):
                        prev = mx[b][:, H * (t - 1):H * t] if t else mx[1 - b][:, H * (T - 1):]
                        c.step(ve.scalar_tensor_tensor(mx[b][:, H * t:H * t + H], prev, kc[tr.q][:, t, 1:2],
                                                       al[:, H * t:H * t + H], op0=ALU.add, op1=ALU.max))
                    ve.tensor_tensor(dd[:, 0, :], al[:, :], mx[b][:, :], ALU.subtract)
                    ve.tensor_tensor(dd[:, 1, 0:H], mx[1 - b][:, H * (T - 1):], mx[b][:, 0:H], ALU.subtract)
                    c.step(ve.tensor_tensor(dd[:, 1, H:], mx[b][:, 0:H * (T - 1)], mx[b][:, H:], ALU.subtract))
                    d1 = dd[:, 1, :].rearrange("p (t h) -> p t h", h=H)
                    ve.tensor_tensor(d1, d1, bc(kc[tr.q][:, :, 1:2], (EP, T, H)), ALU.add).then_inc(S["d_ready"], 1)
                    times_u(o, 256, yc[tr.q], c)
                    ve.wait_ge(S["tanh_done"], cnt(ph, "tanh_done", tr))
                    ve.tensor_scalar(MG2[:, :, 96:F], SG[:, :, 0:CS], 0.5, 0.5, ALU.mult, ALU.add)
                    c.step(ve.tensor_scalar(SG2[:, :, :], SG[:, :, CS:96], 0.5, 0.5, ALU.mult, ALU.add))
                    c.step(ve.tensor_tensor(MG2[:, :, 0:96].rearrange("p t (d c) -> p t d c", d=3),
                                            o[:, :, 0:96].rearrange("p t (d c) -> p t d c", d=3),
                                            bc(SG2[:, :, :].unsqueeze(2), (EP, T, 3, CV)), ALU.mult))
                    tp_inputs(MG2, yc[tr.q], E2, c, "e2_done")
                    c.end()

                def attention(tr):
                    b = tr.b
                    c = Chain(ve, S, ph, "d_fin", tr)
                    ve.wait_ge(S["ob_evac"], ob_val(ph, tr, "O2"))
                    o4 = O2[:, :, :].rearrange("p (t h) f -> p t h f", h=H)
                    y = yc[tr.q]
                    for d in range(3):
                        ins = ve.tensor_tensor(tmp3[:, :, 32 * d:32 * d + 32].rearrange("p t (h f) -> p t h f", h=H),
                                               o4[:, :, :, 0:AV],
                                               bc(y[:, :, 1 + d:2 + d].unsqueeze(3), (EP, T, H, AV)), ALU.mult)
                    c.step(ins)
                    for d in range(3):
                        hv = o4[:, :, :, 24 + AV * d:24 + AV * d + AV]
                        ins = ve.tensor_tensor(hv, hv,
                                               tmp3[:, :, 32 * d:32 * d + 32].rearrange("p t (h f) -> p t h f", h=H),
                                               ALU.add)
                    c.step(ins)
                    ve.wait_ge(S["exp_done"], cnt(ph, "exp_done", tr))
                    c.step(ve.tensor_tensor(MS[:, :, :], O2[:, :, 8:49],
                                            bc(pc[:, 0, :].unsqueeze(2), (EP, T * H, HC + 1)), ALU.mult))
                    out_free(tr)
                    mw = H * (HC + 1)
                    ve.tensor_copy(OUT[b][:, :, mw:mw + H], mx[b][:, :].rearrange("p (t h) -> p t h", h=H))
                    for t in range(T):
                        prev = OUT[b][:, t - 1, 0:mw] if t else OUT[1 - b][:, T - 1, 0:mw]
                        c.step(ve.tensor_tensor(OUT[b][:, t, 0:mw].rearrange("p (h f) -> p h f", h=H),
                                                prev.rearrange("p (h f) -> p h f", h=H),
                                                bc(pc[:, 1, H * t:H * t + H].unsqueeze(2), (EP, H, HC + 1)), ALU.mult))
                        ins = ve.tensor_tensor(OUT[b][:, t, 0:mw], OUT[b][:, t, 0:mw],
                                               MS[:, H * t:H * t + H, :].rearrange("p h f -> p (h f)"), ALU.add)
                        if t < T - 1:
                            c.step(ins)
                    ins.then_inc(S["msg_done"], 1)
                    ve.wait_ge(S["msg_done"], cnt(ph, "msg_done", tr))
                    c.end()

                if l == 0:
                    norm_stats(Trip(0, 0))
                    norm_rows(Trip(0, 0))
                    inputs(Trip(0, 0))

                    def edge_trip(tr):
                        if tr.has(1, ETRIPS):
                            norm_stats(tr.shift(1))
                        products(tr)
                        if tr.has(1, ETRIPS):
                            norm_rows(tr.shift(1))
                        if tr.has(-1, ETRIPS):
                            attention(tr.shift(-1))
                        first_outputs(tr)
                        if tr.has(1, ETRIPS):
                            inputs(tr.shift(1))

                    trips(ve, ETRIPS, edge_trip, EBUF)
                    later_weights()
                    attention(Trip(0, ETRIPS - 1))
                else:
                    inputs(Trip(0, 0))
                    inputs(Trip(0, 1))

                    def edge_trip(tr):
                        products(tr)
                        if tr.has(-1, ETRIPS):
                            messages(tr.shift(-1))
                        if tr.has(2, ETRIPS):
                            inputs(tr.shift(2))

                    trips(ve, ETRIPS, edge_trip, EBUF)
                    messages(Trip(0, ETRIPS - 1))

                ve.wait_ge(fx_rd, 16 * (l + 1))
                mw = H * (HC + 1)
                if l == 0:
                    cn, mrow = cf[:, 2:3], FX[:, mw:mw + H]
                    fxx = Chain0(ve, w_dve, SETUP_STEPS)
                    fxx.step(ve.tensor_scalar(fm[:, 0, :], mrow, cn, None, ALU.mult))
                    fxx.step(ve.tensor_scalar(cf[:, 7:8], cn, -1.0, BIG, ALU.add, ALU.mult))
                    fxx.step(ve.tensor_scalar(fm[:, 0, :], fm[:, 0, :], cf[:, 7:8], None, ALU.add))
                    for h in range(H):
                        ins = ve.tensor_scalar(fdg[:, h * EP:(h + 1) * EP], ident[0:EP, 0:EP], fm[:, 0, h:h + 1],
                                               None, ALU.mult)
                    fstep(ins)
                    ve.wait_ge(fx_mm, 1)
                    f3 = fdg[:, :].rearrange("p (h q) -> p h q", h=H)
                    fxx.step(ve.tensor_tensor(f3, psF[0:EP, 0, 0:H * EP].rearrange("p (h q) -> p h q", h=H),
                                              bc(samen[:, :].unsqueeze(1), (EP, H, EP)), ALU.add))
                    fxx.step(ve.tensor_reduce(fm[:, 1, :], f3, AX.X, ALU.max))
                    ve.wait_ge(fx_g, 16)
                    fstep(ve.tensor_tensor(fm[:, 1, :], fm[:, 1, :], FB[:, mw:mw + H], ALU.max))
                    ve.tensor_tensor(fm[:, 2, :], fm[:, 0, :], fm[:, 1, :], ALU.subtract)
                    fstep(ve.tensor_tensor(fm[:, 3, :], FB[:, mw:mw + H], fm[:, 1, :], ALU.subtract))
                    ve.wait_ge(fx_act, 1)
                    for row, k in ((FX, 2), (FB, 3)):
                        r4 = row[:, 0:mw].rearrange("p (h f) -> p h f", h=H)
                        ins = ve.tensor_tensor(r4, r4, bc(fm[:, k, :].unsqueeze(2), (EP, H, HC + 1)), ALU.mult)
                    fstep(ins)
                    ve.wait_ge(fx_mm, 2)
                    ve.tensor_copy(FN[:, mw + H:AW], FB[:, mw + H:AW])
                    ve.tensor_copy(FN[:, mw:mw + H], fm[:, 1, :])
                    fstep(ve.tensor_tensor(FN[:, 0:mw], FB[:, 0:mw], psO[0:EP, 0, 0:mw], ALU.add))
                else:
                    ve.wait_ge(fx_g, 16 * (l + 1))
                    ve.wait_ge(fx_mm, l + 2)
                    fstep(ve.tensor_tensor(FN[:, :], FB[:, :], psO[0:EP, 0, 0:AW], ALU.add))
                assert fx[0] == FIX_STEPS[l], fx

                ph = f"N{l}"

                def ob(b, lo, w):
                    v = NPO[b][:, :, 0:2 * NOW[l]].rearrange("p b (t f) -> p b t f", t=2)
                    return v[:, :, :, lo:lo + w]

                def by_bank(t, lo, w):
                    return t[:, :, lo:lo + w].rearrange("p (b t) f -> p b t f", b=2)

                def agn(tr):
                    b, q = tr.b, tr.m
                    ve.wait_ge(S4["nlda"][q], node_dma(l, tr, PERA))
                    if tr.has(-2, NTRIPS):
                        ve.wait_ge(S["pe_ring"], cnt(ph, "pe_ring", tr.shift(-2), 2))
                    c = Chain(ve, S, ph, "d_norm", tr)
                    a4 = AG[q][:, :, 0:mw].rearrange("p t (h f) -> p t h f", h=H)
                    den = rden[b][:, :].rearrange("p (t h) -> p t h", h=H)
                    c.step(ve.tensor_scalar(den, a4[:, :, :, HC], 1e-16, None, ALU.add))
                    c.step(ve.reciprocal(rden[b][:, :], rden[b][:, :]))
                    ve.tensor_tensor(AGN[b][:, :, 96:F].rearrange("p t (h f) -> p t h f", h=H), a4[:, :, :, 0:AS],
                                     bc(den.unsqueeze(3), (NP, T, H, AS)), ALU.mult)
                    for j in range(T):
                        r4 = a4[:, j, :, AS:HC].rearrange("p h (d c) -> p d h c", d=3)
                        last = ve.tensor_tensor(AGN[b][:, j, 0:96].rearrange("p (d h c) -> p d h c", d=3, h=H), r4,
                                                bc(den[:, j, :].unsqueeze(1).unsqueeze(3), (NP, 3, H, AV)), ALU.mult)
                    last.then_inc(S["agn_done"], 1)
                    c.end()

                def counts(tr):
                    b, q = tr.b, tr.m
                    ve.wait_ge(S4["nlda"][q], node_dma(l, tr, PERA))
                    if tr.has(-2, NTRIPS):
                        ve.wait_ge(S["t2_done"], cnt(ph, "t2_done", tr.shift(-2)))
                    c = Chain(ve, S, ph, "d_norm", tr)
                    c.step(ve.tensor_scalar(rden[b][:, 0:T], AG[q][:, :, F + 1], 1.0, None, ALU.max))
                    ve.reciprocal(co[b][:, T:], rden[b][:, 0:T]).then_inc(S["ang_done"], 1)
                    c.end()

                def angles(tr):
                    b, q = tr.b, tr.m
                    ve.wait_ge(S4["nlda"][q], node_dma(l, tr, PERA))
                    ve.wait_ge(S4["nldx"][q], node_dma(l, tr, PERX))
                    if tr.has(-1, NTRIPS):
                        ve.wait_ge(S["ang_done"], cnt(ph, "ang_done", tr.shift(-1)))
                    c = Chain(ve, S, ph, "d_norm", tr)
                    c.step(ve.tensor_tensor(ang[:, 0:T], AG[q][:, :, F], X[q][:, :, ATTR], ALU.mult))
                    c.step(ve.tensor_scalar(ang[:, T:], ang[:, 0:T], HALF_PI, None, ALU.add))
                    c.step(ve.tensor_scalar(angk[:, :], ang[:, :], INV_2PI, MAGIC, ALU.mult, ALU.add))
                    c.step(ve.tensor_scalar(angk[:, :], angk[:, :], -MAGIC, None, ALU.add))
                    for part in TWO_PI:
                        c.step(ve.scalar_tensor_tensor(ang[:, :], angk[:, :], -part, ang[:, :],
                                                       op0=ALU.mult, op1=ALU.add))
                    if tr.has(-2, NTRIPS):
                        ve.wait_ge(S["sin_done"], cnt(ph, "sin_done", tr.shift(-2)))
                    ve.tensor_scalar(angr[b][:, :], ang[:, :], PI, -PI, ALU.min, ALU.max)\
                      .then_inc(S["ang_done"], 1)
                    c.end()

                def before_gates(tr):
                    b, q = tr.b, tr.m
                    ve.wait_ge(S4["nlda"][q], node_dma(l, tr, PERA))
                    ve.wait_ge(S["ob_full"], cnt(ph, "ob_full", tr))
                    ve.tensor_tensor(by_bank(R3[b], 0, 192), ob(b, 0, 192), by_bank(AG[q], 0, 192), ALU.add)\
                      .then_inc(S["ob_used"], 1)

                def update(tr):
                    b, q = tr.b, tr.m
                    ve.wait_ge(S4["nldx"][q], node_dma(l, tr, PERX))
                    c = Chain(ve, S, ph, "dve", tr)
                    r, x = R[tr.y], X[q]
                    if l < 3:
                        ve.wait_ge(S["ob_full"], cnt(ph, "ob_full", tr))
                    if tr.has(-YBUF, NTRIPS):
                        wait(ve, S["y_done"], cnt(ph, "y_done", tr.shift(-YBUF)))
                    if l == 0:
                        for k in range(2):
                            ve.scalar_tensor_tensor(r[:, 2 * k:2 * k + 2, 96:F], x[:, 2 * k:2 * k + 2, 0:CS], 2.0,
                                                    ob(b, 96, CS)[:, k], op0=ALU.mult, op1=ALU.add)
                        for j in range(T):
                            ins = ve.scalar_tensor_tensor(
                                r[:, j, 0:96].rearrange("p (d c) -> p d c", d=3),
                                x[:, j, CS:F].rearrange("p (c d) -> p d c", d=3), 2.0,
                                NPO[b][:, j // 2, F * (j % 2):F * (j % 2) + 96].rearrange("p (d c) -> p d c", d=3),
                                op0=ALU.mult, op1=ALU.add)
                        ins.then_inc(S["ob_used"], 1)
                        ve.wait_ge(S["ob_used"], cnt(ph, "ob_used", tr))
                    elif l in (1, 2):
                        if l == 1:
                            ve.wait_ge(S["coef_done"], cnt(ph, "coef_done", tr))
                            k = co[b][:, 0:T]
                        else:
                            k = x[:, :, ATTR]
                        k4 = bc(k.rearrange("p (b t) -> p b t", b=2).unsqueeze(3), (NP, 2, 2, F))
                        ve.tensor_tensor(by_bank(r, 0, F), ob(b, 0, F), k4, ALU.mult).then_inc(S["ob_used"], 1)
                        ve.wait_ge(S["ob_used"], cnt(ph, "ob_used", tr))
                        ve.wait_ge(S["t2_done"], cnt(ph, "t2_done", tr))
                        c.step(ve.tensor_tensor(r[:, :, 0:F], r[:, :, 0:F], T2B[b][:, :, :], ALU.add))
                    else:
                        ve.wait_ge(S["sig_done"], cnt(ph, "sig_done", tr))
                        r3 = R3[b]
                        ve.tensor_tensor(r3[:, :, 96:F], r3[:, :, 96:F], SGN[b][:, :, 0:CS], ALU.mult)
                        r4 = r3[:, :, 0:96].rearrange("p t (d c) -> p t d c", d=3)
                        c.step(ve.tensor_tensor(r4, r4, bc(SGN[b][:, :, CS:96].unsqueeze(2), (NP, T, 3, CV)),
                                                ALU.mult))
                        ve.tensor_tensor(r[:, :, 0:CS], r3[:, :, 96:F], x[:, :, 96:F], ALU.add)
                        c.step(ve.tensor_tensor(r[:, :, CS:F].rearrange("p t (c d) -> p t d c", d=3), r4,
                                                x[:, :, 0:96].rearrange("p t (d c) -> p t d c", d=3), ALU.add))
                    for j in range(T):
                        ins = ve.bn_stats(nbs[:, j, :], r[:, j, 0:F])
                    c.step(ins)
                    if tr.has(-2, NTRIPS):
                        ve.wait_ge(S["rstd_done"], cnt(ph, "rstd_done", tr.shift(-2)))
                    ve.sem_inc(ve_go, 1)
                    for j in range(T):
                        ins = ve.bn_aggr(nmv[b][:, j, :], nbs[:, j, :])
                    ins.then_inc(S["r_done"], 1)
                    c.end()

                if l == 0:
                    agn(Trip(0, 0))
                    agn(Trip(0, 1))
                if l in (1, 2):
                    coefs = (angles, counts)[l - 1]
                    coefs(Trip(0, 0))
                    coefs(Trip(0, 1))
                if l == 3:
                    before_gates(Trip(0, 0))

                def node_trip(tr):
                    if l == 0 and tr.has(2, NTRIPS):
                        agn(tr.shift(2))
                    if l == 3 and tr.has(1, NTRIPS):
                        before_gates(tr.shift(1))
                    update(tr)
                    if l in (1, 2) and tr.has(2, NTRIPS):
                        coefs(tr.shift(2))

                trips(ve, NTRIPS, node_trip, NBUF)


_INS = [
    "x", "src", "dst", "edge_attr_16", "edge_attr_4", "edge_attr_64", "edge_attr_8", "node_vec1",
    "L0_gnn_gamma_s", "L0_gnn_beta_s", "L0_gnn_gamma_v", "L0_gnn_Ws_src", "L0_gnn_Wv_src", "L0_gnn_Ws_dst",
    "L0_gnn_Wv_dst", "L0_gnn_W_rbf", "L0_gnn_W_alpha", "L0_gnn_alpha_dot", "L0_gnn_Ws_val", "L0_gnn_Wv_val",
    "L0_gnn_Wg", "L0_gnn_w2_ss", "L0_gnn_w2_sv", "L0_gnn_w2_vs", "L0_gnn_w2_vv0", "L0_gnn_w2_vv1",
    "L0_gnn_Ws_vlin", "L0_gnn_Wv_vlin", "L0_gnn_Wps", "L0_gnn_Wpv",
    "L1_gnn_W_sc_s", "L1_gnn_W_sc_v", "L1_gnn_W1_s", "L1_gnn_W1_v", "L1_gnn_W2_s", "L1_gnn_W2_v", "L1_gnn_W3",
    "L1_gnn_fcW1", "L1_gnn_fcW2",
    "L2_gnn_Wfc1", "L2_gnn_Wfc2", "L2_gnn_Wsc0", "L2_gnn_Wsc1", "L2_gnn_Wl1_0", "L2_gnn_Wl1_1", "L2_gnn_Wl2_s",
    "L2_gnn_Wl2_v", "L2_gnn_Wa",
    "L3_gnn_lin1_ws", "L3_gnn_lin1_wv", "L3_gnn_fc_w1", "L3_gnn_fc_w2", "L3_gnn_sc_ws", "L3_gnn_sc_wv",
    "L3_gnn_lin2_ws", "L3_gnn_lin2_wv",
]


def kernel(**inputs):
    import numpy as _np
    import concourse.bacc as _bacc
    from concourse import mybir as _mybir
    from concourse.bass_utils import run_bass_kernel_spmd as _run

    nc = _bacc.Bacc("TRN2", target_bir_lowering=False, num_devices=1)
    arrays, args = {}, {}
    for name in _INS:
        a = _np.ascontiguousarray(inputs[name])
        arrays[f"in_{name}"] = a
        args[name] = nc.dram_tensor(f"in_{name}", a.shape, _mybir.dt.from_np(a.dtype), kind="ExternalInput").ap()
    out = nc.dram_tensor("out_0", (N, F), _mybir.dt.float32, kind="ExternalOutput").ap()
    gnn_kernel(nc, args, out)
    r = _run(nc, [arrays], core_ids=[0])
    return r.results[0]["out_0"]
```
